# Optimizing a Trainium2 kernel written in Bass

```python
import numpy as np
import jax
import jax.numpy as jnp

def _softmax(x, axis=-1):
    return jax.nn.softmax(x, axis=axis)

def _gelu(x):
    return jax.nn.gelu(x, approximate=True)

def _silu(x):
    return jax.nn.silu(x)

def _sigmoid(x):
    return jax.nn.sigmoid(x)

def _layernorm(x, axis=-1, eps=1e-05):
    m = jnp.mean(x, axis=axis, keepdims=True)
    v = jnp.var(x, axis=axis, keepdims=True)
    return (x - m) / jnp.sqrt(v + eps)

def _scatter_add(tgt, idx, src, axis=0):
    return tgt.at[idx].add(src)

def _segment_sum(src, seg, n):
    return jax.ops.segment_sum(src, seg, n)
kernel_name = 'mk_gnn_resnorm_d2_gnn_r64_4245c4'

def setup_inputs(seed: int=0):
    np.random.seed(seed)
    _w = jnp.asarray

    def _rec_inputs():
        import jax
        import jax.numpy as jnp
        _gk = jax.random.key(seed)
        x = -0.0008691 + 1 * jax.random.normal(jax.random.fold_in(_gk, 1), (50000, 128), jnp.float32)
        src = jax.random.randint(jax.random.fold_in(_gk, 2), (25000,), 0, 50000, jnp.int32)
        dst = jax.random.randint(jax.random.fold_in(_gk, 3), (25000,), 0, 50000, jnp.int32)
        _o = jnp.argsort(dst, stable=True)
        src = src[_o]
        dst = dst[_o]
        edge_type_5 = jax.random.randint(jax.random.fold_in(_gk, 13), (25000,), 0, 5, jnp.int32)
        edge_weight = jax.random.uniform(jax.random.fold_in(_gk, 14), (25000,), jnp.float32, 0.0, 1)
        return (x, src, dst, edge_type_5, edge_weight)
    x, src, dst, edge_type_5, edge_weight = _rec_inputs()

    def _L0_gnn_setup():
        import jax, jax.numpy as jnp
        import numpy as np
        N_NODES = 10000
        N_EDGES = 10000
        D_IN = 128
        D_OUT = 128
        EPS = 0.0
        key = jax.random.key(seed)
        k_h, k_mask, k_src, k_dst, k_w = jax.random.split(key, 5)
        h = jax.random.normal(k_h, (N_NODES, D_IN), dtype=jnp.float32)
        mask = jax.random.uniform(k_mask, (N_EDGES,), dtype=jnp.float32)
        src = jax.random.randint(k_src, (N_EDGES,), 0, N_NODES, dtype=jnp.int32)
        dst = jax.random.randint(k_dst, (N_EDGES,), 0, N_NODES, dtype=jnp.int32)
        W = jax.random.normal(k_w, (D_OUT, D_IN), dtype=jnp.float32) / np.sqrt(D_IN)
        return {'h': h, 'mask': mask, 'src': src, 'dst': dst, 'W': W}
    _L0_gnn_all = _L0_gnn_setup()
    _L0_gnn_in = {k: v for k, v in _L0_gnn_all.items() if k in ('W',)}
    del _L0_gnn_all

    def _L1_gnn_setup():
        import jax, jax.numpy as jnp
        import numpy as np
        N = 50000
        E = 10000
        HIDDEN = 128
        R = 5
        HEADS = 8
        HEAD_DIM = HIDDEN // HEADS
        LN_EPS = 1e-05

        def _fused_forward(node_embeddings, W_Q, W_K, W_V, attn_bias, out_proj_w, out_proj_b, ln_gamma, ln_beta, edge_index, edge_types):
            src, dst = (edge_index[0], edge_index[1])
            n = node_embeddings.shape[0]
            x_src = node_embeddings[src]
            x_dst = node_embeddings[dst]
            scale = HEAD_DIM ** 0.5
            NEG = jnp.float32(-1000000000.0)
            out = jnp.zeros((n, HEADS, HEAD_DIM), dtype=node_embeddings.dtype)
            for r in range(R):
                mask = edge_types == r
                q = jnp.einsum('eh,khd->ekd', x_dst, W_Q[r])
                k = jnp.einsum('eh,khd->ekd', x_src, W_K[r])
                v = jnp.einsum('eh,khd->ekd', x_src, W_V[r])
                logits = (q * k).sum(-1) / scale + attn_bias[r][None, :]
                masked_logits = jnp.where(mask[:, None], logits, NEG)
                max_v = jax.ops.segment_max(masked_logits, dst, num_segments=n)
                max_v = jnp.maximum(max_v, NEG)
                exp_l = jnp.where(mask[:, None], jnp.exp(masked_logits - max_v[dst]), 0.0)
                sum_exp = jax.ops.segment_sum(exp_l, dst, num_segments=n)
                attn = exp_l / (sum_exp[dst] + 1e-12)
                out = out + jax.ops.segment_sum(attn[:, :, None] * v, dst, num_segments=n)
            out = out.reshape(n, HIDDEN)
            out = out @ out_proj_w.T + out_proj_b
            h = out + node_embeddings
            mu = h.mean(-1, keepdims=True)
            var = ((h - mu) ** 2).mean(-1, keepdims=True)
            return (h - mu) / jnp.sqrt(var + LN_EPS) * ln_gamma + ln_beta
        key = jax.random.key(seed)
        ks = jax.random.split(key, 10)
        bound = float(np.sqrt(6.0 / (HIDDEN + HEAD_DIM)))
        pbound = float(np.sqrt(1.0 / HIDDEN))
        return {'node_embeddings': jax.random.normal(ks[0], (N, HIDDEN), dtype=jnp.float32), 'edge_index': jax.random.randint(ks[1], (2, E), 0, N, dtype=jnp.int64), 'edge_types': jax.random.randint(ks[2], (E,), 0, R, dtype=jnp.int64), 'W_Q': jax.random.uniform(ks[3], (R, HEADS, HIDDEN, HEAD_DIM), minval=-bound, maxval=bound, dtype=jnp.float32), 'W_K': jax.random.uniform(ks[4], (R, HEADS, HIDDEN, HEAD_DIM), minval=-bound, maxval=bound, dtype=jnp.float32), 'W_V': jax.random.uniform(ks[5], (R, HEADS, HIDDEN, HEAD_DIM), minval=-bound, maxval=bound, dtype=jnp.float32), 'attn_bias': jnp.zeros((R, HEADS), dtype=jnp.float32), 'out_proj_w': jax.random.uniform(ks[6], (HIDDEN, HIDDEN), minval=-pbound, maxval=pbound, dtype=jnp.float32), 'out_proj_b': jax.random.uniform(ks[7], (HIDDEN,), minval=-pbound, maxval=pbound, dtype=jnp.float32), 'ln_gamma': jnp.ones((HIDDEN,), dtype=jnp.float32), 'ln_beta': jnp.zeros((HIDDEN,), dtype=jnp.float32)}
    _L1_gnn_all = _L1_gnn_setup()
    _L1_gnn_in = {k: v for k, v in _L1_gnn_all.items() if k in ('W_Q', 'W_K', 'W_V', 'attn_bias', 'out_proj_w', 'out_proj_b', 'ln_gamma', 'ln_beta')}
    del _L1_gnn_all
    return {'x': x, 'src': src, 'dst': dst, 'edge_type_5': edge_type_5, 'edge_weight': edge_weight, 'L0_gnn_W': _L0_gnn_in['W'], 'L1_gnn_W_Q': _L1_gnn_in['W_Q'], 'L1_gnn_W_K': _L1_gnn_in['W_K'], 'L1_gnn_W_V': _L1_gnn_in['W_V'], 'L1_gnn_attn_bias': _L1_gnn_in['attn_bias'], 'L1_gnn_out_proj_w': _L1_gnn_in['out_proj_w'], 'L1_gnn_out_proj_b': _L1_gnn_in['out_proj_b'], 'L1_gnn_ln_gamma': _L1_gnn_in['ln_gamma'], 'L1_gnn_ln_beta': _L1_gnn_in['ln_beta']}

def reference(x, src, dst, edge_type_5, edge_weight, L0_gnn_W, L1_gnn_W_Q, L1_gnn_W_K, L1_gnn_W_V, L1_gnn_attn_bias, L1_gnn_out_proj_w, L1_gnn_out_proj_b, L1_gnn_ln_gamma, L1_gnn_ln_beta):
    import jax
    import jax.numpy as jnp

    def _L0_gnn_ref(h, mask, src, dst, W):
        import jax, jax.numpy as jnp
        import numpy as np
        N_NODES = 10000
        N_EDGES = 10000
        D_IN = 128
        D_OUT = 128
        EPS = 0.0
        msgs = h[src] * mask[:, None]
        neigh = jax.ops.segment_sum(msgs, dst, num_segments=h.shape[0])
        out = (1.0 + EPS) * h + neigh
        return out @ W.T

    def _L1_gnn_ref(node_embeddings, edge_index, edge_types, W_Q, W_K, W_V, attn_bias, out_proj_w, out_proj_b, ln_gamma, ln_beta):
        import jax, jax.numpy as jnp
        import numpy as np
        N = 50000
        E = 10000
        HIDDEN = 128
        R = 5
        HEADS = 8
        HEAD_DIM = HIDDEN // HEADS
        LN_EPS = 1e-05

        def _fused_forward(node_embeddings, W_Q, W_K, W_V, attn_bias, out_proj_w, out_proj_b, ln_gamma, ln_beta, edge_index, edge_types):
            src, dst = (edge_index[0], edge_index[1])
            n = node_embeddings.shape[0]
            x_src = node_embeddings[src]
            x_dst = node_embeddings[dst]
            scale = HEAD_DIM ** 0.5
            NEG = jnp.float32(-1000000000.0)
            out = jnp.zeros((n, HEADS, HEAD_DIM), dtype=node_embeddings.dtype)
            for r in range(R):
                mask = edge_types == r
                q = jnp.einsum('eh,khd->ekd', x_dst, W_Q[r])
                k = jnp.einsum('eh,khd->ekd', x_src, W_K[r])
                v = jnp.einsum('eh,khd->ekd', x_src, W_V[r])
                logits = (q * k).sum(-1) / scale + attn_bias[r][None, :]
                masked_logits = jnp.where(mask[:, None], logits, NEG)
                max_v = jax.ops.segment_max(masked_logits, dst, num_segments=n)
                max_v = jnp.maximum(max_v, NEG)
                exp_l = jnp.where(mask[:, None], jnp.exp(masked_logits - max_v[dst]), 0.0)
                sum_exp = jax.ops.segment_sum(exp_l, dst, num_segments=n)
                attn = exp_l / (sum_exp[dst] + 1e-12)
                out = out + jax.ops.segment_sum(attn[:, :, None] * v, dst, num_segments=n)
            out = out.reshape(n, HIDDEN)
            out = out @ out_proj_w.T + out_proj_b
            h = out + node_embeddings
            mu = h.mean(-1, keepdims=True)
            var = ((h - mu) ** 2).mean(-1, keepdims=True)
            return (h - mu) / jnp.sqrt(var + LN_EPS) * ln_gamma + ln_beta
        return _fused_forward(node_embeddings, W_Q, W_K, W_V, attn_bias, out_proj_w, out_proj_b, ln_gamma, ln_beta, edge_index, edge_types)
    edge_index = jnp.stack([src, dst])
    x = _layernorm(x + _L0_gnn_ref(x, edge_weight, src, dst, L0_gnn_W), axis=-1)
    x = _layernorm(x + _L1_gnn_ref(x, edge_index, edge_type_5, L1_gnn_W_Q, L1_gnn_W_K, L1_gnn_W_V, L1_gnn_attn_bias, L1_gnn_out_proj_w, L1_gnn_out_proj_b, L1_gnn_ln_gamma, L1_gnn_ln_beta), axis=-1)
    return x

_drawn_inputs = setup_inputs


def setup_inputs(seed=0):
    import zlib

    import numpy as np

    out = dict(_drawn_inputs(seed))
    spreads = {'L1_gnn_attn_bias': (0.0, 0.1),
     'L1_gnn_ln_gamma': (1.0, 0.2),
     'L1_gnn_ln_beta': (0.0, 0.1)}
    factors = {}
    for name, (base, spread) in spreads.items():
        noise = np.random.default_rng([zlib.crc32(name.encode()), seed]).standard_normal(out[name].shape)
        drawn = base * np.exp(spread * noise) if base else spread * noise
        out[name] = jnp.asarray(drawn.astype(out[name].dtype))
    for name, factor in factors.items():
        out[name] = (out[name] * factor).astype(out[name].dtype)
    return out
```

```python
import concourse.bass as bass
from concourse import mybir
from contextlib import ExitStack

F32 = mybir.dt.float32
I32 = mybir.dt.int32
ALU = mybir.AluOpType
ACT = mybir.ActivationFunctionType
AX = mybir.AxisListType
ENG = mybir.EngineType

P = 128
N, F = 50000, 128
E, R, H, HD = 25000, 5, 8, 16
NT = (E + P - 1) // P
EP = NT * P
HALF = NT // 2
TAIL = E - (NT - 1) * P
NB = (N + P - 1) // P
LAST_ROWS = N - (NB - 1) * P
BT = 4
GB = 2
GT = BT * GB
GROUPS = NB // GT
PAIRS = GROUPS // 2
REST = NB - GROUPS * GT
NCH = 4
PAD_DST = 1 << 17
NO_DST = 1.0e6
EPS = 1e-5
NEG = -1.0e9
MASK = 1.0e30
SCALE = float(HD) ** 0.5
LEAD = 8
SLOTS = 7
STEPS = 4
TURN = 14
FAR = [(8, 63), (64, 511), (512, 4095), (4096, EP)]
NEAR = 7
NPROBE = NEAR + len(FAR) + 1


def done(step):
    return LEAD + 1 + step


class Memory:
    pass


def scoped(nc, ctx):
    sems = []

    def clear():
        if sems:
            nc.clear_and_free_semaphores(sems)
            nc.all_engine_barrier(sem_only=True)

    ctx.callback(clear)

    def sb(name, shape, dt=F32):
        return ctx.enter_context(nc.sbuf_tensor(name, shape, dt))

    def pb(name, shape):
        return ctx.enter_context(nc.psum_tensor(name, shape, F32))

    def sem(name):
        sems.append(nc.alloc_semaphore(name))
        return sems[-1]

    return sb, pb, sem


def gnn(nc, x, src, dst, typ, wgt, w0, wq, wk, wv, bias, wo, bo, gamma, beta, out):
    m = Memory()
    m.x, m.src, m.dst, m.typ, m.wgt, m.out = x, src, dst, typ, wgt, out
    m.w0, m.wq, m.wk, m.wv, m.wo = w0, wq, wk, wv, wo
    m.bias, m.bo, m.gamma, m.beta = bias, bo, gamma, beta
    m.x1_d = nc.dram_tensor("x1_d", [N, F], F32).ap()
    m.sums_d = nc.dram_tensor("sums_d", [NB * P, F], F32).ap()
    m.key_d = nc.dram_tensor("key_d", [3 * EP], F32).ap()
    m.dst_d = nc.dram_tensor("dst_d", [EP + FAR[-1][0]], F32).ap()
    m.logit_d = nc.dram_tensor("logit_d", [H, 3 * EP], F32).ap()
    m.prob_d = nc.dram_tensor("prob_d", [H, 3 * EP], F32).ap()
    m.attn_d = nc.dram_tensor("attn_d", [H, EP], F32).ap()

    with ExitStack() as ctx:
        sb, _, _ = scoped(nc, ctx)
        m.msg = sb("msg", [P, NT + 1, F])
        m.ident = sb("ident", [P, P])
        m.local_id = sb("local_id", [P, GT * P])
        m.src_i = sb("src_i", [P, NT + SLOTS], I32)
        m.dst_i = sb("dst_i", [P, NT + SLOTS], I32)
        m.dst_f = sb("dst_f", [P, NT + 1])
        m.wgt_f = sb("wgt_f", [P, NT])
        m.of_type = sb("of_type", [P, R, NT])
        m.key_b = sb("key_b", [P, NT])
        m.bias_e = sb("bias_e", [P, NT, H])
        m.w_self = sb("w_self", [P, F])
        m.w_nb = sb("w_nb", [P, F])
        m.w_out = sb("w_out", [P, F])
        m.w_qkv = sb("w_qkv", [P, R, 3, F])
        m.gam_b = sb("gam_b", [P, F])
        m.bet_b = sb("bet_b", [P, F])
        m.bo_row = sb("bo_row", [1, BT, F])
        m.ones_row = sb("ones_row", [1, P])
        m.logit = sb("logit", [P, NT, H])
        m.eps_c = sb("eps_c", [P, 1])
        m.first_i = sb("first_i", [1, NCH * HALF], I32)
        m.end_i = sb("end_i", [1, NCH * HALF], I32)
        m.wide_i = sb("wide_i", [1, 1], I32)
        m.band_i = sb("band_i", [1, 2], I32)

        setup(nc, m)
        edge_messages(nc, m)
        wide = nc.values_load(m.wide_i[0:1, 0:1], min_val=0, max_val=1)
        with nc.If(wide == 1):
            general_sums(nc, m, "a")
            layer0_nodes(nc, m, from_sums=True)
        with nc.Else():
            layer0_nodes(nc, m, from_sums=False)
        project_edges(nc, m)
        segment_softmax(nc, m)
        attended_messages(nc, m)
        with nc.If(wide == 1):
            general_sums(nc, m, "b")
            layer1_nodes(nc, m, from_sums=True)
        with nc.Else():
            layer1_nodes(nc, m, from_sums=False)


def setup(nc, m):
    with ExitStack() as ctx:
        sb, pb, sem = scoped(nc, ctx)
        src_r, dst_r, typ_r = (sb(n, [HALF, 2, P], I32) for n in ("src_r", "dst_r", "typ_r"))
        wgt_r, srcf_r, dstf_r, typf_r, dstc_r, key_r = (
            sb(n, [HALF, 2, P]) for n in ("wgt_r", "srcf_r", "dstf_r", "typf_r", "dstc_r", "key_r"))
        pad_dst = sb("pad_dst", [1, P - TAIL], I32)
        pad_0 = sb("pad_0", [1, P - TAIL], I32)
        pad_w = sb("pad_w", [1, P - TAIL])
        no_dst = sb("no_dst", [32, P])
        typ_f = sb("typ_f", [P, NT])
        w0_r = sb("w0_r", [P, F])
        wo_r = sb("wo_r", [P, F])
        bias_r = sb("bias_r", [P, R, H])
        bias_t = sb("bias_t", [P, NT, H])
        ones = sb("ones", [HALF, P])
        ends = sb("ends", [HALF, 2, 2])
        ends_d = sb("ends_d", [HALF, 2, 2, HALF])
        ends_b = sb("ends_b", [P, 2, NT])
        node_0 = sb("node_0", [HALF, NCH])
        node_1 = sb("node_1", [HALF, NCH])
        below = sb("below", [HALF, NCH, NT])
        cover = sb("cover", [HALF, NCH, NT])
        tile_1 = sb("tile_1", [HALF, NT])
        tile_hi = sb("tile_hi", [HALF, NT])
        cand = sb("cand", [HALF, NCH, NT])
        cand2 = sb("cand2", [HALF, NCH, NT])
        first_c = sb("first_c", [HALF, NCH])
        end_c = sb("end_c", [HALF, NCH])
        first_f = sb("first_f", [1, NCH * HALF])
        end_f = sb("end_f", [1, NCH * HALF])
        span_f = sb("span_f", [1, NCH * HALF])
        widest = sb("widest", [1, 1])
        shifted = sb("shifted", [P, NPROBE, NT])
        dst_b = sb("dst_b", [P, NT])
        same = sb("same", [P, NPROBE, NT])
        found = sb("found", [P, NPROBE])
        found_all = sb("found_all", [P, NPROBE])
        reach_of = sb("reach_of", [1, NPROBE])
        reach = sb("reach", [1, NPROBE + 4])
        ps_edge = [pb(f"ps_edge{i}", [P, 2, NT]) for i in range(3)]
        ps_w = pb("ps_w", [P, 2, F])
        ps_ends = pb("ps_ends", [P, 2, NT])
        ps_first = pb("ps_first", [1, NCH * HALF])
        ps_end = pb("ps_end", [1, NCH * HALF])

        edges_in, weights_in, pads = sem("edges_in"), sem("weights_in"), sem("pads")
        consts, zeroed, ident_ok = sem("consts"), sem("zeroed"), sem("ident_ok")
        rows_ok, circ_out, probes_in = sem("rows_ok"), sem("circ_out"), sem("probes_in")
        transposed, ends_ok, ends_ps = sem("transposed"), sem("ends_ok"), sem("ends_ps")
        cols_ok, cols_ps, found_ok, found_red = (
            sem("cols_ok"), sem("cols_ps"), sem("found_ok"), sem("found_red"))
        chain = sem("chain")

        block = ctx.enter_context(nc.Block())
        main = (NT - 1) * P

        @block.sync
        def _(sp):
            sp.wait_ge(pads, 4)
            for a, rows, pad in ((m.src, src_r, pad_0), (m.dst, dst_r, pad_dst),
                                 (m.typ, typ_r, pad_0), (m.wgt, wgt_r, pad_w)):
                sp.dma_start(rows[:, 0, :], a[0:HALF * P].rearrange("(p c) -> p c", c=P)).then_inc(edges_in, 16)
                sp.dma_start(rows[0:HALF - 1, 1, :],
                             a[HALF * P:main].rearrange("(p c) -> p c", c=P)).then_inc(edges_in, 16)
                sp.dma_start(rows[HALF - 1:HALF, 1, 0:TAIL],
                             a[main:E].rearrange("(p c) -> p c", p=1)).then_inc(edges_in, 16)
                sp.dma_start(rows[HALF - 1:HALF, 1, TAIL:P], pad[:]).then_inc(edges_in, 16)
            sp.wait_ge(rows_ok, 1)
            for a in range(2):
                at = a * HALF * P
                sp.dma_start(m.dst_d[at:at + HALF * P].rearrange("(p c) -> p c", c=P),
                             dstf_r[:, a, :]).then_inc(circ_out, 16)
                for copy in range(3):
                    at = copy * EP + a * HALF * P
                    sp.dma_start(m.key_d[at:at + HALF * P].rearrange("(p c) -> p c", c=P),
                                 key_r[:, a, :]).then_inc(circ_out, 16)
            sp.dma_start(m.dst_d[EP:EP + FAR[-1][0]].rearrange("(p c) -> p c", c=P),
                         no_dst[:]).then_inc(circ_out, 16)
            sp.wait_ge(circ_out, 9 * 16)

            def probe(to, a, shift):
                sp.dma_start(to, a[shift:shift + EP].rearrange("(p t) -> p t", t=NT)).then_inc(probes_in, 16)

            probe(m.key_b[:], m.key_d, 0)
            probe(dst_b[:], m.dst_d, 0)
            for d in range(1, NEAR + 1):
                probe(shifted[:, d - 1, :], m.key_d, d)
            for i, (d, _) in enumerate(FAR):
                probe(shifted[:, NEAR + i, :], m.dst_d, d)
            probe(shifted[:, NPROBE - 1, :], m.dst_d, 1)

        @block.scalar
        def _(act):
            act.dma_start(w0_r[:], m.w0).then_inc(weights_in, 16)
            act.dma_start(wo_r[:], m.wo).then_inc(weights_in, 16)
            act.dma_start(bias_r[:], m.bias.partition_broadcast(P)).then_inc(weights_in, 16)
            act.dma_start(m.gam_b[:], m.gamma.partition_broadcast(P)).then_inc(weights_in, 16)
            act.dma_start(m.bet_b[:], m.beta.partition_broadcast(P)).then_inc(weights_in, 16)
            act.dma_start(m.bo_row[:], m.bo[None, None, :].broadcast_to([1, BT, F])).then_inc(weights_in, 16)
            for i, w in enumerate((m.wq, m.wk, m.wv)):
                for r in range(R):
                    act.dma_start(m.w_qkv[:, r, i, :].rearrange("i (h d) -> i h d", h=H),
                                  w[r].rearrange("h i d -> i h d")).then_inc(weights_in, 16)
            act.wait_ge(weights_in, (6 + 3 * R) * 16)

        @block.gpsimd
        def _(pool):
            nc.gpsimd.iota(pad_dst[:], [[1, P - TAIL]], base=PAD_DST + TAIL, channel_multiplier=0).then_inc(pads, 1)
            nc.gpsimd.memset(pad_0[:], 0).then_inc(pads, 1)
            nc.gpsimd.memset(pad_w[:], 0.0).then_inc(pads, 1)
            nc.gpsimd.memset(no_dst[:], NO_DST).then_inc(pads, 1)
            nc.gpsimd.memset(m.ident[:], 0.0).then_inc(zeroed, 1)
            pool.wait_ge(zeroed, 1)
            nc.gpsimd.affine_select(out=m.ident[:], in_=m.ident[:], compare_op=ALU.not_equal, fill=1.0,
                                    base=0, pattern=[[-1, P]], channel_multiplier=1).then_inc(ident_ok, 1)
            nc.gpsimd.iota(m.local_id[:], [[1, GT * P]], base=0, channel_multiplier=0,
                           allow_small_or_imprecise_dtypes=True).then_inc(consts, 1)
            nc.gpsimd.iota(node_0[:], [[HALF * P, NCH]], base=0, channel_multiplier=P,
                           allow_small_or_imprecise_dtypes=True).then_inc(consts, 1)
            nc.gpsimd.memset(ones[:], 1.0).then_inc(consts, 1)
            nc.gpsimd.memset(m.ones_row[:], 1.0).then_inc(consts, 1)
            nc.gpsimd.memset(m.eps_c[:], EPS).then_inc(consts, 1)
            nc.gpsimd.memset(m.msg[:, NT, :], 0.0).then_inc(consts, 1)
            nc.gpsimd.memset(m.src_i[:, NT:NT + SLOTS], 0).then_inc(consts, 1)
            nc.gpsimd.memset(m.dst_i[:, NT:NT + SLOTS], 0).then_inc(consts, 1)
            nc.gpsimd.memset(m.dst_f[:, NT:NT + 1], NO_DST).then_inc(consts, 1)
            pool.wait_ge(found_ok, 1)
            nc.gpsimd.partition_all_reduce(found_all[:], found[:], P, bass.bass_isa.ReduceOp.max).then_inc(found_red, 1)

        @block.vector
        def _(dve):
            links = [0]

            def link(ins):
                links[0] += 1
                ins.then_inc(chain, 1)
                dve.wait_ge(chain, links[0])

            dve.wait_ge(edges_in, 16 * 16)
            nc.vector.tensor_copy(srcf_r[:], src_r[:])
            nc.vector.tensor_copy(typf_r[:], typ_r[:])
            link(nc.vector.tensor_copy(dstf_r[:], dst_r[:]))
            nc.vector.tensor_scalar(dstc_r[:], dstf_r[:], float(N - 1), None, ALU.min)
            nc.vector.tensor_reduce(ends[:, 0, :], dstf_r[:], AX.X, ALU.min)
            nc.vector.tensor_reduce(ends[:, 1, :], dstf_r[:], AX.X, ALU.max)
            nc.vector.scalar_tensor_tensor(key_r[:], dstf_r[:], 8.0, typf_r[:], ALU.mult, ALU.add).then_inc(rows_ok, 1)
            dve.wait_ge(rows_ok, 1)
            dve.wait_ge(ident_ok, 1)
            for i in range(2):
                for a in range(2):
                    last = nc.vector.tensor_scalar(ends_d[:, i, a, :], m.ident[0:HALF, 0:HALF],
                                                   ends[:, i, a:a + 1], None, ALU.mult)
            last.then_inc(ends_ok, 1)
            for i, d in enumerate([*range(1, NEAR + 1), *(far for _, far in FAR), EP]):
                last = nc.vector.memset(reach_of[:, i:i + 1], float(d))
            link(last)

            dve.wait_ge(transposed, 1)
            nc.vector.tensor_copy(m.src_i[:, 0:NT], ps_edge[0][:, 0, :])
            nc.vector.tensor_copy(m.dst_i[:, 0:NT], ps_edge[0][:, 1, :])
            nc.vector.tensor_copy(m.dst_f[:, 0:NT], ps_edge[1][:, 0, :])
            nc.vector.tensor_copy(m.wgt_f[:], ps_edge[1][:, 1, :])
            nc.vector.tensor_copy(typ_f[:], ps_edge[2][:, 0, :])
            nc.vector.tensor_copy(m.w_nb[:], ps_w[:, 0, :])
            nc.vector.tensor_copy(m.w_out[:], ps_w[:, 1, :])
            link(nc.vector.tensor_tensor(m.w_self[:], ps_w[:, 0, :], m.ident[:], ALU.add))
            for r in range(R):
                last = nc.vector.tensor_scalar(m.of_type[:, r, :], typ_f[:], float(r), None, ALU.is_equal)
            link(last)

            dve.wait_ge(ends_ps, 1)
            dve.wait_ge(consts, 9)
            nc.vector.tensor_copy(ends_b[:], ps_ends[:])
            nc.vector.tensor_scalar(tile_1[:], m.local_id[0:HALF, 0:NT], 1.0, None, ALU.add)
            nc.vector.tensor_scalar(tile_hi[:], m.local_id[0:HALF, 0:NT], float(EP), None, ALU.add)
            link(nc.vector.tensor_scalar(node_1[:], node_0[:], float(P), None, ALU.add))
            for c in range(NCH):
                last = nc.vector.tensor_scalar(below[:, c, :], ends_b[0:HALF, 0, :], node_1[:, c:c + 1],
                                               None, ALU.is_lt)
            link(last)
            for c in range(NCH):
                last = nc.vector.scalar_tensor_tensor(cover[:, c, :], ends_b[0:HALF, 1, :], node_0[:, c:c + 1],
                                                      below[:, c, :], ALU.is_ge, ALU.mult)
            link(last)
            nc.vector.scalar_tensor_tensor(cand[:], cover[:], -float(EP), tile_hi[:, None, :].broadcast_to([HALF, NCH, NT]),
                                           ALU.mult, ALU.add)
            link(nc.vector.tensor_tensor(cand2[:], cover[:], tile_1[:, None, :].broadcast_to([HALF, NCH, NT]), ALU.mult))
            nc.vector.tensor_reduce(first_c[:], cand[:], AX.X, ALU.min)
            nc.vector.tensor_reduce(end_c[:], cand2[:], AX.X, ALU.max).then_inc(cols_ok, 1)
            dve.wait_ge(cols_ps, 1)
            link(nc.vector.tensor_scalar(first_f[:], ps_first[:], float(NT - 1), None, ALU.min))
            nc.vector.tensor_copy(m.first_i[:], first_f[:])
            link(nc.vector.scalar_tensor_tensor(end_f[:], first_f[:], 1.0, ps_end[:], ALU.add, ALU.max))
            nc.vector.tensor_copy(m.end_i[:], end_f[:])
            link(nc.vector.tensor_tensor(span_f[:], end_f[:], first_f[:], ALU.subtract))
            link(nc.vector.tensor_reduce(widest[:], span_f[:], AX.X, ALU.max))
            nc.vector.tensor_scalar(m.wide_i[:], widest[:], 3.0, None, ALU.is_ge)

            dve.wait_ge(weights_in, (6 + 3 * R) * 16)
            for r in range(R):
                mask = m.of_type[:, r, :, None].broadcast_to([P, NT, H])
                b = bias_r[:, r, None, :].broadcast_to([P, NT, H])
                link(nc.vector.tensor_tensor(bias_t[:] if r else m.bias_e[:], mask, b, ALU.mult))
                if r:
                    link(nc.vector.tensor_tensor(m.bias_e[:], m.bias_e[:], bias_t[:], ALU.add))

            dve.wait_ge(probes_in, (NPROBE + 2) * 16)
            keys = m.key_b[:, None, :].broadcast_to([P, NEAR, NT])
            dsts = dst_b[:, None, :].broadcast_to([P, len(FAR), NT])
            nc.vector.tensor_tensor(same[:, 0:NEAR, :], shifted[:, 0:NEAR, :], keys, ALU.is_equal)
            nc.vector.tensor_tensor(same[:, NEAR:NPROBE - 1, :], shifted[:, NEAR:NPROBE - 1, :], dsts, ALU.is_equal)
            link(nc.vector.tensor_tensor(same[:, NPROBE - 1, :], shifted[:, NPROBE - 1, :], dst_b[:], ALU.is_lt))
            nc.vector.tensor_reduce(found[:], same[:], AX.X, ALU.max).then_inc(found_ok, 1)
            dve.wait_ge(found_red, 1)
            link(nc.vector.tensor_tensor(reach[:, 0:NPROBE], found_all[0:1, :], reach_of[:], ALU.mult))
            r_max, r_low, r_all, r_end = (reach[:, NPROBE + i:NPROBE + i + 1] for i in range(4))
            link(nc.vector.tensor_reduce(r_max, reach[:, 0:NPROBE], AX.X, ALU.max))
            link(nc.vector.tensor_scalar(r_low, r_max, float(EP - 1), None, ALU.min))
            link(nc.vector.tensor_scalar(r_all, r_max, float(EP), None, ALU.is_lt))
            link(nc.vector.scalar_tensor_tensor(r_end, r_max, 1.0, r_all, ALU.add, ALU.mult))
            nc.vector.tensor_scalar(m.band_i[:, 0:1], r_low, -1.0, float(EP), ALU.mult, ALU.add)
            nc.vector.scalar_tensor_tensor(m.band_i[:, 1:2], r_end, 1.0, r_low, ALU.add, ALU.add)

        @block.tensor
        def _(pe):
            pe.wait_ge(ident_ok, 1)
            pe.wait_ge(rows_ok, 1)
            small = m.ident[0:HALF, 0:HALF]
            for i, rows in enumerate((srcf_r, dstc_r, dstf_r, wgt_r, typf_r)):
                for a in range(2):
                    nc.tensor.transpose(ps_edge[i // 2][:, i % 2, a * HALF:(a + 1) * HALF], rows[:, a, :], small)
            pe.wait_ge(weights_in, (6 + 3 * R) * 16)
            nc.tensor.transpose(ps_w[:, 0, :], w0_r[:], m.ident[:])
            nc.tensor.transpose(ps_w[:, 1, :], wo_r[:], m.ident[:]).then_inc(transposed, 1)
            pe.wait_ge(ends_ok, 1)
            pe.wait_ge(consts, 9)
            for i in range(2):
                for a in range(2):
                    last = nc.tensor.matmul(ps_ends[:, i, a * HALF:(a + 1) * HALF], ones[:],
                                            ends_d[:, i, a, :], start=True, stop=True)
            last.then_inc(ends_ps, 1)
            pe.wait_ge(cols_ok, 1)
            for c in range(NCH):
                nc.tensor.matmul(ps_first[:, c * HALF:(c + 1) * HALF], first_c[:, c:c + 1], small,
                                 start=True, stop=True)
                last = nc.tensor.matmul(ps_end[:, c * HALF:(c + 1) * HALF], end_c[:, c:c + 1], small,
                                        start=True, stop=True)
            last.then_inc(cols_ps, 1)


def lead(engine, *sems):
    for s in sems:
        engine.nop().then_inc(s, LEAD)


def edge_messages(nc, m):
    with ExitStack() as ctx:
        sb, pb, sem = scoped(nc, ctx)
        rows = sb("em_rows", [P, SLOTS, F])
        xt = sb("em_xt", [P, 2, P])
        idx = sb("em_idx", [P, SLOTS], I32)
        idx_ok = sem("em_idx_ok")
        ps_t = [pb(f"em_ps_t{i}", [P, P]) for i in range(2)]
        ps_m = [pb(f"em_ps_m{i}", [P, F]) for i in range(2)]
        gathered = [sem(f"em_gathered{i}") for i in range(SLOTS)]
        xt_ready, xt_copied = sem("em_xt_ready"), sem("em_xt_copied")
        product, msg_ok = sem("em_product"), sem("em_msg_ok")
        turns = NT // TURN
        block = ctx.enter_context(nc.Block())

        @block.gpsimd
        def _(pool):
            with pool.Fori(0, turns) as i:
                for j in range(TURN):
                    t = i * TURN + j
                    pool.wait_ge(idx_ok, t + 1)
                    pool.nop(nofuse=True)
                    nc.gpsimd.indirect_dma_start(
                        rows[:, j % SLOTS, :], None, m.x,
                        bass.IndirectOffsetOnAxis(idx[:, j % SLOTS:j % SLOTS + 1], axis=0),
                    ).then_inc(gathered[j % SLOTS], 16)

        @block.tensor
        def _(pe):
            lead(pe, xt_ready, product)

            def turn_rows(i, j):
                t = i * TURN + j
                pe.wait_ge(gathered[j % SLOTS], (i * (TURN // SLOTS) + j // SLOTS) * 16 + 16)
                pe.wait_ge(xt_copied, done(t - 2))
                nc.tensor.transpose(ps_t[j % 2][:], rows[:, j % SLOTS, :], m.ident[:]).then_inc(xt_ready, 1)

            def multiply(i, j):
                t = i * TURN + j
                pe.wait_ge(xt_copied, done(t))
                pe.wait_ge(msg_ok, done(t - 2))
                nc.tensor.matmul(ps_m[j % 2][:], xt[:, j % 2, :], m.w_nb[:], start=True, stop=True).then_inc(product, 1)

            turn_rows(0, 0)
            with pe.Fori(0, turns - 1) as i:
                for j in range(TURN):
                    turn_rows(i, j + 1)
                    multiply(i, j)
            for j in range(TURN):
                if j + 1 < TURN:
                    turn_rows(turns - 1, j + 1)
                multiply(turns - 1, j)

        @block.scalar
        def _(act):
            lead(act, xt_copied)
            with act.Fori(0, turns) as i:
                for j in range(TURN):
                    t = i * TURN + j
                    act.wait_ge(xt_ready, done(t))
                    act.wait_ge(product, done(t - 2))
                    nc.scalar.copy(xt[:, j % 2, :], ps_t[j % 2][:]).then_inc(xt_copied, 1)

        @block.vector
        def _(dve):
            lead(dve, msg_ok)
            for j in range(SLOTS):
                nc.vector.tensor_copy(idx[:, j:j + 1], m.src_i[:, j:j + 1]).then_inc(idx_ok, 1)
            with dve.Fori(0, turns) as i:
                for j in range(TURN):
                    t = i * TURN + j
                    dve.wait_ge(product, done(t))
                    nc.vector.tensor_copy(idx[:, j % SLOTS:j % SLOTS + 1],
                                          m.src_i[:, bass.ds(t + SLOTS, 1)]).then_inc(idx_ok, 1)
                    nc.vector.tensor_scalar(m.msg[:, bass.ds(t, 1), :], ps_m[j % 2][:, None, :],
                                            m.wgt_f[:, bass.ds(t, 1)], None, ALU.mult).then_inc(msg_ok, 1)


def general_sums(nc, m, name):
    with ExitStack() as ctx:
        sb, pb, sem = scoped(nc, ctx)
        onehot = sb("gs_onehot" + name, [P, P])
        dst_n = sb("gs_dst" + name, [P, 2, NT + 1])
        total = sb("gs_total" + name, [P, F])
        ps = pb("gs_ps" + name, [P, F])
        with nc.Block() as block:
            @block.vector
            def _(dve):
                nc.vector.tensor_copy(dst_n[:, 1, :], m.dst_f[:])
        with nc.Fori(0, NB) as n:
            with nc.Block() as block:
                @block.vector
                def _(dve):
                    nc.vector.tensor_copy(dst_n[:, 0, :], dst_n[:, 1, :])
                    nc.vector.memset(total[:], 0.0)
            start = nc.values_load(m.first_i[0:1, bass.ds(n, 1)], min_val=0, max_val=NT - 1)
            end = nc.values_load(m.end_i[0:1, bass.ds(n, 1)], min_val=1, max_val=NT)
            with nc.Fori(start, end) as k:
                with ExitStack() as c1:
                    _, _, sem1 = scoped(nc, c1)
                    hot, summed = sem1("gs_hot" + name), sem1("gs_summed" + name)
                    with nc.Block() as block:
                        @block.vector
                        def _(dve):
                            nc.vector.tensor_scalar(onehot[:], m.local_id[:, 0:P], dst_n[:, 0, bass.ds(k, 1)],
                                                    None, ALU.is_equal).then_inc(hot, 1)
                            dve.wait_ge(summed, 1)
                            nc.vector.tensor_tensor(total[:], total[:], ps[:], ALU.add)

                        @block.tensor
                        def _(pe):
                            pe.wait_ge(hot, 1)
                            nc.tensor.matmul(ps[:], onehot[:], m.msg[:, bass.ds(k, 1), :], start=True,
                                             stop=True).then_inc(summed, 1)
            with ExitStack() as c2:
                _, _, sem2 = scoped(nc, c2)
                stored = sem2("gs_stored" + name)
                with nc.Block() as block:
                    @block.vector
                    def _(dve):
                        nc.vector.tensor_scalar(dst_n[:, 1, :], dst_n[:, 0, :], -float(P), None, ALU.add)

                    @block.sync
                    def _(sp):
                        sp.dma_start(m.sums_d[bass.ds(n * P, P), :], total[:]).then_inc(stored, 16)
                        sp.wait_ge(stored, 16)


def rows_of(a, first, count):
    return a[bass.ds(first, count * P), :].rearrange("(g p) f -> p g f", p=P)


def load_group(engine, to, a, g, landed, tail_landed):
    if isinstance(g, int) and g == GROUPS:
        engine.dma_start(to[:, 0:REST - 1, :], rows_of(a, g * GT * P, REST - 1)).then_inc(landed, 16)
        engine.dma_start(to[0:LAST_ROWS, REST - 1, :], a[(NB - 1) * P:N, :]).then_inc(tail_landed, 16)
    else:
        engine.dma_start(to, rows_of(a, g * (GT * P), GT)).then_inc(landed, 16)


def store_group(engine, a, of, g, landed, tail_landed):
    if isinstance(g, int) and g == GROUPS:
        engine.dma_start(rows_of(a, g * GT * P, REST - 1), of[:, 0:REST - 1, :]).then_inc(landed, 16)
        engine.dma_start(a[(NB - 1) * P:N, :], of[0:LAST_ROWS, REST - 1, :]).then_inc(tail_landed, 16)
    else:
        engine.dma_start(rows_of(a, g * (GT * P), GT), of).then_inc(landed, 16)




def layer0_nodes(nc, m, from_sums):
    name = "n0s_" if from_sums else "n0_"
    with ExitStack() as ctx:
        sb, pb, sem = scoped(nc, ctx)
        xg = sb(name + "xg", [P, 2, GT, F])
        sg = sb(name + "sg", [P, 2, GT, F]) if from_sums else None
        yg = sb(name + "yg", [P, 2, GT, F])
        xt = sb(name + "xt", [P, 2, BT, F])
        onehot = sb(name + "onehot", [P, 2, BT, 2, P])
        dst_g = sb(name + "dst_g", [P, 2, NT + 1])
        stats = sb(name + "stats", [P, 2, BT, 6])
        mv = sb(name + "mv", [P, 2, BT, 2])
        std = sb(name + "std", [P, 2, BT])
        rstd = sb(name + "rstd", [P, 2, BT])
        shift = sb(name + "shift", [P, 2, BT])
        ps_t = [pb(f"{name}ps_t{i}", [P, BT, P]) for i in range(2)]
        ps_h = [pb(f"{name}ps_h{i}", [P, BT, F]) for i in range(2)]
        x_in = [sem(f"{name}x_in{i}") for i in range(2)]
        s_in = [sem(f"{name}s_in{i}") for i in range(2)]
        stored = [sem(f"{name}stored{i}") for i in range(2)]
        x_tail, s_tail, y_tail = (sem(name + n) for n in ("x_tail", "s_tail", "y_tail"))
        xt_ready, xt_copied, h_ready = (sem(name + n) for n in ("xt_ready", "xt_copied", "h_ready"))
        dst_moved, hot_ready = sem(name + "dst_moved"), sem(name + "hot_ready")
        stats_ok, mv_ready, std_ready = (sem(name + n) for n in ("stats_ok", "mv_ready", "std_ready"))
        rstd_ok, shift_ready, y_ready = (sem(name + n) for n in ("rstd_ok", "shift_ready", "y_ready"))
        block = ctx.enter_context(nc.Block())

        @block.sync
        def _(sp):
            def load(i, s):
                b = i * 4 + 2 * s
                sp.wait_ge(xt_ready, done(b - 3))
                load_group(sp, xg[:, s, :, :], m.x, i * 2 + s, x_in[s], x_tail)
                if from_sums:
                    sp.wait_ge(h_ready, done(b - 3))
                    load_group(sp, sg[:, s, :, :], m.sums_d, i * 2 + s, s_in[s], s_tail)

            with sp.Fori(0, PAIRS) as i:
                for s in range(2):
                    load(i, s)
            load(PAIRS, 0)

        @block.gpsimd
        def _(pool):
            def store(i, s):
                pool.wait_ge(y_ready, done(i * 4 + 2 * s + 1))
                store_group(pool, m.x1_d, yg[:, s, :, :], i * 2 + s, stored[s], y_tail)

            with pool.Fori(0, PAIRS) as i:
                for s in range(2):
                    store(i, s)
            store(PAIRS, 0)
            pool.wait_ge(stored[0], PAIRS * 16 + 16)
            pool.wait_ge(stored[1], PAIRS * 16)
            pool.wait_ge(y_tail, 16)

        @block.tensor
        def _(pe):
            lead(pe, xt_ready, h_ready)

            def turn_x(i, o):
                b, u, s = i * 4 + o, o % 2, (o // 2) % 2
                pe.wait_ge(x_in[s], (i + o // 4) * 16 + 16)
                if isinstance(i, int) and i == PAIRS:
                    pe.wait_ge(x_tail, 16)
                pe.wait_ge(xt_copied, done(b - 2))
                for n in range(BT):
                    last = nc.tensor.transpose(ps_t[u][:, n, :], xg[:, s, (o % 2) * BT + n, :], m.ident[:])
                last.then_inc(xt_ready, 1)

            def multiply(i, o):
                b, u, s = i * 4 + o, o % 2, (o // 2) % 2
                if not from_sums:
                    _, first = nc.values_load_multi_w_load_instructions(
                        m.first_i[0:1, bass.ds(b * BT, BT)], engines=[ENG.PE], min_val=0, max_val=NT - 1,
                        skip_runtime_bounds_check_because="the setup holds them to edge tiles")
                pe.wait_ge(xt_copied, done(b))
                pe.wait_ge(y_ready, done(b - 2))
                if from_sums:
                    pe.wait_ge(s_in[s], i * 16 + 16)
                    if isinstance(i, int) and i == PAIRS:
                        pe.wait_ge(s_tail, 16)
                else:
                    pe.wait_ge(hot_ready, done(b))
                for n in range(BT):
                    nc.tensor.matmul(ps_h[u][:, n, :], xt[:, u, n, :], m.w_self[:], start=True, stop=False)
                    if from_sums:
                        last = nc.tensor.matmul(ps_h[u][:, n, :], m.ident[:], sg[:, s, (o % 2) * BT + n, :],
                                                start=False, stop=True)
                    else:
                        for k in range(2):
                            last = nc.tensor.matmul(ps_h[u][:, n, :], onehot[:, u, n, k, :],
                                                    m.msg[:, bass.ds(first[n] + k, 1), :],
                                                    start=False, stop=(k == 1))
                last.then_inc(h_ready, 1)

            turn_x(0, 0)
            with pe.Fori(0, PAIRS) as i:
                for o in range(4):
                    turn_x(i, o + 1)
                    multiply(i, o)
            turn_x(PAIRS, 1)
            multiply(PAIRS, 0)
            multiply(PAIRS, 1)

        @block.scalar
        def _(act):
            lead(act, xt_copied, std_ready, y_ready)

            def copy_xt(i, o):
                b, u = i * 4 + o, o % 2
                act.wait_ge(xt_ready, done(b))
                act.wait_ge(h_ready, done(b - 2))
                nc.scalar.copy(xt[:, u, :, :], ps_t[u][:]).then_inc(xt_copied, 1)

            def root(i, o):
                b, u = i * 4 + o, o % 2
                act.wait_ge(mv_ready, done(b))
                nc.scalar.activation(std[:, u, :], mv[:, u, :, 1], ACT.Sqrt, bias=m.eps_c[:]).then_inc(std_ready, 1)

            def normalise(i, o):
                b, u, s = i * 4 + o, o % 2, (o // 2) % 2
                act.wait_ge(shift_ready, done(b))
                if o % 2 == 0 and not (isinstance(i, int) and i == 0):
                    act.wait_ge(stored[s], i * 16)
                for n in range(BT):
                    last = nc.scalar.activation(yg[:, s, (o % 2) * BT + n, :], ps_h[u][:, n, :], ACT.Identity,
                                                bias=shift[:, u, n:n + 1], scale=rstd[:, u, n:n + 1])
                last.then_inc(y_ready, 1)

            copy_xt(0, 0)
            with act.Fori(0, PAIRS) as i:
                for o in range(4):
                    root(i, o)
                    copy_xt(i, o + 1)
                    normalise(i, o)
            root(PAIRS, 0)
            copy_xt(PAIRS, 1)
            normalise(PAIRS, 0)
            root(PAIRS, 1)
            normalise(PAIRS, 1)

        @block.vector
        def _(dve):
            lead(dve, dst_moved, hot_ready, stats_ok, mv_ready, rstd_ok, shift_ready)
            hots = one_hots(nc, dve, m, dst_g, onehot, dst_moved, hot_ready, h_ready)
            moments, reciprocals = norm_steps(nc, dve, stats, mv, std, rstd, shift,
                                              stats_ok, mv_ready, std_ready, rstd_ok, shift_ready)

            def stats_of(i, o):
                dve.wait_ge(h_ready, done(i * 4 + o))
                moments(i, o, lambda n: ps_h[o % 2][:, n, :])

            if not from_sums:
                hots(0, 0)
            with dve.Fori(0, PAIRS) as i:
                for o in range(4):
                    stats_of(i, o)
                    if not from_sums:
                        hots(i, o + 1)
                    reciprocals(i, o)
            stats_of(PAIRS, 0)
            if not from_sums:
                hots(PAIRS, 1)
            reciprocals(PAIRS, 0)
            stats_of(PAIRS, 1)
            reciprocals(PAIRS, 1)


def one_hots(nc, dve, m, dst_g, onehot, dst_moved, hot_ready, used):
    def hots(i, o):
        b, u, s = i * 4 + o, o % 2, (o // 2) % 2
        if isinstance(i, int) and i == 0 and o == 0:
            nc.vector.tensor_copy(dst_g[:, 0, :], m.dst_f[:]).then_inc(dst_moved, 1)
        elif o % 2 == 0:
            nc.vector.tensor_scalar(dst_g[:, s, :], dst_g[:, 1 - s, :], -float(GT * P), None,
                                    ALU.add).then_inc(dst_moved, 1)
        _, first = nc.values_load_multi_w_load_instructions(
            m.first_i[0:1, bass.ds(b * BT, BT)], engines=[ENG.DVE], min_val=0, max_val=NT - 1,
            skip_runtime_bounds_check_because="the setup holds them to edge tiles")
        dve.wait_ge(dst_moved, done(i * 2 + o // 2))
        dve.wait_ge(used, done(b - 2))
        for n in range(BT):
            node = ((o % 2) * BT + n) * P
            for k in range(2):
                last = nc.vector.tensor_scalar(onehot[:, u, n, k, :], m.local_id[:, node:node + P],
                                               dst_g[:, s, bass.ds(first[n] + k, 1)], None, ALU.is_equal)
        last.then_inc(hot_ready, 1)
    return hots


def norm_steps(nc, dve, stats, mv, std, rstd, shift, stats_ok, mv_ready, std_ready, rstd_ok, shift_ready):
    def moments(i, o, tile):
        b, u = i * 4 + o, o % 2
        for n in range(BT):
            last = nc.vector.bn_stats(stats[:, u, n, :], tile(n))
        last.then_inc(stats_ok, 1)
        dve.wait_ge(stats_ok, done(b))
        dve.nop(nofuse=True)
        for n in range(BT):
            last = nc.vector.bn_aggr(mv[:, u, n, :], stats[:, u, n, :])
        last.then_inc(mv_ready, 1)

    def reciprocals(i, o):
        b, u = i * 4 + o, o % 2
        dve.wait_ge(std_ready, done(b))
        nc.vector.reciprocal(rstd[:, u, :], std[:, u, :]).then_inc(rstd_ok, 1)
        dve.wait_ge(rstd_ok, done(b))
        nc.vector.scalar_tensor_tensor(shift[:, u, :], mv[:, u, :, 0], -1.0, rstd[:, u, :],
                                       ALU.mult, ALU.mult).then_inc(shift_ready, 1)
    return moments, reciprocals


def project_edges(nc, m):
    with ExitStack() as ctx:
        sb, pb, sem = scoped(nc, ctx)
        rows = sb("pe_rows", [P, SLOTS, 2, F])
        idx = sb("pe_idx", [P, SLOTS, 2], I32)
        xt = sb("pe_xt", [P, 2, 2, P])
        qkv = sb("pe_qkv", [P, 2, 3, F])
        qk = sb("pe_qk", [P, 2, H, HD])
        dot = sb("pe_dot", [P, 2, H])
        ps_t = [pb(f"pe_ps_t{i}", [P, 2, P]) for i in range(2)]
        ps_r = [pb(f"pe_ps_r{r}", [P, 3, F]) for r in range(R)]
        src_in = [sem(f"pe_src_in{i}") for i in range(SLOTS)]
        dst_in = [sem(f"pe_dst_in{i}") for i in range(SLOTS)]
        idx_ok, xt_ready, xt_copied = sem("pe_idx_ok"), sem("pe_xt_ready"), sem("pe_xt_copied")
        projected, kept, v_out = sem("pe_projected"), sem("pe_kept"), sem("pe_v_out")
        qk_ok, dot_ok, logit_ok = sem("pe_qk_ok"), sem("pe_dot_ok"), sem("pe_logit_ok")
        turns = NT // TURN
        block = ctx.enter_context(nc.Block())

        @block.gpsimd
        def _(pool):
            with pool.Fori(0, turns) as i:
                for j in range(TURN):
                    t, s = i * TURN + j, j % SLOTS
                    pool.wait_ge(idx_ok, t + 1)
                    pool.nop(nofuse=True)
                    nc.gpsimd.indirect_dma_start(
                        rows[:, s, 0, :], None, m.x1_d,
                        bass.IndirectOffsetOnAxis(idx[:, s, 0:1], axis=0)).then_inc(src_in[s], 16)
                    nc.gpsimd.indirect_dma_start(
                        rows[:, s, 1, :], None, m.x1_d,
                        bass.IndirectOffsetOnAxis(idx[:, s, 1:2], axis=0)).then_inc(dst_in[s], 16)

        @block.tensor
        def _(pe):
            lead(pe, xt_ready, projected)

            def turn_rows(i, j):
                t, s = i * TURN + j, j % SLOTS
                landed = (i * (TURN // SLOTS) + j // SLOTS) * 16 + 16
                pe.wait_ge(src_in[s], landed)
                pe.wait_ge(dst_in[s], landed)
                pe.wait_ge(xt_copied, done(t - 2))
                nc.tensor.transpose(ps_t[j % 2][:, 0, :], rows[:, s, 0, :], m.ident[:])
                nc.tensor.transpose(ps_t[j % 2][:, 1, :], rows[:, s, 1, :], m.ident[:]).then_inc(xt_ready, 1)

            def project(i, j):
                t, u = i * TURN + j, j % 2
                pe.wait_ge(xt_copied, done(t))
                for r in range(R):
                    pe.wait_ge(kept, done(t * R + r - R))
                    nc.tensor.matmul(ps_r[r][:, 0, :], xt[:, u, 1, :], m.w_qkv[:, r, 0, :], start=True, stop=True)
                    nc.tensor.matmul(ps_r[r][:, 1:3, :], xt[:, u, 0, :], m.w_qkv[:, r, 1:3, :],
                                     start=True, stop=True).then_inc(projected, 1)

            turn_rows(0, 0)
            with pe.Fori(0, turns - 1) as i:
                for j in range(TURN):
                    turn_rows(i, j + 1)
                    project(i, j)
            for j in range(TURN):
                if j + 1 < TURN:
                    turn_rows(turns - 1, j + 1)
                project(turns - 1, j)

        @block.scalar
        def _(act):
            lead(act, xt_copied, v_out)

            def copy_xt(i, j):
                t, u = i * TURN + j, j % 2
                act.wait_ge(xt_ready, done(t))
                act.wait_ge(projected, done(t * R - R - 1))
                nc.scalar.copy(xt[:, u, :, :], ps_t[u][:]).then_inc(xt_copied, 1)

            def copy_v(i, j):
                t, u = i * TURN + j, j % 2
                act.wait_ge(kept, done(t * R + R - 1))
                nc.scalar.copy(m.msg[:, bass.ds(t, 1), :], qkv[:, u, 2:3, :]).then_inc(v_out, 1)

            copy_xt(0, 0)
            with act.Fori(0, turns - 1) as i:
                for j in range(TURN):
                    copy_xt(i, j + 1)
                    copy_v(i, j)
            for j in range(TURN):
                if j + 1 < TURN:
                    copy_xt(turns - 1, j + 1)
                copy_v(turns - 1, j)

        @block.vector
        def _(dve):
            lead(dve, kept, qk_ok, dot_ok, logit_ok)
            for j in range(SLOTS):
                nc.vector.tensor_copy(idx[:, j, 0:1], m.src_i[:, j:j + 1])
                nc.vector.tensor_copy(idx[:, j, 1:2], m.dst_i[:, j:j + 1]).then_inc(idx_ok, 1)
            with dve.Fori(0, turns) as i:
                for j in range(TURN):
                    t, u, s = i * TURN + j, j % 2, j % SLOTS
                    dve.wait_ge(v_out, done(t - 2))
                    for r in range(R):
                        mask = m.of_type[:, r, bass.ds(t, 1)]
                        dve.wait_ge(projected, done(t * R + r))
                        if r == 0:
                            nc.vector.tensor_scalar(qkv[:, u, :, :], ps_r[r][:], mask, None, ALU.mult).then_inc(kept, 1)
                            nc.vector.tensor_copy(idx[:, s, 0:1], m.src_i[:, bass.ds(t + SLOTS, 1)])
                            nc.vector.tensor_copy(idx[:, s, 1:2],
                                                  m.dst_i[:, bass.ds(t + SLOTS, 1)]).then_inc(idx_ok, 1)
                        else:
                            dve.wait_ge(kept, done(t * R + r - 1))
                            nc.vector.scalar_tensor_tensor(qkv[:, u, :, :], ps_r[r][:], mask, qkv[:, u, :, :],
                                                           ALU.mult, ALU.add).then_inc(kept, 1)
                    dve.wait_ge(kept, done(t * R + R - 1))
                    nc.vector.tensor_tensor(qk[:, u, :, :].rearrange("p h d -> p (h d)"), qkv[:, u, 0, :],
                                            qkv[:, u, 1, :], ALU.mult).then_inc(qk_ok, 1)
                    dve.wait_ge(qk_ok, done(t))
                    nc.vector.tensor_reduce(dot[:, u, :], qk[:, u, :, :], AX.X, ALU.add).then_inc(dot_ok, 1)
                    dve.wait_ge(dot_ok, done(t))
                    nc.vector.scalar_tensor_tensor(m.logit[:, bass.ds(t, 1), :], dot[:, u:u + 1, :], 1.0 / SCALE,
                                                   m.bias_e[:, bass.ds(t, 1), :], ALU.mult, ALU.add).then_inc(logit_ok, 1)


def segment_softmax(nc, m):
    with ExitStack() as ctx:
        sb, pb, sem = scoped(nc, ctx)
        by_row = sb("ss_by_row", [HALF, 2, H, P])
        own = sb("ss_own", [P, H, NT])
        other = sb("ss_other", [P, 2, H, NT])
        other_key = sb("ss_other_key", [P, 2, NT])
        same = sb("ss_same", [P, 2, NT])
        part = sb("ss_part", [P, H, NT])
        top = sb("ss_top", [P, H, NT])
        total = sb("ss_total", [P, H, NT])
        ps = [pb(f"ss_ps{i}", [HALF, 4, P]) for i in range(4)]
        ps_b = [pb(f"ss_ps_b{i}", [P, 4, HALF]) for i in range(4)]
        band = nc.values_load_multi_w_load_instructions(
            m.band_i[0:1, 0:2], engines=[ENG.Activation, ENG.DVE], min_val=0, max_val=EP,
            skip_runtime_bounds_check_because="the setup holds them within the copies")[1]

        def circle(engine, a, copies_done):
            def store(of, copies):
                for c in range(copies):
                    engine.dma_start(a[:, c * EP:(c + 1) * EP].rearrange("h (p t) -> p h t", t=NT),
                                     of).then_inc(copies_done, 16)
            return store

        def shifted_pass(name, a, step):
            with ExitStack() as inner:
                _, _, sem2 = scoped(nc, inner)
                landed = [sem2(f"{name}_landed{u}") for u in range(2)]
                used, turned = sem2(name + "_used"), sem2(name + "_turned")
                inner_block = inner.enter_context(nc.Block())

                @inner_block.scalar
                def _(act):
                    with act.Fori(0, band[1], 2) as n:
                        for u in range(2):
                            act.wait_ge(used, n + u + 1)
                            act.dma_start(other[:, u, :, :], a[:, bass.ds(band[0] + n + u, EP)].rearrange(
                                "h (p t) -> p h t", t=NT)).then_inc(landed[u], 16)
                            act.dma_start(other_key[:, u, :], m.key_d[bass.ds(band[0] + n + u, EP)].rearrange(
                                "(p t) -> p t", t=NT)).then_inc(landed[u], 16)

                @inner_block.vector
                def _(dve):
                    dve.nop().then_inc(used, 2)
                    with dve.Fori(0, band[1], 2) as n:
                        for u in range(2):
                            dve.wait_ge(landed[u], n * 16 + 32)
                            step(dve, u, n + u, turned, used)

        with ExitStack() as inner:
            _, _, sem1 = scoped(nc, inner)
            turned, copied, stored, loaded = (sem1("ss_" + n) for n in ("turned", "copied", "stored", "loaded"))
            block = inner.enter_context(nc.Block())

            @block.tensor
            def _(pe):
                for a in range(2):
                    for h in range(H):
                        last = nc.tensor.transpose(ps[a * 2 + h // 4][:, h % 4, :],
                                                   m.logit[:, a * HALF:(a + 1) * HALF, h], m.ident[:])
                        if h % 4 == 3:
                            last.then_inc(turned, 1)

            @block.vector
            def _(dve):
                for i in range(4):
                    dve.wait_ge(turned, i + 1)
                    nc.vector.tensor_copy(by_row[:, i // 2, (i % 2) * 4:(i % 2) * 4 + 4, :], ps[i][:]).then_inc(copied, 1)
                nc.vector.memset(top[:], NEG)
                nc.vector.memset(total[:], 0.0)

            @block.sync
            def _(sp):
                for a in range(2):
                    sp.wait_ge(copied, 2 * a + 2)
                    for c in range(3):
                        at = c * EP + a * HALF * P
                        sp.dma_start(m.logit_d[:, at:at + HALF * P].rearrange("h (t e) -> t h e", e=P),
                                     by_row[:, a, :, :]).then_inc(stored, 16)
                sp.wait_ge(stored, 6 * 16)
                sp.dma_start(own[:], m.logit_d[:, 0:EP].rearrange("h (p t) -> p h t", t=NT)).then_inc(loaded, 16)
                sp.wait_ge(loaded, 16)

        def highest(dve, u, n, turned, used):
            nc.vector.tensor_tensor(same[:, u, :], other_key[:, u, :], m.key_b[:], ALU.is_equal).then_inc(turned, 1)
            dve.wait_ge(turned, n * 3 + 1)
            nc.vector.tensor_scalar(same[:, u, :], same[:, u, :], 1.0, MASK, ALU.subtract, ALU.mult).then_inc(turned, 1)
            dve.wait_ge(turned, n * 3 + 2)
            nc.vector.tensor_tensor(part[:], other[:, u, :, :], same[:, u, None, :].broadcast_to([P, H, NT]),
                                    ALU.add).then_inc(turned, 1)
            dve.wait_ge(turned, n * 3 + 3)
            nc.vector.tensor_tensor(top[:], top[:], part[:], ALU.max).then_inc(used, 1)
            dve.wait_ge(used, n + 3)

        def add_up(dve, u, n, turned, used):
            nc.vector.tensor_tensor(same[:, u, :], other_key[:, u, :], m.key_b[:], ALU.is_equal).then_inc(turned, 1)
            dve.wait_ge(turned, n * 2 + 1)
            nc.vector.tensor_tensor(part[:], other[:, u, :, :], same[:, u, None, :].broadcast_to([P, H, NT]),
                                    ALU.mult).then_inc(turned, 1)
            dve.wait_ge(turned, n * 2 + 2)
            nc.vector.tensor_tensor(total[:], total[:], part[:], ALU.add).then_inc(used, 1)
            dve.wait_ge(used, n + 3)

        shifted_pass("ss_max", m.logit_d, highest)

        with ExitStack() as inner:
            _, _, sem1 = scoped(nc, inner)
            less, raised, stored = (sem1("ss_" + n) for n in ("less", "raised", "stored2"))
            block = inner.enter_context(nc.Block())

            @block.vector
            def _(dve):
                nc.vector.tensor_tensor(part[:], own[:], top[:], ALU.subtract).then_inc(less, 1)

            @block.scalar
            def _(act):
                act.wait_ge(less, 1)
                nc.scalar.activation(own[:], part[:], ACT.Exp).then_inc(raised, 1)

            @block.sync
            def _(sp):
                sp.wait_ge(raised, 1)
                circle(sp, m.prob_d, stored)(own[:], 3)
                sp.wait_ge(stored, 3 * 16)

        shifted_pass("ss_sum", m.prob_d, add_up)

        with ExitStack() as inner:
            _, _, sem1 = scoped(nc, inner)
            chain, stored, loaded, turned = (sem1("ss_" + n) for n in ("chain3", "stored3", "loaded3", "turned3"))
            block = inner.enter_context(nc.Block())

            @block.vector
            def _(dve):
                nc.vector.tensor_scalar(total[:], total[:], 1e-12, None, ALU.add).then_inc(chain, 1)
                dve.wait_ge(chain, 1)
                nc.vector.reciprocal(part[:], total[:]).then_inc(chain, 1)
                dve.wait_ge(chain, 2)
                nc.vector.tensor_tensor(own[:], own[:], part[:], ALU.mult).then_inc(chain, 1)
                for i in range(4):
                    dve.wait_ge(turned, i + 1)
                    a, h = i // 2, (i % 2) * 4
                    nc.vector.tensor_copy(m.logit[:, a * HALF:(a + 1) * HALF, h:h + 4].rearrange("p t h -> p h t"),
                                          ps_b[i][:])

            @block.sync
            def _(sp):
                sp.wait_ge(chain, 3)
                sp.dma_start(m.attn_d.rearrange("h (p t) -> p h t", t=NT), own[:]).then_inc(stored, 16)
                sp.wait_ge(stored, 16)
                for a in range(2):
                    sp.dma_start(by_row[:, a, :, :], m.attn_d[:, a * HALF * P:(a + 1) * HALF * P].rearrange(
                        "h (t e) -> t h e", e=P)).then_inc(loaded, 16)

            @block.tensor
            def _(pe):
                pe.wait_ge(loaded, 32)
                for i in range(4):
                    for h in range(4):
                        last = nc.tensor.transpose(ps_b[i][:, h, :], by_row[:, i // 2, (i % 2) * 4 + h, :],
                                                   m.ident[0:HALF, 0:HALF])
                    last.then_inc(turned, 1)


def attended_messages(nc, m):
    with ExitStack() as ctx:
        sb, pb, sem = scoped(nc, ctx)
        av = sb("am_av", [P, 2, H, HD])
        avt = sb("am_avt", [P, 2, P])
        ps_t = [pb(f"am_ps_t{i}", [P, P]) for i in range(2)]
        ps_m = [pb(f"am_ps_m{i}", [P, F]) for i in range(2)]
        av_ready, avt_ready, avt_copied = sem("am_av_ready"), sem("am_avt_ready"), sem("am_avt_copied")
        product, msg_ok = sem("am_product"), sem("am_msg_ok")
        turns = NT // STEPS
        block = ctx.enter_context(nc.Block())

        @block.vector
        def _(dve):
            lead(dve, av_ready)
            with dve.Fori(0, turns) as i:
                for j in range(STEPS):
                    t, u = i * STEPS + j, j % 2
                    dve.wait_ge(avt_ready, done(t - 2))
                    nc.vector.tensor_tensor(
                        av[:, u, :, :], m.msg[:, bass.ds(t, 1), :].rearrange("p o (h d) -> p (o h) d", h=H),
                        m.logit[:, bass.ds(t, 1), :].rearrange("p o h -> p (o h)")[:, :, None].broadcast_to([P, H, HD]),
                        ALU.mult).then_inc(av_ready, 1)

        @block.tensor
        def _(pe):
            lead(pe, avt_ready, product)

            def turn(i, j):
                t = i * STEPS + j
                pe.wait_ge(av_ready, done(t))
                pe.wait_ge(avt_copied, done(t - 2))
                nc.tensor.transpose(ps_t[j % 2][:], av[:, j % 2, :, :].rearrange("p h d -> p (h d)"),
                                    m.ident[:]).then_inc(avt_ready, 1)

            def multiply(i, j):
                t = i * STEPS + j
                pe.wait_ge(avt_copied, done(t))
                pe.wait_ge(msg_ok, done(t - 2))
                nc.tensor.matmul(ps_m[j % 2][:], avt[:, j % 2, :], m.w_out[:], start=True, stop=True).then_inc(product, 1)

            turn(0, 0)
            with pe.Fori(0, turns - 1) as i:
                for j in range(STEPS):
                    turn(i, j + 1)
                    multiply(i, j)
            for j in range(STEPS):
                if j + 1 < STEPS:
                    turn(turns - 1, j + 1)
                multiply(turns - 1, j)

        @block.scalar
        def _(act):
            lead(act, avt_copied, msg_ok)

            def copy_avt(i, j):
                t, u = i * STEPS + j, j % 2
                act.wait_ge(avt_ready, done(t))
                act.wait_ge(product, done(t - 2))
                nc.scalar.copy(avt[:, u, :], ps_t[u][:]).then_inc(avt_copied, 1)

            def copy_msg(i, j):
                t = i * STEPS + j
                act.wait_ge(product, done(t))
                nc.scalar.copy(m.msg[:, bass.ds(t, 1), :], ps_m[j % 2][:, None, :]).then_inc(msg_ok, 1)

            copy_avt(0, 0)
            with act.Fori(0, turns - 1) as i:
                for j in range(STEPS):
                    copy_avt(i, j + 1)
                    copy_msg(i, j)
            for j in range(STEPS):
                if j + 1 < STEPS:
                    copy_avt(turns - 1, j + 1)
                copy_msg(turns - 1, j)


def layer1_nodes(nc, m, from_sums):
    name = "n1s_" if from_sums else "n1_"
    with ExitStack() as ctx:
        sb, pb, sem = scoped(nc, ctx)
        xg = sb(name + "xg", [P, 2, GT, F])
        sg = sb(name + "sg", [P, 2, GT, F]) if from_sums else None
        yg = sb(name + "yg", [P, 2, GT, F])
        xbeta = sb(name + "xbeta", [P, 2, BT, F])
        norm = sb(name + "norm", [P, 2, BT, F])
        scaled = sb(name + "scaled", [P, 2, BT, F])
        z = sb(name + "z", [P, 2, BT, F])
        onehot = sb(name + "onehot", [P, 2, BT, 2, P])
        dst_g = sb(name + "dst_g", [P, 2, NT + 1])
        ps_h = [pb(f"{name}ps_h{i}", [P, BT, F]) for i in range(2)]
        x_in = [sem(f"{name}x_in{i}") for i in range(2)]
        s_in = [sem(f"{name}s_in{i}") for i in range(2)]
        stored = [sem(f"{name}stored{i}") for i in range(2)]
        x_tail, s_tail, y_tail = (sem(name + n) for n in ("x_tail", "s_tail", "y_tail"))
        h_ready, dst_moved, hot_ready = (sem(name + n) for n in ("h_ready", "dst_moved", "hot_ready"))
        norm_ready, y_ready = sem(name + "norm_ready"), sem(name + "y_ready")
        xbeta_ready, scaled_ready, z_ready = (sem(name + n) for n in ("xbeta_ready", "scaled_ready", "z_ready"))
        buf, ev = [], []
        for k in range(2):
            buf.append([sb(f"{name}{n}{k}", [P, 2, BT, *w]) for n, w in (
                ("stats", [6]), ("mv", [2]), ("std", []), ("rstd", []), ("shift", []))])
            ev.append([sem(f"{name}{n}{k}") for n in ("stats_ok", "mv_ready", "std_ready", "rstd_ok", "shift_ready")])
        block = ctx.enter_context(nc.Block())

        @block.sync
        def _(sp):
            def load(i, s):
                b = i * 4 + 2 * s
                sp.wait_ge(h_ready, done(b - 3))
                sp.wait_ge(xbeta_ready, done(b - 3))
                load_group(sp, xg[:, s, :, :], m.x1_d, i * 2 + s, x_in[s], x_tail)
                if from_sums:
                    load_group(sp, sg[:, s, :, :], m.sums_d, i * 2 + s, s_in[s], s_tail)

            def store(i, s):
                sp.wait_ge(y_ready, done(i * 4 + 2 * s + 1))
                store_group(sp, m.out, yg[:, s, :, :], i * 2 + s, stored[s], y_tail)

            load(0, 0)
            load(0, 1)
            with sp.Fori(0, PAIRS - 1) as i:
                for s in range(2):
                    store(i, s)
                    load(i + 1, s)
            store(PAIRS - 1, 0)
            load(PAIRS, 0)
            store(PAIRS - 1, 1)
            store(PAIRS, 0)
            sp.wait_ge(stored[0], PAIRS * 16 + 16)
            sp.wait_ge(stored[1], PAIRS * 16)
            sp.wait_ge(y_tail, 16)

        def x_landed(engine, i, o):
            engine.wait_ge(x_in[(o // 2) % 2], (i + o // 4) * 16 + 16)
            if isinstance(i, int) and i == PAIRS:
                engine.wait_ge(x_tail, 16)

        @block.tensor
        def _(pe):
            lead(pe, h_ready)

            def multiply(i, o):
                b, u, s, half = i * 4 + o, o % 2, (o // 2) % 2, (o % 2) * BT
                if not from_sums:
                    _, first = nc.values_load_multi_w_load_instructions(
                        m.first_i[0:1, bass.ds(b * BT, BT)], engines=[ENG.PE], min_val=0, max_val=NT - 1,
                        skip_runtime_bounds_check_because="the setup holds them to edge tiles")
                x_landed(pe, i, o)
                pe.wait_ge(norm_ready, done(b - 2))
                if from_sums:
                    pe.wait_ge(s_in[s], i * 16 + 16)
                    if isinstance(i, int) and i == PAIRS:
                        pe.wait_ge(s_tail, 16)
                else:
                    pe.wait_ge(hot_ready, done(b))
                for n in range(BT):
                    nc.tensor.matmul(ps_h[u][:, n, :], m.ident[:], xg[:, s, half + n, :], start=True, stop=False)
                    nc.tensor.matmul(ps_h[u][:, n, :], m.ones_row[:], m.bo_row[:, n, :], start=False, stop=False)
                    if from_sums:
                        last = nc.tensor.matmul(ps_h[u][:, n, :], m.ident[:], sg[:, s, half + n, :],
                                                start=False, stop=True)
                    else:
                        for k in range(2):
                            last = nc.tensor.matmul(ps_h[u][:, n, :], onehot[:, u, n, k, :],
                                                    m.msg[:, bass.ds(first[n] + k, 1), :],
                                                    start=False, stop=(k == 1))
                last.then_inc(h_ready, 1)

            with pe.Fori(0, PAIRS) as i:
                for o in range(4):
                    multiply(i, o)
            multiply(PAIRS, 0)
            multiply(PAIRS, 1)

        @block.scalar
        def _(act):
            lead(act, norm_ready, y_ready, ev[0][2], ev[1][2])

            def root(k, i, o):
                b, u = i * 4 + o, o % 2
                _, mv, std, _, _ = buf[k]
                act.wait_ge(ev[k][1], done(b))
                nc.scalar.activation(std[:, u, :], mv[:, u, :, 1], ACT.Sqrt, bias=m.eps_c[:]).then_inc(ev[k][2], 1)

            def normalise(k, to, of, i, o, ready):
                u = o % 2
                _, _, _, rstd, shift = buf[k]
                act.wait_ge(ev[k][4], done(i * 4 + o))
                for n in range(BT):
                    last = nc.scalar.activation(to(n), of(n), ACT.Identity, bias=shift[:, u, n:n + 1],
                                                scale=rstd[:, u, n:n + 1])
                last.then_inc(ready, 1)

            def first_norm(i, o):
                root(0, i, o)
                act.wait_ge(scaled_ready, done(i * 4 + o - 2))
                normalise(0, lambda n: norm[:, o % 2, n, :], lambda n: ps_h[o % 2][:, n, :], i, o, norm_ready)

            def second_norm(i, o):
                s = (o // 2) % 2
                root(1, i, o)
                if o % 2 == 0:
                    act.wait_ge(stored[s], (i + o // 4) * 16)
                normalise(1, lambda n: yg[:, s, (o % 2) * BT + n, :], lambda n: z[:, o % 2, n, :], i, o, y_ready)

            first_norm(0, 0)
            with act.Fori(0, PAIRS) as i:
                for o in range(4):
                    first_norm(i, o + 1)
                    second_norm(i, o)
            first_norm(PAIRS, 1)
            second_norm(PAIRS, 0)
            second_norm(PAIRS, 1)

        @block.gpsimd
        def _(pool):
            lead(pool, xbeta_ready, scaled_ready)
            beta4 = m.bet_b[:, None, :].broadcast_to([P, BT, F])
            gamma4 = m.gam_b[:, None, :].broadcast_to([P, BT, F])

            def add_beta(i, o):
                b, u, s, half = i * 4 + o, o % 2, (o // 2) % 2, (o % 2) * BT
                x_landed(pool, i, o)
                pool.wait_ge(z_ready, done(b - 2))
                nc.gpsimd.tensor_tensor(xbeta[:, u, :, :], xg[:, s, half:half + BT, :], beta4, ALU.add).then_inc(xbeta_ready, 1)

            def scale(i, o):
                b, u = i * 4 + o, o % 2
                pool.wait_ge(norm_ready, done(b))
                pool.wait_ge(z_ready, done(b - 2))
                nc.gpsimd.tensor_tensor(scaled[:, u, :, :], norm[:, u, :, :], gamma4, ALU.mult).then_inc(scaled_ready, 1)

            add_beta(0, 0)
            with pool.Fori(0, PAIRS) as i:
                for o in range(4):
                    add_beta(i, o + 1)
                    scale(i, o)
            add_beta(PAIRS, 1)
            scale(PAIRS, 0)
            scale(PAIRS, 1)

        @block.vector
        def _(dve):
            lead(dve, dst_moved, hot_ready, z_ready, *(e for k in range(2) for e in (ev[k][0], ev[k][1], ev[k][3], ev[k][4])))
            hots = one_hots(nc, dve, m, dst_g, onehot, dst_moved, hot_ready, h_ready)
            moments, reciprocals = zip(*(norm_steps(nc, dve, *buf[k], *ev[k]) for k in range(2)))

            def first_half(i, o, more):
                dve.wait_ge(h_ready, done(i * 4 + o))
                moments[0](i, o, lambda n: ps_h[o % 2][:, n, :])
                if more and not from_sums:
                    hots(i, o + 1)
                reciprocals[0](i, o)

            def second_half(i, o):
                b, u = i * 4 + o, o % 2
                dve.wait_ge(scaled_ready, done(b))
                dve.wait_ge(xbeta_ready, done(b))
                dve.wait_ge(y_ready, done(b - 2))
                nc.vector.tensor_tensor(z[:, u, :, :], scaled[:, u, :, :], xbeta[:, u, :, :], ALU.add).then_inc(z_ready, 1)
                dve.wait_ge(z_ready, done(b))
                moments[1](i, o, lambda n: z[:, u, n, :])
                reciprocals[1](i, o)

            if not from_sums:
                hots(0, 0)
            first_half(0, 0, True)
            with dve.Fori(0, PAIRS) as i:
                for o in range(4):
                    first_half(i, o + 1, True)
                    second_half(i, o)
            first_half(PAIRS, 1, False)
            second_half(PAIRS, 0)
            second_half(PAIRS, 1)


_INS = ["x", "src", "dst", "edge_type_5", "edge_weight", "L0_gnn_W", "L1_gnn_W_Q", "L1_gnn_W_K", "L1_gnn_W_V",
        "L1_gnn_attn_bias", "L1_gnn_out_proj_w", "L1_gnn_out_proj_b", "L1_gnn_ln_gamma", "L1_gnn_ln_beta"]


def kernel(**inputs):
    import numpy as _np
    import concourse.bacc as _bacc
    from concourse.bass_utils import run_bass_kernel_spmd as _run

    nc = _bacc.Bacc("TRN2", target_bir_lowering=False, num_devices=1)
    arrays, args = {}, []
    for name in _INS:
        a = _np.ascontiguousarray(inputs[name])
        arrays[f"in_{name}"] = a
        args.append(nc.dram_tensor(f"in_{name}", a.shape, mybir.dt.from_np(a.dtype), kind="ExternalInput").ap())
    args.append(nc.dram_tensor("out_x", (N, F), F32, kind="ExternalOutput").ap())
    gnn(nc, *args)
    r = _run(nc, [arrays], core_ids=[0])
    return r.results[0]["out_x"]
```

```python
import concourse.bass as bass
from concourse import mybir
from contextlib import ExitStack

F32 = mybir.dt.float32
I32 = mybir.dt.int32
BF16 = mybir.dt.bfloat16
ALU = mybir.AluOpType
ACT = mybir.ActivationFunctionType
AX = mybir.AxisListType
ENG = mybir.EngineType

P = 128
N, F = 50000, 128
E, R, H, HD = 25000, 5, 8, 16
NT = (E + P - 1) // P
EP = NT * P
HALF = NT // 2
TAIL = E - (NT - 1) * P
NB = (N + P - 1) // P
LAST_ROWS = N - (NB - 1) * P
BT = 4
GB = 2
GT = BT * GB
GROUPS = NB // GT
XSLOTS = 4
TB = XSLOTS * GB
ROUNDS = GROUPS // XSLOTS
REST = NB - GROUPS * GT
NCH = 4
PAD_DST = 1 << 17
NO_DST = 1.0e6
EPS = 1e-5
NEG = -1.0e9
MASK = 1.0e30
SCALE = float(HD) ** 0.5
LEAD = 8
SLOTS = 7
STEPS = 4
TURN = 14
FAR = [(8, 63), (64, 511), (512, 4095), (4096, EP)]
NEAR = 7
NPROBE = NEAR + len(FAR) + 1


def done(step):
    return LEAD + 1 + step


class Memory:
    pass


def scoped(nc, ctx):
    sems = []

    def clear():
        if sems:
            nc.clear_and_free_semaphores(sems)
            nc.all_engine_barrier(sem_only=True)

    ctx.callback(clear)

    def sb(name, shape, dt=F32):
        return ctx.enter_context(nc.sbuf_tensor(name, shape, dt))

    def pb(name, shape):
        return ctx.enter_context(nc.psum_tensor(name, shape, F32))

    def sem(name):
        sems.append(nc.alloc_semaphore(name))
        return sems[-1]

    return sb, pb, sem


def gnn(nc, x, src, dst, typ, wgt, w0, wq, wk, wv, bias, wo, bo, gamma, beta, out):
    m = Memory()
    m.x, m.src, m.dst, m.typ, m.wgt, m.out = x, src, dst, typ, wgt, out
    m.w0, m.wq, m.wk, m.wv, m.wo = w0, wq, wk, wv, wo
    m.bias, m.bo, m.gamma, m.beta = bias, bo, gamma, beta
    m.x1_d = nc.dram_tensor("x1_d", [N, F], F32).ap()
    m.sums_d = nc.dram_tensor("sums_d", [NB * P, F], F32).ap()
    m.key_d = nc.dram_tensor("key_d", [3 * EP], F32).ap()
    m.typ_d = nc.dram_tensor("typ_d", [EP], F32).ap()
    m.dst_d = nc.dram_tensor("dst_d", [EP + FAR[-1][0]], F32).ap()
    m.logit_d = nc.dram_tensor("logit_d", [H, 3 * EP], F32).ap()
    m.prob_d = nc.dram_tensor("prob_d", [H, 3 * EP], F32).ap()
    m.attn_d = nc.dram_tensor("attn_d", [H, EP], F32).ap()

    with ExitStack() as ctx:
        sb, _, _ = scoped(nc, ctx)
        m.msg = sb("msg", [P, NT + 1, F])
        m.ident = sb("ident", [P, P])
        m.local_id = sb("local_id", [P, GT * P])
        m.edge_i = sb("edge_i", [P, NT + SLOTS, 2], I32)
        m.dst_f = sb("dst_f", [P, NT + 1])
        m.wgt_f = sb("wgt_f", [P, NT])
        m.of_type = sb("of_type", [P, R, NT])
        m.key_b = sb("key_b", [P, NT])
        m.bias_e = sb("bias_e", [P, NT, H])
        m.w_self = sb("w_self", [P, F])
        m.w_nb = sb("w_nb", [P, F])
        m.w_out = sb("w_out", [P, F])
        m.w_qkv = sb("w_qkv", [P, R, 3, F])
        m.gam_b = sb("gam_b", [P, F])
        m.bet_b = sb("bet_b", [P, F])
        m.bo_parts = sb("bo_parts", [3, BT * F], BF16)
        m.ones_3 = sb("ones_3", [3, P], BF16)
        m.logit = sb("logit", [P, NT, H])
        m.eps_c = sb("eps_c", [P, 1])
        m.first_i = sb("first_i", [1, NCH * HALF + 2 * BT], I32)
        m.end_i = sb("end_i", [1, NCH * HALF], I32)
        m.wide_i = sb("wide_i", [1, 1], I32)
        m.band_i = sb("band_i", [1, 2], I32)

        setup(nc, m)
        edge_messages(nc, m)
        wide = nc.values_load(m.wide_i[0:1, 0:1], min_val=0, max_val=1)
        with nc.If(wide == 1):
            general_sums(nc, m, "a")
            layer0_nodes(nc, m, from_sums=True)
        with nc.Else():
            layer0_nodes(nc, m, from_sums=False)
        project_edges(nc, m)
        segment_softmax(nc, m)
        attended_messages(nc, m)
        with nc.If(wide == 1):
            general_sums(nc, m, "b")
            layer1_nodes(nc, m, from_sums=True)
        with nc.Else():
            layer1_nodes(nc, m, from_sums=False)


def setup(nc, m):
    with ExitStack() as ctx:
        sb, pb, sem = scoped(nc, ctx)
        src_r, dst_r, typ_r = (sb(n, [HALF, 2, P], I32) for n in ("src_r", "dst_r", "typ_r"))
        wgt_r, srcf_r, dstf_r, typf_r, dstc_r, key_r = (
            sb(n, [HALF, 2, P]) for n in ("wgt_r", "srcf_r", "dstf_r", "typf_r", "dstc_r", "key_r"))
        pad_dst = sb("pad_dst", [1, P - TAIL], I32)
        pad_0 = sb("pad_0", [1, P - TAIL], I32)
        pad_w = sb("pad_w", [1, P - TAIL])
        no_dst = sb("no_dst", [32, P])
        typ_f = sb("typ_f", [P, NT])
        w0_r = sb("w0_r", [P, F])
        wo_r = sb("wo_r", [P, F])
        bias_r = sb("bias_r", [P, R, H])
        bias_t = sb("bias_t", [P, NT, H])
        ones = sb("ones", [HALF, P])
        bo_r = sb("bo_r", [3, BT, F])
        bo_left = sb("bo_left", [3, BT * F])
        bo_part = sb("bo_part", [3, 3, BT * F], BF16)
        bo_sum = sb("bo_sum", [3, BT * F])
        ends = sb("ends", [HALF, 2, 2])
        ends_d = sb("ends_d", [HALF, 2, 2, HALF])
        ends_b = sb("ends_b", [P, 2, NT])
        node_0 = sb("node_0", [HALF, NCH])
        node_1 = sb("node_1", [HALF, NCH])
        below = sb("below", [HALF, NCH, NT])
        cover = sb("cover", [HALF, NCH, NT])
        tile_1 = sb("tile_1", [HALF, NT])
        tile_hi = sb("tile_hi", [HALF, NT])
        cand = sb("cand", [HALF, NCH, NT])
        cand2 = sb("cand2", [HALF, NCH, NT])
        first_c = sb("first_c", [HALF, NCH])
        end_c = sb("end_c", [HALF, NCH])
        first_f = sb("first_f", [1, NCH * HALF])
        end_f = sb("end_f", [1, NCH * HALF])
        span_f = sb("span_f", [1, NCH * HALF])
        widest = sb("widest", [1, 1])
        shifted = sb("shifted", [P, NPROBE, NT])
        dst_b = sb("dst_b", [P, NT])
        same = sb("same", [P, NPROBE, NT])
        found = sb("found", [P, NPROBE])
        found_all = sb("found_all", [P, NPROBE])
        reach_of = sb("reach_of", [1, NPROBE])
        reach = sb("reach", [1, NPROBE + 4])
        ps_edge = [pb(f"ps_edge{i}", [P, 2, NT]) for i in range(3)]
        ps_w = pb("ps_w", [P, 2, F])
        ps_ends = pb("ps_ends", [P, 2, NT])
        ps_first = pb("ps_first", [1, NCH * HALF])
        ps_end = pb("ps_end", [1, NCH * HALF])

        edges_in, weights_in, pads = sem("edges_in"), sem("weights_in"), sem("pads")
        consts, zeroed, ident_ok = sem("consts"), sem("zeroed"), sem("ident_ok")
        rows_ok, circ_out, probes_in = sem("rows_ok"), sem("circ_out"), sem("probes_in")
        transposed, ends_ok, ends_ps = sem("transposed"), sem("ends_ok"), sem("ends_ps")
        cols_ok, cols_ps, found_ok, found_red = (
            sem("cols_ok"), sem("cols_ps"), sem("found_ok"), sem("found_red"))
        chain = sem("chain")

        block = ctx.enter_context(nc.Block())
        main = (NT - 1) * P

        @block.sync
        def _(sp):
            sp.wait_ge(pads, 4)
            for a, rows, pad in ((m.src, src_r, pad_0), (m.dst, dst_r, pad_dst),
                                 (m.typ, typ_r, pad_0), (m.wgt, wgt_r, pad_w)):
                sp.dma_start(rows[:, 0, :], a[0:HALF * P].rearrange("(p c) -> p c", c=P)).then_inc(edges_in, 16)
                sp.dma_start(rows[0:HALF - 1, 1, :],
                             a[HALF * P:main].rearrange("(p c) -> p c", c=P)).then_inc(edges_in, 16)
                sp.dma_start(rows[HALF - 1:HALF, 1, 0:TAIL],
                             a[main:E].rearrange("(p c) -> p c", p=1)).then_inc(edges_in, 16)
                sp.dma_start(rows[HALF - 1:HALF, 1, TAIL:P], pad[:]).then_inc(edges_in, 16)
            sp.wait_ge(rows_ok, 1)
            for a in range(2):
                at = a * HALF * P
                sp.dma_start(m.dst_d[at:at + HALF * P].rearrange("(p c) -> p c", c=P),
                             dstf_r[:, a, :]).then_inc(circ_out, 16)
                sp.dma_start(m.typ_d[at:at + HALF * P].rearrange("(p c) -> p c", c=P),
                             typf_r[:, a, :]).then_inc(circ_out, 16)
                for copy in range(3):
                    at = copy * EP + a * HALF * P
                    sp.dma_start(m.key_d[at:at + HALF * P].rearrange("(p c) -> p c", c=P),
                                 key_r[:, a, :]).then_inc(circ_out, 16)
            sp.dma_start(m.dst_d[EP:EP + FAR[-1][0]].rearrange("(p c) -> p c", c=P),
                         no_dst[:]).then_inc(circ_out, 16)
            sp.wait_ge(circ_out, 11 * 16)

            def probe(to, a, shift):
                sp.dma_start(to, a[shift:shift + EP].rearrange("(p t) -> p t", t=NT)).then_inc(probes_in, 16)

            probe(m.key_b[:], m.key_d, 0)
            probe(dst_b[:], m.dst_d, 0)
            for d in range(1, NEAR + 1):
                probe(shifted[:, d - 1, :], m.key_d, d)
            for i, (d, _) in enumerate(FAR):
                probe(shifted[:, NEAR + i, :], m.dst_d, d)
            probe(shifted[:, NPROBE - 1, :], m.dst_d, 1)

        @block.scalar
        def _(act):
            act.dma_start(w0_r[:], m.w0).then_inc(weights_in, 16)
            act.dma_start(wo_r[:], m.wo).then_inc(weights_in, 16)
            act.dma_start(bias_r[:], m.bias.partition_broadcast(P)).then_inc(weights_in, 16)
            act.dma_start(m.gam_b[:], m.gamma.partition_broadcast(P)).then_inc(weights_in, 16)
            act.dma_start(m.bet_b[:], m.beta.partition_broadcast(P)).then_inc(weights_in, 16)
            act.dma_start(bo_r[:], m.bo[None, None, :].broadcast_to([3, BT, F])).then_inc(weights_in, 16)
            for i, w in enumerate((m.wq, m.wk, m.wv)):
                for r in range(R):
                    act.dma_start(m.w_qkv[:, r, i, :].rearrange("i (h d) -> i h d", h=H),
                                  w[r].rearrange("h i d -> i h d")).then_inc(weights_in, 16)
            act.wait_ge(weights_in, (6 + 3 * R) * 16)

        @block.gpsimd
        def _(pool):
            nc.gpsimd.iota(pad_dst[:], [[1, P - TAIL]], base=PAD_DST + TAIL, channel_multiplier=0).then_inc(pads, 1)
            nc.gpsimd.memset(pad_0[:], 0).then_inc(pads, 1)
            nc.gpsimd.memset(pad_w[:], 0.0).then_inc(pads, 1)
            nc.gpsimd.memset(no_dst[:], NO_DST).then_inc(pads, 1)
            nc.gpsimd.memset(m.ident[:], 0.0).then_inc(zeroed, 1)
            pool.wait_ge(zeroed, 1)
            nc.gpsimd.affine_select(out=m.ident[:], in_=m.ident[:], compare_op=ALU.not_equal, fill=1.0,
                                    base=0, pattern=[[-1, P]], channel_multiplier=1).then_inc(ident_ok, 1)
            nc.gpsimd.iota(m.local_id[:], [[1, GT * P]], base=0, channel_multiplier=0,
                           allow_small_or_imprecise_dtypes=True).then_inc(consts, 1)
            nc.gpsimd.iota(node_0[:], [[HALF * P, NCH]], base=0, channel_multiplier=P,
                           allow_small_or_imprecise_dtypes=True).then_inc(consts, 1)
            nc.gpsimd.memset(ones[:], 1.0).then_inc(consts, 1)
            nc.gpsimd.memset(m.ones_3[:], 1.0).then_inc(consts, 1)
            nc.gpsimd.memset(m.eps_c[:], EPS).then_inc(consts, 1)
            nc.gpsimd.memset(m.msg[:, NT, :], 0.0).then_inc(consts, 1)
            nc.gpsimd.memset(m.edge_i[:, NT:NT + SLOTS, :], 0).then_inc(consts, 1)
            nc.gpsimd.memset(m.dst_f[:, NT:NT + 1], NO_DST).then_inc(consts, 1)
            pool.wait_ge(found_ok, 1)
            nc.gpsimd.partition_all_reduce(found_all[:], found[:], P, bass.bass_isa.ReduceOp.max).then_inc(found_red, 1)

        @block.vector
        def _(dve):
            links = [0]

            def link(ins):
                links[0] += 1
                ins.then_inc(chain, 1)
                dve.wait_ge(chain, links[0])

            dve.wait_ge(edges_in, 16 * 16)
            nc.vector.tensor_copy(srcf_r[:], src_r[:])
            nc.vector.tensor_copy(typf_r[:], typ_r[:])
            link(nc.vector.tensor_copy(dstf_r[:], dst_r[:]))
            nc.vector.tensor_scalar(dstc_r[:], dstf_r[:], float(N - 1), None, ALU.min)
            nc.vector.tensor_reduce(ends[:, 0, :], dstf_r[:], AX.X, ALU.min)
            nc.vector.tensor_reduce(ends[:, 1, :], dstf_r[:], AX.X, ALU.max)
            nc.vector.scalar_tensor_tensor(key_r[:], dstf_r[:], 8.0, typf_r[:], ALU.mult, ALU.add).then_inc(rows_ok, 1)
            dve.wait_ge(rows_ok, 1)
            dve.wait_ge(ident_ok, 1)
            for i in range(2):
                for a in range(2):
                    last = nc.vector.tensor_scalar(ends_d[:, i, a, :], m.ident[0:HALF, 0:HALF],
                                                   ends[:, i, a:a + 1], None, ALU.mult)
            last.then_inc(ends_ok, 1)
            for i, d in enumerate([*range(1, NEAR + 1), *(far for _, far in FAR), EP]):
                last = nc.vector.memset(reach_of[:, i:i + 1], float(d))
            link(last)

            dve.wait_ge(transposed, 1)
            nc.vector.tensor_copy(m.edge_i[:, 0:NT, :], ps_edge[0][:].rearrange("p i t -> p t i"))
            nc.vector.tensor_copy(m.dst_f[:, 0:NT], ps_edge[1][:, 0, :])
            nc.vector.tensor_copy(m.wgt_f[:], ps_edge[1][:, 1, :])
            nc.vector.tensor_copy(typ_f[:], ps_edge[2][:, 0, :])
            nc.vector.tensor_copy(m.w_nb[:], ps_w[:, 0, :])
            nc.vector.tensor_copy(m.w_out[:], ps_w[:, 1, :])
            link(nc.vector.tensor_tensor(m.w_self[:], ps_w[:, 0, :], m.ident[:], ALU.add))
            for r in range(R):
                last = nc.vector.tensor_scalar(m.of_type[:, r, :], typ_f[:], float(r), None, ALU.is_equal)
            link(last)

            dve.wait_ge(ends_ps, 1)
            dve.wait_ge(consts, 8)
            nc.vector.tensor_copy(ends_b[:], ps_ends[:])
            nc.vector.tensor_scalar(tile_1[:], m.local_id[0:HALF, 0:NT], 1.0, None, ALU.add)
            nc.vector.tensor_scalar(tile_hi[:], m.local_id[0:HALF, 0:NT], float(EP), None, ALU.add)
            link(nc.vector.tensor_scalar(node_1[:], node_0[:], float(P), None, ALU.add))
            for c in range(NCH):
                last = nc.vector.tensor_scalar(below[:, c, :], ends_b[0:HALF, 0, :], node_1[:, c:c + 1],
                                               None, ALU.is_lt)
            link(last)
            for c in range(NCH):
                last = nc.vector.scalar_tensor_tensor(cover[:, c, :], ends_b[0:HALF, 1, :], node_0[:, c:c + 1],
                                                      below[:, c, :], ALU.is_ge, ALU.mult)
            link(last)
            nc.vector.scalar_tensor_tensor(cand[:], cover[:], -float(EP), tile_hi[:, None, :].broadcast_to([HALF, NCH, NT]),
                                           ALU.mult, ALU.add)
            link(nc.vector.tensor_tensor(cand2[:], cover[:], tile_1[:, None, :].broadcast_to([HALF, NCH, NT]), ALU.mult))
            nc.vector.tensor_reduce(first_c[:], cand[:], AX.X, ALU.min)
            nc.vector.tensor_reduce(end_c[:], cand2[:], AX.X, ALU.max).then_inc(cols_ok, 1)
            dve.wait_ge(cols_ps, 1)
            link(nc.vector.tensor_scalar(first_f[:], ps_first[:], float(NT - 1), None, ALU.min))
            nc.vector.tensor_copy(m.first_i[:, 0:NCH * HALF], first_f[:])
            nc.vector.memset(m.first_i[:, NCH * HALF:NCH * HALF + 2 * BT], 0)
            link(nc.vector.scalar_tensor_tensor(end_f[:], first_f[:], 1.0, ps_end[:], ALU.add, ALU.max))
            nc.vector.tensor_copy(m.end_i[:], end_f[:])
            link(nc.vector.tensor_tensor(span_f[:], end_f[:], first_f[:], ALU.subtract))
            link(nc.vector.tensor_reduce(widest[:], span_f[:], AX.X, ALU.max))
            nc.vector.tensor_scalar(m.wide_i[:], widest[:], 3.0, None, ALU.is_ge)

            dve.wait_ge(weights_in, (6 + 3 * R) * 16)
            for r in range(R):
                mask = m.of_type[:, r, :, None].broadcast_to([P, NT, H])
                b = bias_r[:, r, None, :].broadcast_to([P, NT, H])
                link(nc.vector.tensor_tensor(bias_t[:] if r else m.bias_e[:], mask, b, ALU.mult))
                if r:
                    link(nc.vector.tensor_tensor(m.bias_e[:], m.bias_e[:], bias_t[:], ALU.add))

            bo_flat = bo_r[:].rearrange("p b f -> p (b f)")
            for k in range(3):
                link(nc.vector.tensor_copy(bo_part[:, k, :], bo_left[:] if k else bo_flat))
                if k < 2:
                    link(nc.vector.tensor_tensor(bo_left[:], bo_left[:] if k else bo_flat, bo_part[:, k, :], ALU.subtract))
            link(nc.vector.tensor_scalar(bo_sum[:], bo_part[:, 0, :], m.ident[0:3, 0:1], None, ALU.mult))
            for k in (1, 2):
                link(nc.vector.scalar_tensor_tensor(bo_sum[:], bo_part[:, k, :], m.ident[0:3, k:k + 1], bo_sum[:],
                                                    ALU.mult, ALU.add))
            nc.vector.tensor_copy(m.bo_parts[:], bo_sum[:])

            dve.wait_ge(probes_in, (NPROBE + 2) * 16)
            keys = m.key_b[:, None, :].broadcast_to([P, NEAR, NT])
            dsts = dst_b[:, None, :].broadcast_to([P, len(FAR), NT])
            nc.vector.tensor_tensor(same[:, 0:NEAR, :], shifted[:, 0:NEAR, :], keys, ALU.is_equal)
            nc.vector.tensor_tensor(same[:, NEAR:NPROBE - 1, :], shifted[:, NEAR:NPROBE - 1, :], dsts, ALU.is_equal)
            link(nc.vector.tensor_tensor(same[:, NPROBE - 1, :], shifted[:, NPROBE - 1, :], dst_b[:], ALU.is_lt))
            nc.vector.tensor_reduce(found[:], same[:], AX.X, ALU.max).then_inc(found_ok, 1)
            dve.wait_ge(found_red, 1)
            link(nc.vector.tensor_tensor(reach[:, 0:NPROBE], found_all[0:1, :], reach_of[:], ALU.mult))
            r_max, r_low, r_all, r_end = (reach[:, NPROBE + i:NPROBE + i + 1] for i in range(4))
            link(nc.vector.tensor_reduce(r_max, reach[:, 0:NPROBE], AX.X, ALU.max))
            link(nc.vector.tensor_scalar(r_low, r_max, float(EP - 1), None, ALU.min))
            link(nc.vector.tensor_scalar(r_all, r_max, float(EP), None, ALU.is_lt))
            link(nc.vector.scalar_tensor_tensor(r_end, r_max, 1.0, r_all, ALU.add, ALU.mult))
            nc.vector.tensor_scalar(m.band_i[:, 0:1], r_low, -1.0, float(EP), ALU.mult, ALU.add)
            nc.vector.scalar_tensor_tensor(m.band_i[:, 1:2], r_end, 1.0, r_low, ALU.add, ALU.add)

        @block.tensor
        def _(pe):
            pe.wait_ge(ident_ok, 1)
            pe.wait_ge(rows_ok, 1)
            small = m.ident[0:HALF, 0:HALF]
            for i, rows in enumerate((srcf_r, dstc_r, dstf_r, wgt_r, typf_r)):
                for a in range(2):
                    nc.tensor.transpose(ps_edge[i // 2][:, i % 2, a * HALF:(a + 1) * HALF], rows[:, a, :], small)
            pe.wait_ge(weights_in, (6 + 3 * R) * 16)
            nc.tensor.transpose(ps_w[:, 0, :], w0_r[:], m.ident[:])
            nc.tensor.transpose(ps_w[:, 1, :], wo_r[:], m.ident[:]).then_inc(transposed, 1)
            pe.wait_ge(ends_ok, 1)
            pe.wait_ge(consts, 8)
            for i in range(2):
                for a in range(2):
                    last = nc.tensor.matmul(ps_ends[:, i, a * HALF:(a + 1) * HALF], ones[:],
                                            ends_d[:, i, a, :], start=True, stop=True)
            last.then_inc(ends_ps, 1)
            pe.wait_ge(cols_ok, 1)
            for c in range(NCH):
                nc.tensor.matmul(ps_first[:, c * HALF:(c + 1) * HALF], first_c[:, c:c + 1], small,
                                 start=True, stop=True)
                last = nc.tensor.matmul(ps_end[:, c * HALF:(c + 1) * HALF], end_c[:, c:c + 1], small,
                                        start=True, stop=True)
            last.then_inc(cols_ps, 1)


def lead(engine, *sems):
    for s in sems:
        engine.nop().then_inc(s, LEAD)


def edge_messages(nc, m):
    with ExitStack() as ctx:
        sb, pb, sem = scoped(nc, ctx)
        rows = sb("em_rows", [P, SLOTS, F])
        xt = sb("em_xt", [P, 2, P])
        idx = sb("em_idx", [P, SLOTS], I32)
        idx_ok = sem("em_idx_ok")
        ps_t = [pb(f"em_ps_t{i}", [P, P]) for i in range(2)]
        ps_m = [pb(f"em_ps_m{i}", [P, F]) for i in range(2)]
        gathered = [sem(f"em_gathered{i}") for i in range(SLOTS)]
        xt_ready, xt_copied = sem("em_xt_ready"), sem("em_xt_copied")
        product, msg_ok = sem("em_product"), sem("em_msg_ok")
        turns = NT // TURN
        block = ctx.enter_context(nc.Block())

        @block.gpsimd
        def _(pool):
            with pool.Fori(0, turns) as i:
                for j in range(TURN):
                    t = i * TURN + j
                    pool.wait_ge(idx_ok, t + 1)
                    pool.nop(nofuse=True)
                    nc.gpsimd.indirect_dma_start(
                        rows[:, j % SLOTS, :], None, m.x,
                        bass.IndirectOffsetOnAxis(idx[:, j % SLOTS:j % SLOTS + 1], axis=0),
                    ).then_inc(gathered[j % SLOTS], 16)

        @block.tensor
        def _(pe):
            lead(pe, xt_ready, product)

            def turn_rows(i, j):
                t = i * TURN + j
                pe.wait_ge(gathered[j % SLOTS], (i * (TURN // SLOTS) + j // SLOTS) * 16 + 16)
                pe.wait_ge(xt_copied, done(t - 2))
                nc.tensor.transpose(ps_t[j % 2][:], rows[:, j % SLOTS, :], m.ident[:]).then_inc(xt_ready, 1)

            def multiply(i, j):
                t = i * TURN + j
                pe.wait_ge(xt_copied, done(t))
                pe.wait_ge(msg_ok, done(t - 2))
                nc.tensor.matmul(ps_m[j % 2][:], xt[:, j % 2, :], m.w_nb[:], start=True, stop=True).then_inc(product, 1)

            turn_rows(0, 0)
            with pe.Fori(0, turns - 1) as i:
                for j in range(TURN):
                    turn_rows(i, j + 1)
                    multiply(i, j)
            for j in range(TURN):
                if j + 1 < TURN:
                    turn_rows(turns - 1, j + 1)
                multiply(turns - 1, j)

        @block.scalar
        def _(act):
            lead(act, xt_copied)
            with act.Fori(0, turns) as i:
                for j in range(TURN):
                    t = i * TURN + j
                    act.wait_ge(xt_ready, done(t))
                    act.wait_ge(product, done(t - 2))
                    nc.scalar.copy(xt[:, j % 2, :], ps_t[j % 2][:]).then_inc(xt_copied, 1)

        @block.vector
        def _(dve):
            lead(dve, msg_ok)
            for j in range(SLOTS):
                nc.vector.tensor_copy(idx[:, j:j + 1], m.edge_i[:, j, 0:1]).then_inc(idx_ok, 1)
            with dve.Fori(0, turns) as i:
                for j in range(TURN):
                    t = i * TURN + j
                    dve.wait_ge(product, done(t))
                    nc.vector.tensor_copy(idx[:, j % SLOTS:j % SLOTS + 1],
                                          m.edge_i[:, bass.ds(t + SLOTS, 1), 0]).then_inc(idx_ok, 1)
                    nc.vector.tensor_scalar(m.msg[:, bass.ds(t, 1), :], ps_m[j % 2][:, None, :],
                                            m.wgt_f[:, bass.ds(t, 1)], None, ALU.mult).then_inc(msg_ok, 1)


def general_sums(nc, m, name):
    with ExitStack() as ctx:
        sb, pb, sem = scoped(nc, ctx)
        onehot = sb("gs_onehot" + name, [P, P])
        dst_n = sb("gs_dst" + name, [P, 2, NT + 1])
        total = sb("gs_total" + name, [P, F])
        ps = pb("gs_ps" + name, [P, F])
        with nc.Block() as block:
            @block.vector
            def _(dve):
                nc.vector.tensor_copy(dst_n[:, 1, :], m.dst_f[:])
        with nc.Fori(0, NB) as n:
            with nc.Block() as block:
                @block.vector
                def _(dve):
                    nc.vector.tensor_copy(dst_n[:, 0, :], dst_n[:, 1, :])
                    nc.vector.memset(total[:], 0.0)
            start = nc.values_load(m.first_i[0:1, bass.ds(n, 1)], min_val=0, max_val=NT - 1)
            end = nc.values_load(m.end_i[0:1, bass.ds(n, 1)], min_val=1, max_val=NT)
            with nc.Fori(start, end) as k:
                with ExitStack() as c1:
                    _, _, sem1 = scoped(nc, c1)
                    hot, summed = sem1("gs_hot" + name), sem1("gs_summed" + name)
                    with nc.Block() as block:
                        @block.vector
                        def _(dve):
                            nc.vector.tensor_scalar(onehot[:], m.local_id[:, 0:P], dst_n[:, 0, bass.ds(k, 1)],
                                                    None, ALU.is_equal).then_inc(hot, 1)
                            dve.wait_ge(summed, 1)
                            nc.vector.tensor_tensor(total[:], total[:], ps[:], ALU.add)

                        @block.tensor
                        def _(pe):
                            pe.wait_ge(hot, 1)
                            nc.tensor.matmul(ps[:], onehot[:], m.msg[:, bass.ds(k, 1), :], start=True,
                                             stop=True).then_inc(summed, 1)
            with ExitStack() as c2:
                _, _, sem2 = scoped(nc, c2)
                stored = sem2("gs_stored" + name)
                with nc.Block() as block:
                    @block.vector
                    def _(dve):
                        nc.vector.tensor_scalar(dst_n[:, 1, :], dst_n[:, 0, :], -float(P), None, ALU.add)

                    @block.sync
                    def _(sp):
                        sp.dma_start(m.sums_d[bass.ds(n * P, P), :], total[:]).then_inc(stored, 16)
                        sp.wait_ge(stored, 16)


def rows_of(a, first, count):
    return a[bass.ds(first, count * P), :].rearrange("(g p) f -> p g f", p=P)


def load_group(engine, to, a, g, landed, tail_landed):
    if isinstance(g, int) and g == GROUPS:
        engine.dma_start(to[:, 0:REST - 1, :], rows_of(a, g * GT * P, REST - 1)).then_inc(tail_landed, 16)
        engine.wait_ge(tail_landed, 16)
        engine.dma_start(to[0:LAST_ROWS, REST - 1, :], a[(NB - 1) * P:N, :]).then_inc(landed, 16)
    else:
        engine.dma_start(to, rows_of(a, g * (GT * P), GT)).then_inc(landed, 16)


def store_group(engine, a, of, g, landed, tail_landed):
    if isinstance(g, int) and g == GROUPS:
        engine.dma_start(rows_of(a, g * GT * P, REST - 1), of[:, 0:REST - 1, :]).then_inc(landed, 16)
        engine.dma_start(a[(NB - 1) * P:N, :], of[0:LAST_ROWS, REST - 1, :]).then_inc(tail_landed, 16)
    else:
        engine.dma_start(rows_of(a, g * (GT * P), GT), of).then_inc(landed, 16)




def x_slot(o):
    return (o // GB) % XSLOTS


def y_slot(o):
    return (o // GB) % 2


def loads_and_stores(sp, load, store):
    ahead = (XSLOTS - 1) * GB
    for o in range(0, ahead, GB):
        load(0, o)
    with sp.Fori(0, ROUNDS - 1) as i:
        for o in range(0, TB, GB):
            load(i, o + ahead)
            store(i, o)
    for o in range(0, TB, GB):
        if o + ahead < TB:
            load(ROUNDS - 1, o + ahead)
        elif o + ahead == TB:
            load(ROUNDS, 0)
        store(ROUNDS - 1, o)
    store(ROUNDS, 0)


def layer0_nodes(nc, m, from_sums):
    name = "n0s_" if from_sums else "n0_"
    with ExitStack() as ctx:
        sb, pb, sem = scoped(nc, ctx)
        xg = sb(name + "xg", [P, XSLOTS, GT, F])
        sg = sb(name + "sg", [P, 2, GT, F]) if from_sums else None
        yg = sb(name + "yg", [P, 2, GT, F])
        xt = sb(name + "xt", [P, 4, BT, F])
        onehot = sb(name + "onehot", [P, 2, BT, 2, P])
        dst_g = sb(name + "dst_g", [P, 2, NT + 1])
        stats = sb(name + "stats", [P, 2, BT, 6])
        mv = sb(name + "mv", [P, 2, BT, 2])
        std = sb(name + "std", [P, 2, BT])
        rstd = sb(name + "rstd", [P, 2, BT])
        shift = sb(name + "shift", [P, 2, BT])
        ps_t = [pb(f"{name}ps_t{i}", [P, BT, P]) for i in range(4)]
        ps_h = [pb(f"{name}ps_h{i}", [P, BT, F]) for i in range(4)]
        x_in = [sem(f"{name}x_in{i}") for i in range(XSLOTS)]
        s_in = [sem(f"{name}s_in{i}") for i in range(2)]
        stored = [sem(f"{name}stored{i}") for i in range(2)]
        x_tail, s_tail, y_tail = (sem(name + n) for n in ("x_tail", "s_tail", "y_tail"))
        xt_ready, xt_copied, h_ready = (sem(name + n) for n in ("xt_ready", "xt_copied", "h_ready"))
        dst_moved, hot_ready = sem(name + "dst_moved"), sem(name + "hot_ready")
        stats_ok, mv_ready, std_ready = (sem(name + n) for n in ("stats_ok", "mv_ready", "std_ready"))
        rstd_ok, shift_ready, y_ready = (sem(name + n) for n in ("rstd_ok", "shift_ready", "y_ready"))
        block = ctx.enter_context(nc.Block())

        @block.sync
        def _(sp):
            def load(i, o):
                b, g = i * TB + o, i * XSLOTS + o // GB
                sp.wait_ge(xt_ready, done(b + 1 - TB))
                load_group(sp, xg[:, x_slot(o), :, :], m.x, g, x_in[x_slot(o)], x_tail)
                if from_sums:
                    sp.wait_ge(h_ready, done(b + 1 - 2 * GB))
                    load_group(sp, sg[:, y_slot(o), :, :], m.sums_d, g, s_in[y_slot(o)], s_tail)

            def store(i, o):
                sp.wait_ge(y_ready, done(i * TB + o + 1))
                store_group(sp, m.x1_d, yg[:, y_slot(o), :, :], i * XSLOTS + o // GB, stored[y_slot(o)], y_tail)

            loads_and_stores(sp, load, store)

        @block.gpsimd
        def _(pool):
            pool.wait_ge(stored[0], LEAD + GROUPS // 2 * 16 + 16)
            pool.wait_ge(stored[1], LEAD + GROUPS // 2 * 16)
            pool.wait_ge(y_tail, 16)

        @block.tensor
        def _(pe):
            lead(pe, xt_ready, h_ready)

            def turn_x(i, o):
                b, s = i * TB + o, x_slot(o)
                pe.wait_ge(x_in[s], (i + o // TB) * 16 + 16)
                pe.wait_ge(xt_copied, done(b - 4))
                for n in range(BT):
                    last = nc.tensor.transpose(ps_t[o % 4][:, n, :], xg[:, s, (o % 2) * BT + n, :], m.ident[:])
                last.then_inc(xt_ready, 1)

            def multiply(i, o):
                b, u, s = i * TB + o, o % 2, y_slot(o)
                if not from_sums:
                    _, first = nc.values_load_multi_w_load_instructions(
                        m.first_i[0:1, bass.ds(b * BT, BT)], engines=[ENG.PE], min_val=0, max_val=NT - 1,
                        skip_runtime_bounds_check_because="the setup holds them to edge tiles")
                pe.wait_ge(xt_copied, done(b))
                pe.wait_ge(y_ready, done(b - 4))
                if from_sums:
                    pe.wait_ge(s_in[s], (i * (XSLOTS // 2) + o // GB // 2) * 16 + 16)
                else:
                    pe.wait_ge(hot_ready, done(b))
                for n in range(BT):
                    nc.tensor.matmul(ps_h[o % 4][:, n, :], xt[:, o % 4, n, :], m.w_self[:], start=True, stop=False)
                    if from_sums:
                        last = nc.tensor.matmul(ps_h[o % 4][:, n, :], m.ident[:], sg[:, s, (o % 2) * BT + n, :],
                                                start=False, stop=True)
                    else:
                        for k in range(2):
                            last = nc.tensor.matmul(ps_h[o % 4][:, n, :], onehot[:, u, n, k, :],
                                                    m.msg[:, bass.ds(first[n] + k, 1), :],
                                                    start=False, stop=(k == 1))
                last.then_inc(h_ready, 1)

            turn_x(0, 0)
            turn_x(0, 1)
            with pe.Fori(0, ROUNDS) as i:
                for o in range(TB):
                    turn_x(i, o + 2)
                    multiply(i, o)
            multiply(ROUNDS, 0)
            multiply(ROUNDS, 1)

        @block.scalar
        def _(act):
            lead(act, xt_copied, std_ready, y_ready, *stored)
            nc.scalar.preload_act_table(ACT.Sqrt)

            def copy_xt(i, o):
                b, u = i * TB + o, o % 4
                act.wait_ge(xt_ready, done(b))
                act.wait_ge(h_ready, done(b - 4))
                nc.scalar.copy(xt[:, u, :, :], ps_t[u][:]).then_inc(xt_copied, 1)

            def root(i, o):
                b, u = i * TB + o, o % 2
                act.wait_ge(mv_ready, done(b))
                nc.scalar.activation(std[:, u, :], mv[:, u, :, 1], ACT.Sqrt, bias=m.eps_c[:]).then_inc(std_ready, 1)

            def normalise(i, o):
                b, u, s = i * TB + o, o % 2, y_slot(o)
                act.wait_ge(shift_ready, done(b))
                if o % GB == 0:
                    act.wait_ge(stored[s], LEAD + (i * (XSLOTS // 2) + o // GB // 2) * 16)
                for n in range(BT):
                    last = nc.scalar.activation(yg[:, s, (o % 2) * BT + n, :], ps_h[o % 4][:, n, :], ACT.Identity,
                                                bias=shift[:, u, n:n + 1], scale=rstd[:, u, n:n + 1])
                last.then_inc(y_ready, 1)

            copy_xt(0, 0)
            copy_xt(0, 1)
            with act.Fori(0, ROUNDS) as i:
                for o in range(TB):
                    copy_xt(i, o + 2)
                    root(i, o)
                    normalise(i, o)
            root(ROUNDS, 0)
            normalise(ROUNDS, 0)
            root(ROUNDS, 1)
            normalise(ROUNDS, 1)

        @block.vector
        def _(dve):
            lead(dve, dst_moved, hot_ready, stats_ok, mv_ready, rstd_ok, shift_ready)
            hots = one_hots(nc, dve, m, dst_g, onehot, dst_moved, hot_ready, h_ready)
            moments, inverting = norm_steps(nc, dve, stats, mv, std, rstd, shift,
                                              stats_ok, mv_ready, std_ready, rstd_ok, shift_ready)

            def step(i, o, other):
                dve.wait_ge(h_ready, done(i * TB + o))
                moments(i, o, lambda n: ps_h[o % 4][:, n, :], other)
                next(other, None)
                next(other, None)
                invert = inverting(i, o)
                next(invert)
                next(other, None)
                next(invert, None)
                for _ in other:
                    pass

            none = iter(())
            if not from_sums:
                for o in range(2):
                    list(hots(0, o))
            with dve.Fori(0, ROUNDS) as i:
                for o in range(TB):
                    step(i, o, none if from_sums else hots(i, o + 2))
            step(ROUNDS, 0, none)
            step(ROUNDS, 1, none)


def one_hots(nc, dve, m, dst_g, onehot, dst_moved, hot_ready, used):
    def hots(i, o):
        b, u, s = i * TB + o, o % 2, y_slot(o)
        if isinstance(i, int) and i == 0 and o == 0:
            nc.vector.tensor_copy(dst_g[:, 0, :], m.dst_f[:]).then_inc(dst_moved, 1)
        elif o % 2 == 0:
            nc.vector.tensor_scalar(dst_g[:, s, :], dst_g[:, 1 - s, :], -float(GT * P), None,
                                    ALU.add).then_inc(dst_moved, 1)
        _, first = nc.values_load_multi_w_load_instructions(
            m.first_i[0:1, bass.ds(b * BT, BT)], engines=[ENG.DVE], min_val=0, max_val=NT - 1,
            skip_runtime_bounds_check_because="the setup holds them to edge tiles")
        dve.wait_ge(dst_moved, done(i * XSLOTS + o // GB))
        dve.wait_ge(used, done(b - 2))
        for n in range(BT):
            node = ((o % 2) * BT + n) * P
            last = nc.vector.tensor_tensor(
                onehot[:, u, n, :, :], m.local_id[:, None, node:node + P].broadcast_to([P, 2, P]),
                dst_g[:, s, bass.ds(first[n], 2)][:, :, None].broadcast_to([P, 2, P]), ALU.is_equal)
            if n == BT - 1:
                last.then_inc(hot_ready, 1)
            yield
    return hots


def norm_steps(nc, dve, stats, mv, std, rstd, shift, stats_ok, mv_ready, std_ready, rstd_ok, shift_ready):
    def moments(i, o, tile, other):
        b, u = i * TB + o, o % 2
        for n in range(BT):
            last = nc.vector.bn_stats(stats[:, u, n, :], tile(n))
        last.then_inc(stats_ok, 1)
        next(other, None)
        dve.wait_ge(stats_ok, done(b))
        dve.nop(nofuse=True)
        for n in range(BT):
            last = nc.vector.bn_aggr(mv[:, u, n, :], stats[:, u, n, :])
        last.then_inc(mv_ready, 1)

    def inverting(i, o):
        b, u = i * TB + o, o % 2
        dve.wait_ge(std_ready, done(b))
        nc.vector.reciprocal(rstd[:, u, :], std[:, u, :]).then_inc(rstd_ok, 1)
        yield
        dve.wait_ge(rstd_ok, done(b))
        nc.vector.scalar_tensor_tensor(shift[:, u, :], mv[:, u, :, 0], -1.0, rstd[:, u, :],
                                       ALU.mult, ALU.mult).then_inc(shift_ready, 1)
    return moments, inverting


def project_edges(nc, m):
    with ExitStack() as ctx:
        sb, pb, sem = scoped(nc, ctx)
        rows = sb("pe_rows", [P, SLOTS, 2, F])
        idx = sb("pe_idx", [P, SLOTS, 2], I32)
        typ_b = sb("pe_typ_b", [P, TURN, P])
        xt = sb("pe_xt", [P, 2, R, 2, P])
        q = sb("pe_q", [P, 2, F])
        qk = sb("pe_qk", [P, 2, H, HD])
        dot = sb("pe_dot", [P, 2, H])
        ps_t = [pb(f"pe_ps_t{i}", [P, 2, P]) for i in range(2)]
        ps_qkv = [pb(f"pe_ps_qkv{i}", [P, 3, F]) for i in range(2)]
        src_in = [sem(f"pe_src_in{i}") for i in range(SLOTS)]
        dst_in = [sem(f"pe_dst_in{i}") for i in range(SLOTS)]
        typ_in = [sem(f"pe_typ_in{i}") for i in range(2)]
        idx_ok, xt_ready, masked = sem("pe_idx_ok"), sem("pe_xt_ready"), sem("pe_masked")
        projected, v_out = sem("pe_projected"), sem("pe_v_out")
        qk_ok, dot_ok, logit_ok = sem("pe_qk_ok"), sem("pe_dot_ok"), sem("pe_logit_ok")
        turns = NT // TURN
        half = TURN // 2
        block = ctx.enter_context(nc.Block())

        @block.sync
        def _(sp):
            with sp.Fori(0, turns) as i:
                for h in range(2):
                    sp.wait_ge(masked, done(i * TURN + (h + 1) * half - 1 - TURN))
                    sp.dma_start(typ_b[:, h * half:(h + 1) * half, :].rearrange("p t e -> p (t e)"),
                                 m.typ_d[bass.ds((i * TURN + h * half) * P, half * P)].partition_broadcast(P)
                                 ).then_inc(typ_in[h], 16)

        @block.gpsimd
        def _(pool):
            with pool.Fori(0, turns) as i:
                for j in range(TURN):
                    t, s = i * TURN + j, j % SLOTS
                    pool.wait_ge(idx_ok, t + 1)
                    pool.nop(nofuse=True)
                    nc.gpsimd.indirect_dma_start(
                        rows[:, s, 0, :], None, m.x1_d,
                        bass.IndirectOffsetOnAxis(idx[:, s, 0:1], axis=0)).then_inc(src_in[s], 16)
                    nc.gpsimd.indirect_dma_start(
                        rows[:, s, 1, :], None, m.x1_d,
                        bass.IndirectOffsetOnAxis(idx[:, s, 1:2], axis=0)).then_inc(dst_in[s], 16)

        @block.tensor
        def _(pe):
            lead(pe, xt_ready, projected)

            def turn_rows(i, j):
                t, s = i * TURN + j, j % SLOTS
                landed = (i * (TURN // SLOTS) + j // SLOTS) * 16 + 16
                pe.wait_ge(src_in[s], landed)
                pe.wait_ge(dst_in[s], landed)
                pe.wait_ge(masked, done(t - 2))
                nc.tensor.transpose(ps_t[j % 2][:, 0, :], rows[:, s, 0, :], m.ident[:])
                nc.tensor.transpose(ps_t[j % 2][:, 1, :], rows[:, s, 1, :], m.ident[:]).then_inc(xt_ready, 1)

            def project(i, j):
                t, u = i * TURN + j, j % 2
                pe.wait_ge(masked, done(t))
                pe.wait_ge(qk_ok, done(t - 2))
                for r in range(R):
                    nc.tensor.matmul(ps_qkv[u][:, 0, :], xt[:, u, r, 1, :], m.w_qkv[:, r, 0, :],
                                     start=(r == 0), stop=(r == R - 1))
                for r in range(R):
                    last = nc.tensor.matmul(ps_qkv[u][:, 1:3, :], xt[:, u, r, 0, :], m.w_qkv[:, r, 1:3, :],
                                            start=(r == 0), stop=(r == R - 1))
                last.then_inc(projected, 1)

            turn_rows(0, 0)
            turn_rows(0, 1)
            with pe.Fori(0, turns - 1) as i:
                for j in range(TURN):
                    turn_rows(i, j + 2)
                    project(i, j)
            for j in range(TURN):
                if j + 2 < TURN:
                    turn_rows(turns - 1, j + 2)
                project(turns - 1, j)

        @block.scalar
        def _(act):
            lead(act, v_out)
            with act.Fori(0, turns) as i:
                for j in range(TURN):
                    t = i * TURN + j
                    act.wait_ge(projected, done(t))
                    act.wait_ge(qk_ok, done(t - 2))
                    nc.scalar.copy(q[:, j % 2, :], ps_qkv[j % 2][:, 0, :])
                    nc.scalar.copy(m.msg[:, bass.ds(t, 1), :], ps_qkv[j % 2][:, 2:3, :]).then_inc(v_out, 1)

        @block.vector
        def _(dve):
            lead(dve, masked, qk_ok, dot_ok, logit_ok)
            for j in range(SLOTS):
                nc.vector.tensor_copy(idx[:, j, :], m.edge_i[:, j, :]).then_inc(idx_ok, 1)

            def mask(i, j, r):
                t, s, u = i * TURN + j, j % SLOTS, j % 2
                if r == 0:
                    dve.wait_ge(xt_ready, done(t))
                    nc.vector.tensor_copy(idx[:, s, :].rearrange("p (o e) -> p o e", o=1),
                                          m.edge_i[:, bass.ds(t + SLOTS, 1), :]).then_inc(idx_ok, 1)
                    if j % half == 0:
                        dve.wait_ge(typ_in[(j // half) % 2], (i + j // TURN) * 16 + 16)
                    dve.wait_ge(projected, done(t - 2))
                last = nc.vector.scalar_tensor_tensor(
                    xt[:, u, r, :, :], typ_b[:, j % TURN, None, :].broadcast_to([P, 2, P]), float(r), ps_t[u][:],
                    ALU.is_equal, ALU.mult)
                if r == R - 1:
                    last.then_inc(masked, 1)

            def dots(i, j):
                t, u = i * TURN + j, j % 2
                dve.wait_ge(v_out, done(t))
                nc.vector.tensor_tensor(qk[:, u, :, :].rearrange("p h d -> p (h d)"), q[:, u, :],
                                        ps_qkv[u][:, 1, :], ALU.mult).then_inc(qk_ok, 1)
                yield
                dve.wait_ge(qk_ok, done(t))
                nc.vector.tensor_reduce(dot[:, u, :], qk[:, u, :, :], AX.X, ALU.add).then_inc(dot_ok, 1)
                yield
                dve.wait_ge(dot_ok, done(t))
                nc.vector.scalar_tensor_tensor(m.logit[:, bass.ds(t, 1), :], dot[:, u:u + 1, :], 1.0 / SCALE,
                                               m.bias_e[:, bass.ds(t, 1), :], ALU.mult, ALU.add).then_inc(logit_ok, 1)
                yield

            def step(i, j):
                of_t = dots(i, j)
                for r in range(R):
                    mask(i, j + 2, r)
                    if r >= 2:
                        next(of_t)

            for j in range(2):
                for r in range(R):
                    mask(0, j, r)
            with dve.Fori(0, turns - 1) as i:
                for j in range(TURN):
                    step(i, j)
            for j in range(TURN):
                if j + 2 < TURN:
                    step(turns - 1, j)
                else:
                    list(dots(turns - 1, j))


def segment_softmax(nc, m):
    with ExitStack() as ctx:
        sb, pb, sem = scoped(nc, ctx)
        by_row = sb("ss_by_row", [HALF, 2, H, P])
        own = sb("ss_own", [P, H, NT])
        other = sb("ss_other", [P, 2, H, NT])
        other_key = sb("ss_other_key", [P, 2, NT])
        same = sb("ss_same", [P, 2, NT])
        part = sb("ss_part", [P, H, NT])
        top = sb("ss_top", [P, H, NT])
        total = sb("ss_total", [P, H, NT])
        ps = [pb(f"ss_ps{i}", [HALF, 4, P]) for i in range(4)]
        ps_b = [pb(f"ss_ps_b{i}", [P, 4, HALF]) for i in range(4)]
        band = nc.values_load_multi_w_load_instructions(
            m.band_i[0:1, 0:2], engines=[ENG.Activation, ENG.DVE], min_val=0, max_val=EP,
            skip_runtime_bounds_check_because="the setup holds them within the copies")[1]

        def circle(engine, a, copies_done):
            def store(of, copies):
                for c in range(copies):
                    engine.dma_start(a[:, c * EP:(c + 1) * EP].rearrange("h (p t) -> p h t", t=NT),
                                     of).then_inc(copies_done, 16)
            return store

        def shifted_pass(name, a, step):
            with ExitStack() as inner:
                _, _, sem2 = scoped(nc, inner)
                landed = [sem2(f"{name}_landed{u}") for u in range(2)]
                used, turned = sem2(name + "_used"), sem2(name + "_turned")
                inner_block = inner.enter_context(nc.Block())

                @inner_block.scalar
                def _(act):
                    with act.Fori(0, band[1], 2) as n:
                        for u in range(2):
                            act.wait_ge(used, n + u + 1)
                            act.dma_start(other[:, u, :, :], a[:, bass.ds(band[0] + n + u, EP)].rearrange(
                                "h (p t) -> p h t", t=NT)).then_inc(landed[u], 16)
                            act.dma_start(other_key[:, u, :], m.key_d[bass.ds(band[0] + n + u, EP)].rearrange(
                                "(p t) -> p t", t=NT)).then_inc(landed[u], 16)

                @inner_block.vector
                def _(dve):
                    dve.nop().then_inc(used, 2)
                    with dve.Fori(0, band[1], 2) as n:
                        for u in range(2):
                            dve.wait_ge(landed[u], n * 16 + 32)
                            step(dve, u, n + u, turned, used)

        with ExitStack() as inner:
            _, _, sem1 = scoped(nc, inner)
            turned, copied, stored, loaded = (sem1("ss_" + n) for n in ("turned", "copied", "stored", "loaded"))
            block = inner.enter_context(nc.Block())

            @block.tensor
            def _(pe):
                for a in range(2):
                    for h in range(H):
                        last = nc.tensor.transpose(ps[a * 2 + h // 4][:, h % 4, :],
                                                   m.logit[:, a * HALF:(a + 1) * HALF, h], m.ident[:])
                        if h % 4 == 3:
                            last.then_inc(turned, 1)

            @block.vector
            def _(dve):
                for i in range(4):
                    dve.wait_ge(turned, i + 1)
                    nc.vector.tensor_copy(by_row[:, i // 2, (i % 2) * 4:(i % 2) * 4 + 4, :], ps[i][:]).then_inc(copied, 1)
                nc.vector.memset(top[:], NEG)
                nc.vector.memset(total[:], 0.0)

            @block.sync
            def _(sp):
                for a in range(2):
                    sp.wait_ge(copied, 2 * a + 2)
                    for c in range(3):
                        at = c * EP + a * HALF * P
                        sp.dma_start(m.logit_d[:, at:at + HALF * P].rearrange("h (t e) -> t h e", e=P),
                                     by_row[:, a, :, :]).then_inc(stored, 16)
                sp.wait_ge(stored, 6 * 16)
                sp.dma_start(own[:], m.logit_d[:, 0:EP].rearrange("h (p t) -> p h t", t=NT)).then_inc(loaded, 16)
                sp.wait_ge(loaded, 16)

        def highest(dve, u, n, turned, used):
            nc.vector.tensor_tensor(same[:, u, :], other_key[:, u, :], m.key_b[:], ALU.is_equal).then_inc(turned, 1)
            dve.wait_ge(turned, n * 3 + 1)
            nc.vector.tensor_scalar(same[:, u, :], same[:, u, :], 1.0, MASK, ALU.subtract, ALU.mult).then_inc(turned, 1)
            dve.wait_ge(turned, n * 3 + 2)
            nc.vector.tensor_tensor(part[:], other[:, u, :, :], same[:, u, None, :].broadcast_to([P, H, NT]),
                                    ALU.add).then_inc(turned, 1)
            dve.wait_ge(turned, n * 3 + 3)
            nc.vector.tensor_tensor(top[:], top[:], part[:], ALU.max).then_inc(used, 1)
            dve.wait_ge(used, n + 3)

        def add_up(dve, u, n, turned, used):
            nc.vector.tensor_tensor(same[:, u, :], other_key[:, u, :], m.key_b[:], ALU.is_equal).then_inc(turned, 1)
            dve.wait_ge(turned, n * 2 + 1)
            nc.vector.tensor_tensor(part[:], other[:, u, :, :], same[:, u, None, :].broadcast_to([P, H, NT]),
                                    ALU.mult).then_inc(turned, 1)
            dve.wait_ge(turned, n * 2 + 2)
            nc.vector.tensor_tensor(total[:], total[:], part[:], ALU.add).then_inc(used, 1)
            dve.wait_ge(used, n + 3)

        shifted_pass("ss_max", m.logit_d, highest)

        with ExitStack() as inner:
            _, _, sem1 = scoped(nc, inner)
            less, raised, stored = (sem1("ss_" + n) for n in ("less", "raised", "stored2"))
            block = inner.enter_context(nc.Block())

            @block.vector
            def _(dve):
                nc.vector.tensor_tensor(part[:], own[:], top[:], ALU.subtract).then_inc(less, 1)

            @block.scalar
            def _(act):
                act.wait_ge(less, 1)
                nc.scalar.activation(own[:], part[:], ACT.Exp).then_inc(raised, 1)

            @block.sync
            def _(sp):
                sp.wait_ge(raised, 1)
                circle(sp, m.prob_d, stored)(own[:], 3)
                sp.wait_ge(stored, 3 * 16)

        shifted_pass("ss_sum", m.prob_d, add_up)

        with ExitStack() as inner:
            _, _, sem1 = scoped(nc, inner)
            chain, stored, loaded, turned = (sem1("ss_" + n) for n in ("chain3", "stored3", "loaded3", "turned3"))
            block = inner.enter_context(nc.Block())

            @block.vector
            def _(dve):
                nc.vector.tensor_scalar(total[:], total[:], 1e-12, None, ALU.add).then_inc(chain, 1)
                dve.wait_ge(chain, 1)
                nc.vector.reciprocal(part[:], total[:]).then_inc(chain, 1)
                dve.wait_ge(chain, 2)
                nc.vector.tensor_tensor(own[:], own[:], part[:], ALU.mult).then_inc(chain, 1)
                for i in range(4):
                    dve.wait_ge(turned, i + 1)
                    a, h = i // 2, (i % 2) * 4
                    nc.vector.tensor_copy(m.logit[:, a * HALF:(a + 1) * HALF, h:h + 4].rearrange("p t h -> p h t"),
                                          ps_b[i][:])

            @block.sync
            def _(sp):
                sp.wait_ge(chain, 3)
                sp.dma_start(m.attn_d.rearrange("h (p t) -> p h t", t=NT), own[:]).then_inc(stored, 16)
                sp.wait_ge(stored, 16)
                for a in range(2):
                    sp.dma_start(by_row[:, a, :, :], m.attn_d[:, a * HALF * P:(a + 1) * HALF * P].rearrange(
                        "h (t e) -> t h e", e=P)).then_inc(loaded, 16)

            @block.tensor
            def _(pe):
                pe.wait_ge(loaded, 32)
                for i in range(4):
                    for h in range(4):
                        last = nc.tensor.transpose(ps_b[i][:, h, :], by_row[:, i // 2, (i % 2) * 4 + h, :],
                                                   m.ident[0:HALF, 0:HALF])
                    last.then_inc(turned, 1)


def attended_messages(nc, m):
    with ExitStack() as ctx:
        sb, pb, sem = scoped(nc, ctx)
        av = sb("am_av", [P, 2, H, HD])
        avt = sb("am_avt", [P, 2, P])
        ps_t = [pb(f"am_ps_t{i}", [P, P]) for i in range(2)]
        ps_m = [pb(f"am_ps_m{i}", [P, F]) for i in range(2)]
        av_ready, avt_ready, avt_copied = sem("am_av_ready"), sem("am_avt_ready"), sem("am_avt_copied")
        product, msg_ok = sem("am_product"), sem("am_msg_ok")
        turns = NT // STEPS
        block = ctx.enter_context(nc.Block())

        @block.vector
        def _(dve):
            lead(dve, av_ready)
            with dve.Fori(0, turns) as i:
                for j in range(STEPS):
                    t, u = i * STEPS + j, j % 2
                    dve.wait_ge(avt_ready, done(t - 2))
                    nc.vector.tensor_tensor(
                        av[:, u, :, :], m.msg[:, bass.ds(t, 1), :].rearrange("p o (h d) -> p (o h) d", h=H),
                        m.logit[:, bass.ds(t, 1), :].rearrange("p o h -> p (o h)")[:, :, None].broadcast_to([P, H, HD]),
                        ALU.mult).then_inc(av_ready, 1)

        @block.tensor
        def _(pe):
            lead(pe, avt_ready, product)

            def turn(i, j):
                t = i * STEPS + j
                pe.wait_ge(av_ready, done(t))
                pe.wait_ge(avt_copied, done(t - 2))
                nc.tensor.transpose(ps_t[j % 2][:], av[:, j % 2, :, :].rearrange("p h d -> p (h d)"),
                                    m.ident[:]).then_inc(avt_ready, 1)

            def multiply(i, j):
                t = i * STEPS + j
                pe.wait_ge(avt_copied, done(t))
                pe.wait_ge(msg_ok, done(t - 2))
                nc.tensor.matmul(ps_m[j % 2][:], avt[:, j % 2, :], m.w_out[:], start=True, stop=True).then_inc(product, 1)

            turn(0, 0)
            with pe.Fori(0, turns - 1) as i:
                for j in range(STEPS):
                    turn(i, j + 1)
                    multiply(i, j)
            for j in range(STEPS):
                if j + 1 < STEPS:
                    turn(turns - 1, j + 1)
                multiply(turns - 1, j)

        @block.scalar
        def _(act):
            lead(act, avt_copied, msg_ok)

            def copy_avt(i, j):
                t, u = i * STEPS + j, j % 2
                act.wait_ge(avt_ready, done(t))
                act.wait_ge(product, done(t - 2))
                nc.scalar.copy(avt[:, u, :], ps_t[u][:]).then_inc(avt_copied, 1)

            def copy_msg(i, j):
                t = i * STEPS + j
                act.wait_ge(product, done(t))
                nc.scalar.copy(m.msg[:, bass.ds(t, 1), :], ps_m[j % 2][:, None, :]).then_inc(msg_ok, 1)

            copy_avt(0, 0)
            with act.Fori(0, turns - 1) as i:
                for j in range(STEPS):
                    copy_avt(i, j + 1)
                    copy_msg(i, j)
            for j in range(STEPS):
                if j + 1 < STEPS:
                    copy_avt(turns - 1, j + 1)
                copy_msg(turns - 1, j)


def layer1_nodes(nc, m, from_sums):
    name = "n1s_" if from_sums else "n1_"
    with ExitStack() as ctx:
        sb, pb, sem = scoped(nc, ctx)
        xg = sb(name + "xg", [P, XSLOTS, GT, F])
        sg = sb(name + "sg", [P, 2, GT, F]) if from_sums else None
        yg = sb(name + "yg", [P, 2, GT, F])
        xbeta = sb(name + "xbeta", [P, 2, BT, F])
        norm = sb(name + "norm", [P, 2, BT, F])
        scaled = sb(name + "scaled", [P, 2, BT, F])
        z = sb(name + "z", [P, 2, BT, F])
        onehot = sb(name + "onehot", [P, 2, BT, 2, P])
        dst_g = sb(name + "dst_g", [P, 2, NT + 1])
        ps_h = [pb(f"{name}ps_h{i}", [P, BT, F]) for i in range(4)]
        x_in = [sem(f"{name}x_in{i}") for i in range(XSLOTS)]
        s_in = [sem(f"{name}s_in{i}") for i in range(2)]
        stored = [sem(f"{name}stored{i}") for i in range(2)]
        x_tail, s_tail, y_tail = (sem(name + n) for n in ("x_tail", "s_tail", "y_tail"))
        h_ready, dst_moved, hot_ready = (sem(name + n) for n in ("h_ready", "dst_moved", "hot_ready"))
        norm_ready, y_ready = sem(name + "norm_ready"), sem(name + "y_ready")
        xbeta_ready, scaled_ready, z_ready = (sem(name + n) for n in ("xbeta_ready", "scaled_ready", "z_ready"))
        buf, ev = [], []
        for k in range(2):
            buf.append([sb(f"{name}{n}{k}", [P, 2, BT, *w]) for n, w in (
                ("stats", [6]), ("mv", [2]), ("std", []), ("rstd", []), ("shift", []))])
            ev.append([sem(f"{name}{n}{k}") for n in ("stats_ok", "mv_ready", "std_ready", "rstd_ok", "shift_ready")])
        block = ctx.enter_context(nc.Block())

        @block.sync
        def _(sp):
            def load(i, o):
                b, g = i * TB + o, i * XSLOTS + o // GB
                sp.wait_ge(h_ready, done(b + 1 - TB))
                sp.wait_ge(xbeta_ready, done(b + 1 - TB))
                load_group(sp, xg[:, x_slot(o), :, :], m.x1_d, g, x_in[x_slot(o)], x_tail)
                if from_sums:
                    sp.wait_ge(h_ready, done(b + 1 - 2 * GB))
                    load_group(sp, sg[:, y_slot(o), :, :], m.sums_d, g, s_in[y_slot(o)], s_tail)

            def store(i, o):
                sp.wait_ge(y_ready, done(i * TB + o + 1))
                store_group(sp, m.out, yg[:, y_slot(o), :, :], i * XSLOTS + o // GB, stored[y_slot(o)], y_tail)

            loads_and_stores(sp, load, store)
            sp.wait_ge(stored[0], LEAD + GROUPS // 2 * 16 + 16)
            sp.wait_ge(stored[1], LEAD + GROUPS // 2 * 16)
            sp.wait_ge(y_tail, 16)

        def x_landed(engine, i, o):
            engine.wait_ge(x_in[x_slot(o)], (i + o // TB) * 16 + 16)

        @block.tensor
        def _(pe):
            lead(pe, h_ready)

            def multiply(i, o):
                b, u, s, half = i * TB + o, o % 2, x_slot(o), (o % 2) * BT
                if not from_sums:
                    _, first = nc.values_load_multi_w_load_instructions(
                        m.first_i[0:1, bass.ds(b * BT, BT)], engines=[ENG.PE], min_val=0, max_val=NT - 1,
                        skip_runtime_bounds_check_because="the setup holds them to edge tiles")
                x_landed(pe, i, o)
                pe.wait_ge(norm_ready, done(b - 4))
                if from_sums:
                    pe.wait_ge(s_in[y_slot(o)], (i * (XSLOTS // 2) + o // GB // 2) * 16 + 16)
                else:
                    pe.wait_ge(hot_ready, done(b))
                nc.tensor.matmul(ps_h[o % 4][:].rearrange("p b f -> p (b f)"), m.ones_3[:], m.bo_parts[:],
                                 start=True, stop=False)
                for n in range(BT):
                    nc.tensor.matmul(ps_h[o % 4][:, n, :], m.ident[:], xg[:, s, half + n, :], start=False, stop=False)
                    if from_sums:
                        last = nc.tensor.matmul(ps_h[o % 4][:, n, :], m.ident[:], sg[:, y_slot(o), half + n, :],
                                                start=False, stop=(n == BT - 1))
                    else:
                        for k in range(2):
                            last = nc.tensor.matmul(ps_h[o % 4][:, n, :], onehot[:, u, n, k, :],
                                                    m.msg[:, bass.ds(first[n] + k, 1), :],
                                                    start=False, stop=(k == 1 and n == BT - 1))
                last.then_inc(h_ready, 1)

            with pe.Fori(0, ROUNDS) as i:
                for o in range(TB):
                    multiply(i, o)
            multiply(ROUNDS, 0)
            multiply(ROUNDS, 1)

        @block.scalar
        def _(act):
            lead(act, norm_ready, y_ready, ev[0][2], ev[1][2], *stored)
            nc.scalar.preload_act_table(ACT.Sqrt)

            def root(k, i, o):
                b, u = i * TB + o, o % 2
                _, mv, std, _, _ = buf[k]
                act.wait_ge(ev[k][1], done(b))
                nc.scalar.activation(std[:, u, :], mv[:, u, :, 1], ACT.Sqrt, bias=m.eps_c[:]).then_inc(ev[k][2], 1)

            def normalise(k, to, of, i, o, ready):
                u = o % 2
                _, _, _, rstd, shift = buf[k]
                act.wait_ge(ev[k][4], done(i * TB + o))
                for n in range(BT):
                    last = nc.scalar.activation(to(n), of(n), ACT.Identity, bias=shift[:, u, n:n + 1],
                                                scale=rstd[:, u, n:n + 1])
                last.then_inc(ready, 1)

            def first_norm(i, o):
                act.wait_ge(scaled_ready, done(i * TB + o - 2))
                normalise(0, lambda n: norm[:, o % 2, n, :], lambda n: ps_h[o % 4][:, n, :], i, o, norm_ready)

            def second_norm(i, o):
                s = y_slot(o)
                if o % GB == 0:
                    act.wait_ge(stored[s], LEAD + (i * (XSLOTS // 2) + o // GB // 2) * 16)
                normalise(1, lambda n: yg[:, s, (o % 2) * BT + n, :], lambda n: z[:, o % 2, n, :], i, o, y_ready)

            for o in range(2):
                root(0, 0, o)
                first_norm(0, o)
            with act.Fori(0, ROUNDS) as i:
                for o in range(TB):
                    root(0, i, o + 2)
                    root(1, i, o)
                    first_norm(i, o + 2)
                    second_norm(i, o)
            for o in range(2):
                root(1, ROUNDS, o)
                second_norm(ROUNDS, o)

        @block.gpsimd
        def _(pool):
            lead(pool, xbeta_ready, scaled_ready, z_ready)
            beta4 = m.bet_b[:, None, :].broadcast_to([P, BT, F])
            gamma4 = m.gam_b[:, None, :].broadcast_to([P, BT, F])

            def add_beta(i, o):
                b, u, s, half = i * TB + o, o % 2, x_slot(o), (o % 2) * BT
                x_landed(pool, i, o)
                pool.wait_ge(z_ready, done(b - 2))
                nc.gpsimd.tensor_tensor(xbeta[:, u, :, :], xg[:, s, half:half + BT, :], beta4, ALU.add).then_inc(xbeta_ready, 1)

            def scale(i, o):
                b, u = i * TB + o, o % 2
                pool.wait_ge(norm_ready, done(b))
                pool.wait_ge(z_ready, done(b - 2))
                nc.gpsimd.tensor_tensor(scaled[:, u, :, :], norm[:, u, :, :], gamma4, ALU.mult).then_inc(scaled_ready, 1)

            def add(i, o):
                b, u = i * TB + o, o % 2
                pool.wait_ge(scaled_ready, done(b))
                pool.wait_ge(xbeta_ready, done(b))
                pool.wait_ge(y_ready, done(b - 2))
                nc.gpsimd.tensor_tensor(z[:, u, :, :], scaled[:, u, :, :], xbeta[:, u, :, :], ALU.add).then_inc(z_ready, 1)

            add_beta(0, 0)
            with pool.Fori(0, ROUNDS) as i:
                for o in range(TB):
                    scale(i, o)
                    add_beta(i, o + 1)
                    add(i, o)
            scale(ROUNDS, 0)
            add_beta(ROUNDS, 1)
            add(ROUNDS, 0)
            scale(ROUNDS, 1)
            add(ROUNDS, 1)

        @block.vector
        def _(dve):
            lead(dve, dst_moved, hot_ready, *(e for k in range(2) for e in (ev[k][0], ev[k][1], ev[k][3], ev[k][4])))
            hots = one_hots(nc, dve, m, dst_g, onehot, dst_moved, hot_ready, h_ready)
            moments, inverting = zip(*(norm_steps(nc, dve, *buf[k], *ev[k]) for k in range(2)))

            def first_moments(i, o, other):
                dve.wait_ge(h_ready, done(i * TB + o))
                moments[0](i, o, lambda n: ps_h[o % 4][:, n, :], other)

            def second_moments(i, o, other):
                dve.wait_ge(z_ready, done(i * TB + o))
                moments[1](i, o, lambda n: z[:, o % 2, n, :], other)

            none = iter(())

            def first_half(i, o):
                first_moments(i, o, none)
                list(inverting[0](i, o))

            def second_half(i, o):
                second_moments(i, o, none)
                list(inverting[1](i, o))

            def step(i, o, other):
                invert_0, invert_1 = inverting[0](i, o + 2), inverting[1](i, o)
                first_moments(i, o + 2, other)
                second_moments(i, o, invert_0)
                next(invert_0, None)
                next(other, None)
                next(other, None)
                next(invert_1)
                next(other, None)
                next(invert_1, None)

            for o in range(4):
                if not from_sums:
                    list(hots(0, o))
                if o % 2:
                    first_half(0, o // 2)
            with dve.Fori(0, ROUNDS) as i:
                for o in range(TB):
                    step(i, o, none if from_sums else hots(i, o + 4))
            second_half(ROUNDS, 0)
            second_half(ROUNDS, 1)


_INS = ["x", "src", "dst", "edge_type_5", "edge_weight", "L0_gnn_W", "L1_gnn_W_Q", "L1_gnn_W_K", "L1_gnn_W_V",
        "L1_gnn_attn_bias", "L1_gnn_out_proj_w", "L1_gnn_out_proj_b", "L1_gnn_ln_gamma", "L1_gnn_ln_beta"]


def kernel(**inputs):
    import numpy as _np
    import concourse.bacc as _bacc
    from concourse.bass_utils import run_bass_kernel_spmd as _run

    nc = _bacc.Bacc("TRN2", target_bir_lowering=False, num_devices=1)
    arrays, args = {}, []
    for name in _INS:
        a = _np.ascontiguousarray(inputs[name])
        arrays[f"in_{name}"] = a
        args.append(nc.dram_tensor(f"in_{name}", a.shape, mybir.dt.from_np(a.dtype), kind="ExternalInput").ap())
    args.append(nc.dram_tensor("out_x", (N, F), F32, kind="ExternalOutput").ap())
    gnn(nc, *args)
    r = _run(nc, [arrays], core_ids=[0])
    return r.results[0]["out_x"]
```

```python
import concourse.bass as bass
from concourse import mybir
from contextlib import ExitStack

F32 = mybir.dt.float32
I32 = mybir.dt.int32
BF16 = mybir.dt.bfloat16
ALU = mybir.AluOpType
ACT = mybir.ActivationFunctionType
AX = mybir.AxisListType
ENG = mybir.EngineType

P = 128
N, F = 50000, 128
E, R, H, HD = 25000, 5, 8, 16
NT = (E + P - 1) // P
EP = NT * P
HALF = NT // 2
TAIL = E - (NT - 1) * P
NB = (N + P - 1) // P
LAST_ROWS = N - (NB - 1) * P
BT = 4
BATCHES = (NB + BT - 1) // BT
GB = 2
GT = BT * GB
GROUPS = NB // GT
XSLOTS = 4
TB = XSLOTS * GB
ROUNDS = GROUPS // XSLOTS
REST = NB - GROUPS * GT
NCH = 4
W = F + 2
AHEAD = 4
RING = 4
STORED = RING + 1
QUADS = ROUNDS * RING + STORED
GATHERS = 4 * QUADS
WSLOTS = 8
MOST_AHEAD = (2 * AHEAD - 1) * P - (BT - 1) * P // 2
PAD_DST = 1 << 17
NO_DST = 1.0e6
EPS = 1e-5
NEG = -1.0e9
MASK = 1.0e30
SCALE = float(HD) ** 0.5
LEAD = 12
SLOTS = 7
TURN = 14
EC = EP + 1
SHIFTS = 4
FAR = [(8, 63), (64, 511), (512, 4095), (4096, EP)]
NEAR = 7
NPROBE = NEAR + len(FAR) + 1


assert LEAD > max(2 * SHIFTS, TB - 2, WSLOTS - 1, TURN // 2)


def done(step):
    return LEAD + 1 + step


class Memory:
    pass


def scoped(nc, ctx):
    sems = []

    def clear():
        if sems:
            nc.clear_and_free_semaphores(sems)
            nc.all_engine_barrier(sem_only=True)

    ctx.callback(clear)

    def sb(name, shape, dt=F32):
        return ctx.enter_context(nc.sbuf_tensor(name, shape, dt))

    def pb(name, shape):
        return ctx.enter_context(nc.psum_tensor(name, shape, F32))

    def sem(name):
        sems.append(nc.alloc_semaphore(name))
        return sems[-1]

    return sb, pb, sem


def gnn(nc, x, src, dst, typ, wgt, w0, wq, wk, wv, bias, wo, bo, gamma, beta, out):
    m = Memory()
    m.x, m.src, m.dst, m.typ, m.wgt, m.out = x, src, dst, typ, wgt, out
    m.w0, m.wq, m.wk, m.wv, m.wo = w0, wq, wk, wv, wo
    m.bias, m.bo, m.gamma, m.beta = bias, bo, gamma, beta
    m.x1_d = nc.dram_tensor("x1_d", [N, F], F32).ap()
    m.rows_d = nc.dram_tensor("rows_d", [GATHERS * P, W], F32).ap()
    m.att_d = nc.dram_tensor("att_d", [(NT + 1) * P, W], F32).ap()
    m.sums_d = nc.dram_tensor("sums_d", [NB * P, F], F32).ap()
    m.key_d = nc.dram_tensor("key_d", [3 * EC], F32).ap()
    m.typ_d = nc.dram_tensor("typ_d", [EP], F32).ap()
    m.dst_d = nc.dram_tensor("dst_d", [EP + FAR[-1][0]], F32).ap()
    m.logit_d = nc.dram_tensor("logit_d", [H, 3 * EC], F32).ap()
    m.prob_d = nc.dram_tensor("prob_d", [H, 3 * EC], F32).ap()
    m.attn_d = nc.dram_tensor("attn_d", [H, EP], F32).ap()

    with ExitStack() as ctx:
        sb, _, _ = scoped(nc, ctx)
        m.msg = sb("msg", [P, NT + 1, W])
        m.ident = sb("ident", [P, P])
        m.local_id = sb("local_id", [P, BT * P])
        m.batch_0 = sb("batch_0", [P, BATCHES])
        m.edge_i = sb("edge_i", [P, GATHERS, 2], I32)
        m.edge_f = sb("edge_f", [P, GATHERS, 2])
        m.key_b = sb("key_b", [P, NT])
        m.of_type = sb("of_type", [P, NT, R])
        m.bias_r = sb("bias_r", [P, R, H])
        m.w_nb = sb("w_nb", [P, F])
        m.w_out = sb("w_out", [P, F])
        m.w_qkv = sb("w_qkv", [P, R, 3, F])
        m.gam_b = sb("gam_b", [P, F])
        m.bet_b = sb("bet_b", [P, F])
        m.bo_parts = sb("bo_parts", [3, BT * F], BF16)
        m.ones_3 = sb("ones_3", [3, P], BF16)
        m.logit = sb("logit", [P, NT, H])
        m.eps_c = sb("eps_c", [P, 1])
        m.window_i = sb("window_i", [1, NCH * HALF], I32)
        m.first_i = sb("first_i", [1, NCH * HALF], I32)
        m.end_i = sb("end_i", [1, NCH * HALF], I32)
        m.wide_i = sb("wide_i", [1, 1], I32)
        m.band_i = sb("band_i", [1, 2], I32)

        setup(nc, m)
        wide = nc.values_load(m.wide_i[0:1, 0:1], min_val=0, max_val=1)
        with nc.If(wide == 1):
            gathered_messages(nc, m)
            general_sums(nc, m, "a")
            layer0_nodes(nc, m, from_sums=True)
        with nc.Else():
            layer0_nodes(nc, m, from_sums=False)
        project_edges(nc, m)
        segment_softmax(nc, m)
        attended_messages(nc, m)
        with nc.If(wide == 1):
            general_sums(nc, m, "b")
            layer1_nodes(nc, m, from_sums=True)
        with nc.Else():
            layer1_nodes(nc, m, from_sums=False)


def setup(nc, m):
    with ExitStack() as ctx:
        sb, pb, sem = scoped(nc, ctx)
        src_r, dst_r, typ_r = (sb(n, [HALF, 2, P], I32) for n in ("src_r", "dst_r", "typ_r"))
        wgt_r, srcf_r, dstf_r, typf_r, dstc_r, key_r = (
            sb(n, [HALF, 2, P]) for n in ("wgt_r", "srcf_r", "dstf_r", "typf_r", "dstc_r", "key_r"))
        pad_dst = sb("pad_dst", [1, P - TAIL], I32)
        pad_0 = sb("pad_0", [1, P - TAIL], I32)
        pad_w = sb("pad_w", [1, P - TAIL])
        no_dst = sb("no_dst", [32, P])
        no_key = sb("no_key", [3, 1])
        no_logit = sb("no_logit", [H, 3])
        typ_f = sb("typ_f", [P, NT])
        w0_r = sb("w0_r", [P, F])
        wo_r = sb("wo_r", [P, F])
        bias_in = sb("bias_in", [P, R, H])
        ones = sb("ones", [HALF, P])
        bo_r = sb("bo_r", [3, BT, F])
        bo_left = sb("bo_left", [3, BT * F])
        bo_part = sb("bo_part", [3, 3, BT * F], BF16)
        bo_sum = sb("bo_sum", [3, BT * F])
        ends = sb("ends", [HALF, 2, 2])
        ends_d = sb("ends_d", [HALF, 2, 2, HALF])
        ends_b = sb("ends_b", [P, 2, NT])
        node_0 = sb("node_0", [HALF, NCH])
        node_1 = sb("node_1", [HALF, NCH])
        below = sb("below", [HALF, NCH, NT])
        cover = sb("cover", [HALF, NCH, NT])
        tile_1 = sb("tile_1", [HALF, NT])
        tile_hi = sb("tile_hi", [HALF, NT])
        cand = sb("cand", [HALF, NCH, NT])
        cand2 = sb("cand2", [HALF, NCH, NT])
        not_before = sb("not_before", [HALF, NCH, NT])
        cand3 = sb("cand3", [HALF, NCH, NT])
        start_c = sb("start_c", [HALF, NCH])
        start_low = sb("start_low", [HALF, NCH])
        start_i = sb("start_i", [HALF, NCH], I32)
        dst_at = sb("dst_at", [HALF, NCH, P])
        before = sb("before", [HALF, NCH, P])
        n_before = sb("n_before", [HALF, NCH])
        window_c = sb("window_c", [HALF, NCH])
        window_f = sb("window_f", [1, NCH * HALF])
        tile_id = sb("tile_id", [1, NCH * HALF])
        lag = sb("lag", [1, NCH * HALF])
        apart = sb("apart", [1, NCH * HALF - 1])
        limits = sb("limits", [1, 4])
        first_c = sb("first_c", [HALF, NCH])
        end_c = sb("end_c", [HALF, NCH])
        first_f = sb("first_f", [1, NCH * HALF])
        end_f = sb("end_f", [1, NCH * HALF])
        spare = m.msg[:].rearrange("p t f -> p (t f)")
        early = spare[:, 2 * NPROBE * NT:2 * NPROBE * NT + 4 * RING * W].rearrange("p (t f) -> p t f", f=W)
        shifted, same = (spare[:, k * NPROBE * NT:(k + 1) * NPROBE * NT].rearrange("p (d t) -> p d t", t=NT)
                         for k in range(2))
        dst_b = sb("dst_b", [P, NT])
        found = sb("found", [P, NPROBE])
        found_all = sb("found_all", [P, NPROBE])
        reach_of = sb("reach_of", [1, NPROBE])
        reach = sb("reach", [1, NPROBE + 2])
        ps_edge = [pb(f"ps_edge{i}", [P, 2, NT]) for i in range(3)]
        ps_w = pb("ps_w", [P, 2, F])
        ps_ends = pb("ps_ends", [P, 2, NT])
        ps_first = pb("ps_first", [1, NCH * HALF])
        ps_end = pb("ps_end", [1, NCH * HALF])
        ps_window = pb("ps_window", [1, NCH * HALF])

        edges_in, weights_in, pads = sem("edges_in"), sem("weights_in"), sem("pads")
        pads_out = sem("pads_out")
        w_in, w_turned, edge_ok = sem("w_in"), sem("w_turned"), sem("edge_ok")
        early_tail, early_in, early_out = sem("early_tail"), sem("early_in"), sem("early_out")
        consts, zeroed, ident_ok = sem("consts"), sem("zeroed"), sem("ident_ok")
        rows_ok, circ_out, probes_in = sem("rows_ok"), sem("circ_out"), sem("probes_in")
        transposed, ends_ok, ends_ps = sem("transposed"), sem("ends_ok"), sem("ends_ps")
        cols_ok, cols_ps, found_ok, found_red = (
            sem("cols_ok"), sem("cols_ps"), sem("found_ok"), sem("found_red"))
        start_ok, dst_in, window_ok, window_ps = (
            sem("start_ok"), sem("dst_in"), sem("window_ok"), sem("window_ps"))
        chain = sem("chain")

        block = ctx.enter_context(nc.Block())
        main = (NT - 1) * P

        def load_edges(engine, *arrays):
            for a, rows, pad in arrays:
                engine.dma_start(rows[:, 0, :], a[0:HALF * P].rearrange("(p c) -> p c", c=P)).then_inc(edges_in, 16)
                engine.dma_start(rows[0:HALF - 1, 1, :],
                                 a[HALF * P:main].rearrange("(p c) -> p c", c=P)).then_inc(edges_in, 16)
                engine.dma_start(rows[HALF - 1:HALF, 1, 0:TAIL],
                                 a[main:E].rearrange("(p c) -> p c", p=1)).then_inc(edges_in, 16)
                engine.dma_start(rows[HALF - 1:HALF, 1, TAIL:P], pad[:]).then_inc(edges_in, 16)

        @block.sync
        def _(sp):
            sp.wait_ge(pads, 6)
            load_edges(sp, (m.dst, dst_r, pad_dst), (m.src, src_r, pad_0))
            sp.wait_ge(rows_ok, 1)
            for a in range(2):
                at = a * HALF * P
                sp.dma_start(m.dst_d[at:at + HALF * P].rearrange("(p c) -> p c", c=P),
                             dstf_r[:, a, :]).then_inc(circ_out, 16)
                sp.dma_start(m.typ_d[at:at + HALF * P].rearrange("(p c) -> p c", c=P),
                             typf_r[:, a, :]).then_inc(circ_out, 16)
                for copy in range(3):
                    at = copy * EC + a * HALF * P
                    sp.dma_start(m.key_d[at:at + HALF * P].rearrange("(p c) -> p c", c=P),
                                 key_r[:, a, :]).then_inc(circ_out, 16)
            sp.dma_start(m.dst_d[EP:EP + FAR[-1][0]].rearrange("(p c) -> p c", c=P),
                         no_dst[:]).then_inc(circ_out, 16)
            sp.dma_start(m.key_d.rearrange("(c e) -> c e", c=3)[:, EP:EC], no_key[:],
                         allow_slow_non_contiguous=True).then_inc(circ_out, 16)
            sp.wait_ge(circ_out, 12 * 16)

            def probe(to, a, shift):
                sp.dma_start(to, a[shift:shift + EP].rearrange("(p t) -> p t", t=NT)).then_inc(probes_in, 16)

            probe(m.key_b[:], m.key_d, 0)
            probe(dst_b[:], m.dst_d, 0)
            for d in range(1, NEAR + 1):
                probe(shifted[:, d - 1, :], m.key_d, d)
            for i, (d, _) in enumerate(FAR):
                probe(shifted[:, NEAR + i, :], m.dst_d, d)
            probe(shifted[:, NPROBE - 1, :], m.dst_d, 1)
            sp.wait_ge(early_tail, 1)
            sp.wait_ge(early_in, 4 * RING * 16)
            sp.dma_start(m.rows_d[0:4 * RING * P, :].rearrange("(t p) f -> p t f", p=P), early).then_inc(early_out, 16)
            sp.wait_ge(early_out, 16)

        @block.scalar
        def _(act):
            act.wait_ge(pads, 6)
            load_edges(act, (m.typ, typ_r, pad_0), (m.wgt, wgt_r, pad_w))
            act.dma_start(w0_r[:], m.w0).then_inc(w_in, 16)
            act.dma_start(wo_r[:], m.wo).then_inc(w_in, 16)
            act.dma_start(bias_in[:], m.bias.partition_broadcast(P)).then_inc(weights_in, 16)
            act.dma_start(m.gam_b[:], m.gamma.partition_broadcast(P)).then_inc(weights_in, 16)
            act.dma_start(m.bet_b[:], m.beta.partition_broadcast(P)).then_inc(weights_in, 16)
            act.dma_start(bo_r[:], m.bo[None, None, :].broadcast_to([3, BT, F])).then_inc(weights_in, 16)
            for i, w in enumerate((m.wq, m.wk, m.wv)):
                for r in range(R):
                    act.dma_start(m.w_qkv[:, r, i, :].rearrange("i (h d) -> i h d", h=H),
                                  w[r].rearrange("h i d -> i h d")).then_inc(weights_in, 16)
            for a in (m.logit_d, m.prob_d):
                act.dma_start(a.rearrange("h (c e) -> h c e", c=3)[:, :, EP:EC], no_logit[:, :, None],
                              allow_slow_non_contiguous=True).then_inc(pads_out, 16)
            act.wait_ge(weights_in, (4 + 3 * R) * 16)
            act.wait_ge(pads_out, 32)

        @block.gpsimd
        def _(pool):
            nc.gpsimd.iota(pad_dst[:], [[1, P - TAIL]], base=PAD_DST + TAIL, channel_multiplier=0).then_inc(pads, 1)
            nc.gpsimd.memset(pad_0[:], 0).then_inc(pads, 1)
            nc.gpsimd.memset(pad_w[:], 0.0).then_inc(pads, 1)
            nc.gpsimd.memset(no_dst[:], NO_DST).then_inc(pads, 1)
            nc.gpsimd.memset(no_key[:], -1.0).then_inc(pads, 1)
            nc.gpsimd.memset(no_logit[:], 0.0).then_inc(pads, 1)
            nc.gpsimd.memset(m.ident[:], 0.0).then_inc(zeroed, 1)
            pool.wait_ge(zeroed, 1)
            nc.gpsimd.affine_select(out=m.ident[:], in_=m.ident[:], compare_op=ALU.not_equal, fill=1.0,
                                    base=0, pattern=[[-1, P]], channel_multiplier=1).then_inc(ident_ok, 1)
            nc.gpsimd.iota(m.local_id[:], [[1, BT * P]], base=0, channel_multiplier=0,
                           allow_small_or_imprecise_dtypes=True).then_inc(consts, 1)
            nc.gpsimd.iota(node_0[:], [[HALF * P, NCH]], base=0, channel_multiplier=P,
                           allow_small_or_imprecise_dtypes=True).then_inc(consts, 1)
            nc.gpsimd.memset(ones[:], 1.0).then_inc(consts, 1)
            nc.gpsimd.memset(m.ones_3[:], 1.0).then_inc(consts, 1)
            nc.gpsimd.memset(m.eps_c[:], EPS).then_inc(consts, 1)
            nc.gpsimd.memset(m.msg[:, NT, :], 0.0).then_inc(consts, 1)
            nc.gpsimd.iota(m.batch_0[:], [[BT * P, BATCHES]], base=0, channel_multiplier=0,
                           allow_small_or_imprecise_dtypes=True).then_inc(consts, 1)
            nc.gpsimd.iota(tile_id[:], [[1, NCH * HALF]], base=0, channel_multiplier=0,
                           allow_small_or_imprecise_dtypes=True).then_inc(consts, 1)
            nc.gpsimd.memset(m.edge_i[:, NT:GATHERS, :], 0).then_inc(consts, 1)
            nc.gpsimd.memset(m.edge_f[:, NT:GATHERS, 0:1], NO_DST).then_inc(consts, 1)
            nc.gpsimd.memset(m.edge_f[:, NT:GATHERS, 1:2], 0.0).then_inc(consts, 1)
            pool.wait_ge(circ_out, 12 * 16)
            pool.wait_ge(start_ok, 1)
            pool.nop(nofuse=True)
            for c in range(NCH):
                nc.gpsimd.indirect_dma_start(
                    dst_at[:, c, :], None, m.dst_d.rearrange("(t e) -> t e", e=P),
                    bass.IndirectOffsetOnAxis(start_i[:, c:c + 1], axis=0)).then_inc(dst_in, 16)
            pool.wait_ge(edge_ok, 1)
            nc.gpsimd.tensor_copy(early[:, :, F:W], m.edge_f[:, 0:4 * RING, :]).then_inc(early_tail, 1)
            pool.nop(nofuse=True)
            for t in range(4 * RING):
                nc.gpsimd.indirect_dma_start(
                    early[:, t, 0:F], None, m.x,
                    bass.IndirectOffsetOnAxis(m.edge_i[:, t, 0:1], axis=0)).then_inc(early_in, 16)
            pool.wait_ge(found_ok, 1)
            nc.gpsimd.partition_all_reduce(found_all[:], found[:], P, bass.bass_isa.ReduceOp.max).then_inc(found_red, 1)

        @block.vector
        def _(dve):
            links = [0]

            def link(ins):
                links[0] += 1
                ins.then_inc(chain, 1)
                dve.wait_ge(chain, links[0])

            dve.wait_ge(edges_in, 16 * 16)
            nc.vector.tensor_copy(srcf_r[:], src_r[:])
            nc.vector.tensor_copy(typf_r[:], typ_r[:])
            link(nc.vector.tensor_copy(dstf_r[:], dst_r[:]))
            nc.vector.tensor_scalar(dstc_r[:], dstf_r[:], float(N - 1), None, ALU.min)
            nc.vector.tensor_reduce(ends[:, 0, :], dstf_r[:], AX.X, ALU.min)
            nc.vector.tensor_reduce(ends[:, 1, :], dstf_r[:], AX.X, ALU.max)
            nc.vector.scalar_tensor_tensor(key_r[:], dstf_r[:], 8.0, typf_r[:], ALU.mult, ALU.add).then_inc(rows_ok, 1)
            dve.wait_ge(rows_ok, 1)
            dve.wait_ge(ident_ok, 1)
            for i in range(2):
                for a in range(2):
                    last = nc.vector.tensor_scalar(ends_d[:, i, a, :], m.ident[0:HALF, 0:HALF],
                                                   ends[:, i, a:a + 1], None, ALU.mult)
            last.then_inc(ends_ok, 1)
            for i, d in enumerate([*range(1, NEAR + 1), *(far for _, far in FAR), EP // 2]):
                last = nc.vector.memset(reach_of[:, i:i + 1], float(-(-min(d, EP // 2) // SHIFTS)))
            link(last)

            dve.wait_ge(transposed, 1)
            nc.vector.tensor_copy(m.edge_i[:, 0:NT, :], ps_edge[0][:].rearrange("p i t -> p t i"))
            nc.vector.tensor_copy(m.edge_f[:, 0:NT, :], ps_edge[1][:].rearrange("p i t -> p t i")).then_inc(edge_ok, 1)

            dve.wait_ge(ends_ps, 1)
            dve.wait_ge(consts, 11)
            nc.vector.tensor_copy(ends_b[:], ps_ends[:])
            nc.vector.tensor_scalar(tile_1[:], m.local_id[0:HALF, 0:NT], 1.0, None, ALU.add)
            nc.vector.tensor_scalar(tile_hi[:], m.local_id[0:HALF, 0:NT], float(EP), None, ALU.add)
            link(nc.vector.tensor_scalar(node_1[:], node_0[:], float(P), None, ALU.add))
            for c in range(NCH):
                nc.vector.tensor_scalar(not_before[:, c, :], ends_b[0:HALF, 1, :], node_0[:, c:c + 1],
                                        None, ALU.is_ge)
                last = nc.vector.tensor_scalar(below[:, c, :], ends_b[0:HALF, 0, :], node_1[:, c:c + 1],
                                               None, ALU.is_lt)
            link(last)
            link(nc.vector.scalar_tensor_tensor(cand3[:], not_before[:], -float(EP),
                                                tile_hi[:, None, :].broadcast_to([HALF, NCH, NT]), ALU.mult, ALU.add))
            link(nc.vector.tensor_reduce(start_low[:], cand3[:], AX.X, ALU.min))
            link(nc.vector.tensor_scalar(start_c[:], start_low[:], float(NT), None, ALU.min))
            nc.vector.tensor_copy(start_i[:], start_c[:]).then_inc(start_ok, 1)
            for c in range(NCH):
                last = nc.vector.scalar_tensor_tensor(cover[:, c, :], ends_b[0:HALF, 1, :], node_0[:, c:c + 1],
                                                      below[:, c, :], ALU.is_ge, ALU.mult)
            link(last)
            nc.vector.scalar_tensor_tensor(cand[:], cover[:], -float(EP), tile_hi[:, None, :].broadcast_to([HALF, NCH, NT]),
                                           ALU.mult, ALU.add)
            link(nc.vector.tensor_tensor(cand2[:], cover[:], tile_1[:, None, :].broadcast_to([HALF, NCH, NT]), ALU.mult))
            nc.vector.tensor_reduce(first_c[:], cand[:], AX.X, ALU.min)
            nc.vector.tensor_reduce(end_c[:], cand2[:], AX.X, ALU.max).then_inc(cols_ok, 1)
            dve.wait_ge(cols_ps, 1)
            link(nc.vector.tensor_scalar(first_f[:], ps_first[:], float(NT - 1), None, ALU.min))
            nc.vector.tensor_copy(m.first_i[:], first_f[:])
            link(nc.vector.scalar_tensor_tensor(end_f[:], first_f[:], 1.0, ps_end[:], ALU.add, ALU.max))
            nc.vector.tensor_copy(m.end_i[:], end_f[:])

            dve.wait_ge(dst_in, NCH * 16)
            for c in range(NCH):
                last = nc.vector.tensor_scalar(before[:, c, :], dst_at[:, c, :], node_0[:, c:c + 1], None, ALU.is_lt)
            link(last)
            link(nc.vector.tensor_reduce(n_before[:], before[:], AX.X, ALU.add))
            nc.vector.scalar_tensor_tensor(window_c[:], start_c[:], float(P), n_before[:],
                                           ALU.mult, ALU.add).then_inc(window_ok, 1)
            dve.wait_ge(window_ps, 1)
            link(nc.vector.tensor_copy(window_f[:], ps_window[:]))
            nc.vector.tensor_copy(m.window_i[:], window_f[:])
            nc.vector.tensor_tensor(apart[:], window_f[:, 1:], window_f[:, 0:NCH * HALF - 1], ALU.subtract)
            link(nc.vector.scalar_tensor_tensor(lag[:], tile_id[:], -float(P // 2), window_f[:], ALU.mult, ALU.add))
            nc.vector.tensor_reduce(limits[:, 0:1], apart[:], AX.X, ALU.max)
            link(nc.vector.tensor_reduce(limits[:, 1:2], lag[:], AX.X, ALU.max))
            nc.vector.tensor_scalar(limits[:, 0:1], limits[:, 0:1], float(P), None, ALU.is_gt)
            link(nc.vector.tensor_scalar(limits[:, 1:2], limits[:, 1:2], float(MOST_AHEAD), None, ALU.is_gt))
            link(nc.vector.tensor_tensor(limits[:, 2:3], limits[:, 0:1], limits[:, 1:2], ALU.max))

            link(nc.vector.tensor_copy(typ_f[:], ps_edge[2][:, 0, :]))
            for r in range(R):
                nc.vector.tensor_scalar(m.of_type[:, :, r], typ_f[:], float(r), None, ALU.is_equal)
            dve.wait_ge(w_turned, 1)
            nc.vector.tensor_copy(m.w_nb[:], ps_w[:, 0, :])
            nc.vector.tensor_copy(m.w_out[:], ps_w[:, 1, :])
            dve.wait_ge(weights_in, (4 + 3 * R) * 16)
            nc.vector.tensor_scalar(m.bias_r[:], bias_in[:], SCALE, None, ALU.mult)

            bo_flat = bo_r[:].rearrange("p b f -> p (b f)")
            for k in range(3):
                link(nc.vector.tensor_copy(bo_part[:, k, :], bo_left[:] if k else bo_flat))
                if k < 2:
                    link(nc.vector.tensor_tensor(bo_left[:], bo_left[:] if k else bo_flat, bo_part[:, k, :], ALU.subtract))
            link(nc.vector.tensor_scalar(bo_sum[:], bo_part[:, 0, :], m.ident[0:3, 0:1], None, ALU.mult))
            for k in (1, 2):
                link(nc.vector.scalar_tensor_tensor(bo_sum[:], bo_part[:, k, :], m.ident[0:3, k:k + 1], bo_sum[:],
                                                    ALU.mult, ALU.add))
            nc.vector.tensor_copy(m.bo_parts[:], bo_sum[:])

            dve.wait_ge(probes_in, (NPROBE + 2) * 16)
            keys = m.key_b[:, None, :].broadcast_to([P, NEAR, NT])
            dsts = dst_b[:, None, :].broadcast_to([P, len(FAR), NT])
            nc.vector.tensor_tensor(same[:, 0:NEAR, :], shifted[:, 0:NEAR, :], keys, ALU.is_equal)
            nc.vector.tensor_tensor(same[:, NEAR:NPROBE - 1, :], shifted[:, NEAR:NPROBE - 1, :], dsts, ALU.is_equal)
            link(nc.vector.tensor_tensor(same[:, NPROBE - 1, :], shifted[:, NPROBE - 1, :], dst_b[:], ALU.is_lt))
            nc.vector.tensor_reduce(found[:], same[:], AX.X, ALU.max).then_inc(found_ok, 1)
            dve.wait_ge(found_red, 1)
            nc.vector.tensor_tensor(m.wide_i[:], limits[:, 2:3], found_all[0:1, NPROBE - 1:NPROBE], ALU.max)
            link(nc.vector.tensor_tensor(reach[:, 0:NPROBE], found_all[0:1, :], reach_of[:], ALU.mult))
            r_max, r_steps = reach[:, NPROBE:NPROBE + 1], reach[:, NPROBE + 1:NPROBE + 2]
            link(nc.vector.tensor_reduce(r_max, reach[:, 0:NPROBE], AX.X, ALU.max))
            link(nc.vector.tensor_scalar(r_steps, r_max, 1.0, None, ALU.max))
            nc.vector.tensor_scalar(m.band_i[:, 0:1], r_steps, -float(SHIFTS), float(EC), ALU.mult, ALU.add)
            nc.vector.tensor_copy(m.band_i[:, 1:2], r_steps)

        @block.tensor
        def _(pe):
            pe.wait_ge(ident_ok, 1)
            pe.wait_ge(rows_ok, 1)
            small = m.ident[0:HALF, 0:HALF]
            for i, rows in enumerate((srcf_r, dstc_r, dstf_r, wgt_r, typf_r)):
                for a in range(2):
                    last = nc.tensor.transpose(ps_edge[i // 2][:, i % 2, a * HALF:(a + 1) * HALF], rows[:, a, :], small)
            last.then_inc(transposed, 1)
            pe.wait_ge(ends_ok, 1)
            pe.wait_ge(consts, 11)
            for i in range(2):
                for a in range(2):
                    last = nc.tensor.matmul(ps_ends[:, i, a * HALF:(a + 1) * HALF], ones[:],
                                            ends_d[:, i, a, :], start=True, stop=True)
            last.then_inc(ends_ps, 1)
            pe.wait_ge(w_in, 32)
            nc.tensor.transpose(ps_w[:, 0, :], w0_r[:], m.ident[:])
            nc.tensor.transpose(ps_w[:, 1, :], wo_r[:], m.ident[:]).then_inc(w_turned, 1)
            pe.wait_ge(cols_ok, 1)
            for c in range(NCH):
                nc.tensor.matmul(ps_first[:, c * HALF:(c + 1) * HALF], first_c[:, c:c + 1], small,
                                 start=True, stop=True)
                last = nc.tensor.matmul(ps_end[:, c * HALF:(c + 1) * HALF], end_c[:, c:c + 1], small,
                                        start=True, stop=True)
            last.then_inc(cols_ps, 1)
            pe.wait_ge(window_ok, 1)
            for c in range(NCH):
                last = nc.tensor.matmul(ps_window[:, c * HALF:(c + 1) * HALF], window_c[:, c:c + 1], small,
                                        start=True, stop=True)
            last.then_inc(window_ps, 1)


def lead(engine, *sems):
    for s in sems:
        engine.nop().then_inc(s, LEAD)


def gathered_messages(nc, m):
    with ExitStack() as ctx:
        sb, _, sem = scoped(nc, ctx)
        rows = sb("gm_rows", [P, SLOTS, F])
        idx = sb("gm_idx", [P, SLOTS], I32)
        idx_ok, msg_ok = sem("gm_idx_ok"), sem("gm_msg_ok")
        gathered = [sem(f"gm_gathered{i}") for i in range(SLOTS)]
        turns = NT // TURN
        block = ctx.enter_context(nc.Block())

        @block.gpsimd
        def _(pool):
            with pool.Fori(0, turns) as i:
                for j in range(TURN):
                    pool.wait_ge(idx_ok, i * TURN + j + 1)
                    pool.nop(nofuse=True)
                    nc.gpsimd.indirect_dma_start(
                        rows[:, j % SLOTS, :], None, m.x,
                        bass.IndirectOffsetOnAxis(idx[:, j % SLOTS:j % SLOTS + 1], axis=0),
                    ).then_inc(gathered[j % SLOTS], 16)

        @block.vector
        def _(dve):
            for j in range(SLOTS):
                nc.vector.tensor_copy(idx[:, j:j + 1], m.edge_i[:, j, 0:1]).then_inc(idx_ok, 1)
            with dve.Fori(0, turns) as i:
                for j in range(TURN):
                    t, s = i * TURN + j, j % SLOTS
                    dve.wait_ge(gathered[s], (i * (TURN // SLOTS) + j // SLOTS) * 16 + 16)
                    nc.vector.tensor_scalar(m.msg[:, bass.ds(t, 1), 0:F], rows[:, s:s + 1, :],
                                            m.edge_f[:, bass.ds(t, 1), 1], None, ALU.mult).then_inc(msg_ok, 1)
                    dve.wait_ge(msg_ok, t + 1)
                    nc.vector.tensor_copy(idx[:, s:s + 1], m.edge_i[:, bass.ds(t + SLOTS, 1), 0]).then_inc(idx_ok, 1)


def general_sums(nc, m, name):
    with ExitStack() as ctx:
        sb, pb, sem = scoped(nc, ctx)
        onehot = sb("gs_onehot" + name, [P, P])
        dst_n = sb("gs_dst" + name, [P, 2, NT + 1])
        total = sb("gs_total" + name, [P, F])
        ps = pb("gs_ps" + name, [P, F])
        with nc.Block() as block:
            @block.vector
            def _(dve):
                nc.vector.tensor_copy(dst_n[:, 1, :], m.edge_f[:, 0:NT + 1, 0])
        with nc.Fori(0, NB) as n:
            with nc.Block() as block:
                @block.vector
                def _(dve):
                    nc.vector.tensor_copy(dst_n[:, 0, :], dst_n[:, 1, :])
                    nc.vector.memset(total[:], 0.0)
            start = nc.values_load(m.first_i[0:1, bass.ds(n, 1)], min_val=0, max_val=NT - 1)
            end = nc.values_load(m.end_i[0:1, bass.ds(n, 1)], min_val=1, max_val=NT)
            with nc.Fori(start, end) as k:
                with ExitStack() as c1:
                    _, _, sem1 = scoped(nc, c1)
                    hot, summed = sem1("gs_hot" + name), sem1("gs_summed" + name)
                    with nc.Block() as block:
                        @block.vector
                        def _(dve):
                            nc.vector.tensor_scalar(onehot[:], m.local_id[:, 0:P], dst_n[:, 0, bass.ds(k, 1)],
                                                    None, ALU.is_equal).then_inc(hot, 1)
                            dve.wait_ge(summed, 1)
                            nc.vector.tensor_tensor(total[:], total[:], ps[:], ALU.add)

                        @block.tensor
                        def _(pe):
                            pe.wait_ge(hot, 1)
                            nc.tensor.matmul(ps[:], onehot[:], m.msg[:, bass.ds(k, 1), 0:F], start=True,
                                             stop=True).then_inc(summed, 1)
            with ExitStack() as c2:
                _, _, sem2 = scoped(nc, c2)
                stored = sem2("gs_stored" + name)
                with nc.Block() as block:
                    @block.vector
                    def _(dve):
                        nc.vector.tensor_scalar(dst_n[:, 1, :], dst_n[:, 0, :], -float(P), None, ALU.add)

                    @block.sync
                    def _(sp):
                        sp.dma_start(m.sums_d[bass.ds(n * P, P), :], total[:]).then_inc(stored, 16)
                        sp.wait_ge(stored, 16)


def rows_of(a, first, count):
    return a[bass.ds(first, count * P), :].rearrange("(g p) f -> p g f", p=P)


def load_group(engine, to, a, g, landed, tail_landed):
    if isinstance(g, int) and g == GROUPS:
        engine.dma_start(to[:, 0:REST - 1, :], rows_of(a, g * GT * P, REST - 1)).then_inc(tail_landed, 16)
        engine.wait_ge(tail_landed, 16)
        engine.dma_start(to[0:LAST_ROWS, REST - 1, :], a[(NB - 1) * P:N, :]).then_inc(landed, 16)
    else:
        engine.dma_start(to, rows_of(a, g * (GT * P), GT)).then_inc(landed, 16)


def store_group(engine, a, of, g, landed, tail_landed):
    if isinstance(g, int) and g == GROUPS:
        engine.dma_start(rows_of(a, g * GT * P, REST - 1), of[:, 0:REST - 1, :]).then_inc(landed, 16)
        engine.dma_start(a[(NB - 1) * P:N, :], of[0:LAST_ROWS, REST - 1, :]).then_inc(tail_landed, 16)
    else:
        engine.dma_start(rows_of(a, g * (GT * P), GT), of).then_inc(landed, 16)




def x_slot(o):
    return (o // GB) % XSLOTS


def y_slot(o):
    return (o // GB) % 2


def window_starts(nc, m, i, o):
    _, starts = nc.values_load_multi_w_load_instructions(
        m.window_i[0:1, bass.ds((i * TB + o) * BT, GT)], engines=[ENG.SP], min_val=0, max_val=EP,
        skip_runtime_bounds_check_because="the setup counts them")
    return starts


def load_windows(sp, a, win, win_in, used, starts, i, o):
    sp.wait_ge(used, done(i * TB + o - WSLOTS))
    sp.nop(nofuse=True)
    for n in range(BT):
        start = starts[(o % GB) * BT + n]
        sp.dma_start(win[:, o % WSLOTS, n, :], a[bass.ds(start, P), :]).then_inc(win_in[o % WSLOTS], 16)


def one_hots(nc, dve, m, win, win_in, rel, rel_ok, onehot, hot_ready, used, weighted):
    def hots(i, o):
        b, u, w = i * TB + o, o % 2, o % WSLOTS
        dve.wait_ge(win_in[w], (i * (TB // WSLOTS) + o // WSLOTS) * BT * 16 + BT * 16)
        nc.vector.tensor_scalar(rel[:, u, :], win[:, w, :, F], m.batch_0[:, bass.ds(b, 1)], None,
                                ALU.subtract).then_inc(rel_ok, 1)
        yield
        dve.wait_ge(rel_ok, done(b))
        dve.wait_ge(used, done(b - 2))
        for n in range(BT):
            if weighted:
                last = nc.vector.tensor_scalar(onehot[:, u, n, :], m.local_id[:, n * P:(n + 1) * P],
                                               rel[:, u, n:n + 1], win[:, w, n, F + 1:F + 2], ALU.is_equal, ALU.mult)
            else:
                last = nc.vector.tensor_scalar(onehot[:, u, n, :], m.local_id[:, n * P:(n + 1) * P],
                                               rel[:, u, n:n + 1], None, ALU.is_equal)
            if n == BT - 1:
                last.then_inc(hot_ready, 1)
            yield
    return hots


def steps(engine, step):
    with engine.Fori(0, ROUNDS) as i:
        for o in range(TB):
            step(i, o)
    for o in range(BATCHES - ROUNDS * TB):
        step(ROUNDS, o)


def layer0_nodes(nc, m, from_sums):
    name = "n0s_" if from_sums else "n0_"
    with ExitStack() as ctx:
        sb, pb, sem = scoped(nc, ctx)
        xg = sb(name + "xg", [P, XSLOTS, GT, F])
        if from_sums:
            sg = sb(name + "sg", [P, 2, GT, F])
        else:
            rows = sb(name + "rows", [P, RING, 4, W])
            idx = sb(name + "idx", [P, RING, 4], I32)
            win = sb(name + "win", [P, WSLOTS, BT, W])
            rel = sb(name + "rel", [P, 2, BT])
            onehot = sb(name + "onehot", [P, 2, BT, P])
        yg = sb(name + "yg", [P, 2, GT, F])
        yt = sb(name + "yt", [P, 4, BT, F])
        on_pe = BT // 2
        h = sb(name + "h", [P, 2, BT - on_pe, F])
        stats = sb(name + "stats", [P, 2, BT, 6])
        mv = sb(name + "mv", [P, 2, BT, 2])
        std = sb(name + "std", [P, 2, BT])
        rstd = sb(name + "rstd", [P, 2, BT])
        shift = sb(name + "shift", [P, 2, BT])
        ps_t = [pb(f"{name}ps_t{i}", [P, BT, P]) for i in range(4)]
        ps_m = [pb(f"{name}ps_m{i}", [P, BT, F]) for i in range(4)]
        x_in = [sem(f"{name}x_in{i}") for i in range(XSLOTS)]
        s_in = [sem(f"{name}s_in{i}") for i in range(2)]
        win_in = [sem(f"{name}win_in{i}") for i in range(WSLOTS)]
        gathered = [sem(f"{name}gathered{i}") for i in range(RING)]
        rows_out = [sem(f"{name}rows_out{i}") for i in range(RING)]
        stored = [sem(f"{name}stored{i}") for i in range(2)]
        x_tail, s_tail, y_tail = (sem(name + n) for n in ("x_tail", "s_tail", "y_tail"))
        yt_ready, yt_copied, product = (sem(name + n) for n in ("yt_ready", "yt_copied", "product"))
        idx_ok, rel_ok, hot_ready, h_ready = (sem(name + n) for n in ("idx_ok", "rel_ok", "hot_ready", "h_ready"))
        stats_ok, mv_ready, std_ready = (sem(name + n) for n in ("stats_ok", "mv_ready", "std_ready"))
        rstd_ok, shift_ready, y_ready = (sem(name + n) for n in ("rstd_ok", "shift_ready", "y_ready"))
        block = ctx.enter_context(nc.Block())

        def h_tile(o, n):
            return ps_m[o % 4][:, n, :] if n < on_pe else h[:, o % 2, n - on_pe, :]

        @block.sync
        def _(sp):
            if not from_sums:
                lead(sp, *rows_out)

            starts = []

            def step(i, o):
                if from_sums:
                    if o % GB == 0:
                        sp.wait_ge(yt_ready, done(i * TB + o + 1 - 2 * GB))
                        load_group(sp, sg[:, y_slot(o), :, :], m.sums_d, i * XSLOTS + o // GB, s_in[y_slot(o)], s_tail)
                else:
                    if o % GB == 0:
                        starts[:] = window_starts(nc, m, i, o)
                    q = (o + AHEAD - 1) // 2
                    sp.wait_ge(rows_out[q % RING], LEAD + (i + q // RING) * 16)
                    sp.nop(nofuse=True)
                    load_windows(sp, m.rows_d, win, win_in, yt_ready, starts, i, o)

            steps(sp, step)
            if not from_sums:
                for q in range(QUADS - RING, QUADS):
                    sp.wait_ge(rows_out[q % RING], LEAD + q // RING * 16)

        @block.gpsimd
        def _(pool):
            def gather(i, o):
                q = i * RING + o
                pool.wait_ge(rows_out[o], i * 16 + (LEAD - 16))
                nc.gpsimd.tensor_copy(rows[:, o, :, F:W], m.edge_f[:, bass.ds(q * 4, 4), :])
                nc.gpsimd.tensor_copy(idx[:, o, :], m.edge_i[:, bass.ds(q * 4, 4), 0]).then_inc(idx_ok, 1)
                pool.wait_ge(idx_ok, q - RING + 1)
                pool.nop(nofuse=True)
                for k in range(4):
                    nc.gpsimd.indirect_dma_start(
                        rows[:, o, k, 0:F], None, m.x,
                        bass.IndirectOffsetOnAxis(idx[:, o, k:k + 1], axis=0)).then_inc(gathered[o], 16)

            if not from_sums:
                with pool.Fori(1, QUADS // RING) as i:
                    for o in range(RING):
                        gather(i, o)
                for o in range(QUADS % RING):
                    gather(QUADS // RING, o)
            pool.wait_ge(stored[0], LEAD + GROUPS // 2 * 16 + 16)
            pool.wait_ge(stored[1], LEAD + GROUPS // 2 * 16)
            pool.wait_ge(y_tail, 16)

        @block.tensor
        def _(pe):
            lead(pe, yt_ready, product)

            def sum_up(i, o):
                b, u, s = i * TB + o, o % 2, x_slot(o)
                pe.wait_ge(x_in[s], (i + o // TB) * 16 + 16)
                pe.wait_ge(yt_copied, done(b - 4))
                if from_sums:
                    pe.wait_ge(s_in[y_slot(o)], (i * (XSLOTS // 2) + o // GB // 2) * 16 + 16)
                else:
                    pe.wait_ge(hot_ready, done(b))
                for n in range(BT):
                    nc.tensor.matmul(ps_t[o % 4][:, n, :], xg[:, s, (o % 2) * BT + n, :], m.ident[:], start=True, stop=False)
                    if from_sums:
                        last = nc.tensor.matmul(ps_t[o % 4][:, n, :], sg[:, y_slot(o), (o % 2) * BT + n, :], m.ident[:],
                                                start=False, stop=True)
                    else:
                        last = nc.tensor.matmul(ps_t[o % 4][:, n, :], win[:, o % WSLOTS, n, 0:F], onehot[:, u, n, :],
                                                start=False, stop=True)
                last.then_inc(yt_ready, 1)

            def multiply(i, o):
                b = i * TB + o
                pe.wait_ge(yt_copied, done(b))
                pe.wait_ge(y_ready, done(b - 4))
                for n in range(BT):
                    last = nc.tensor.matmul(ps_m[o % 4][:, n, :], yt[:, o % 4, n, :], m.w_nb[:],
                                            start=True, stop=(n >= on_pe))
                    if n < on_pe:
                        nc.tensor.matmul(ps_m[o % 4][:, n, :], m.ident[:], xg[:, x_slot(o), (o % 2) * BT + n, :],
                                         start=False, stop=True)
                last.then_inc(product, 1)

            sum_up(0, 0)
            sum_up(0, 1)
            with pe.Fori(0, ROUNDS) as i:
                for o in range(TB):
                    multiply(i, o)
                    sum_up(i, o + 2)
            multiply(ROUNDS, 0)
            multiply(ROUNDS, 1)

        @block.scalar
        def _(act):
            lead(act, yt_copied, std_ready, y_ready, *stored)
            nc.scalar.preload_act_table(ACT.Sqrt)

            def store_rows(i, o):
                q = i * RING + o
                act.wait_ge(idx_ok, q - RING + 1)
                act.nop(nofuse=True)
                act.wait_ge(gathered[o % RING], (i + o // RING) * 64)
                act.nop(nofuse=True)
                act.dma_start(m.rows_d[bass.ds(q * (4 * P), 4 * P), :].rearrange("(g p) f -> p g f", p=P),
                              rows[:, o % RING, :, :]).then_inc(rows_out[o % RING], 16)

            ahead = (XSLOTS - 1) * GB

            def load(i, o):
                b, g = i * TB + o, i * XSLOTS + o // GB
                act.wait_ge(yt_ready, done(b + 1 - TB))
                act.wait_ge(h_ready, done(b + 1 - TB))
                act.nop(nofuse=True)
                load_group(act, xg[:, x_slot(o), :, :], m.x, g, x_in[x_slot(o)], x_tail)

            def copy_yt(i, o):
                b, u = i * TB + o, o % 4
                act.wait_ge(yt_ready, done(b))
                act.wait_ge(product, done(b - 4))
                nc.scalar.copy(yt[:, u, :, :], ps_t[u][:]).then_inc(yt_copied, 1)

            def root(i, o):
                b, u = i * TB + o, o % 2
                act.wait_ge(mv_ready, done(b))
                nc.scalar.activation(std[:, u, :], mv[:, u, :, 1], ACT.Sqrt, bias=m.eps_c[:]).then_inc(std_ready, 1)

            def normalise(i, o):
                b, u, s = i * TB + o, o % 2, y_slot(o)
                act.wait_ge(shift_ready, done(b))
                if o % GB == 0:
                    act.wait_ge(stored[s], LEAD + (i * (XSLOTS // 2) + o // GB // 2) * 16)
                for n in range(BT):
                    last = nc.scalar.activation(yg[:, s, (o % 2) * BT + n, :], h_tile(o, n), ACT.Identity,
                                                bias=shift[:, u, n:n + 1], scale=rstd[:, u, n:n + 1])
                last.then_inc(y_ready, 1)
                if o % GB == GB - 1:
                    act.wait_ge(y_ready, done(b))
                    act.nop(nofuse=True)
                    store_group(act, m.x1_d, yg[:, s, :, :], i * XSLOTS + o // GB, stored[s], y_tail)

            for o in range(0, ahead, GB):
                load(0, o)
            if not from_sums:
                for o in range(RING, STORED):
                    store_rows(0, o)
            copy_yt(0, 0)
            copy_yt(0, 1)

            def step(i, o, last):
                root(i, o)
                if not last or o < TB:
                    copy_yt(i, o + 2)
                normalise(i, o)
                if o % GB == 0:
                    if o < TB and not from_sums:
                        store_rows(i, o // 2 + STORED)
                    if not last or o + ahead <= TB:
                        load(i, o + ahead)

            with act.Fori(0, ROUNDS - 1) as i:
                for o in range(TB):
                    step(i, o, False)
            for o in range(TB + GB):
                step(ROUNDS - 1, o, True)

        @block.vector
        def _(dve):
            lead(dve, rel_ok, hot_ready, h_ready, stats_ok, mv_ready, rstd_ok, shift_ready)
            moments, inverting = norm_steps(nc, dve, stats, mv, std, rstd, shift,
                                            stats_ok, mv_ready, std_ready, rstd_ok, shift_ready)
            if not from_sums:
                hots = one_hots(nc, dve, m, win, win_in, rel, rel_ok, onehot, hot_ready, yt_ready, True)

            def step(i, o, other):
                b, u, half = i * TB + o, o % 2, (o % 2) * BT
                dve.wait_ge(product, done(b))
                dve.wait_ge(y_ready, done(b - 2))
                nc.vector.tensor_tensor(h[:, u, :, :], ps_m[o % 4][:, on_pe:BT, :],
                                        xg[:, x_slot(o), half + on_pe:half + BT, :], ALU.add).then_inc(h_ready, 1)
                next(other, None)
                dve.wait_ge(h_ready, done(b))
                moments(i, o, lambda n: h_tile(o, n), other)
                next(other, None)
                next(other, None)
                invert = inverting(i, o)
                next(invert)
                next(other, None)
                next(invert, None)
                for _ in other:
                    pass

            none = iter(())
            if not from_sums:
                for o in range(3):
                    list(hots(0, o))
            with dve.Fori(0, ROUNDS - 1) as i:
                for o in range(TB):
                    step(i, o, none if from_sums else hots(i, o + 3))
            for o in range(TB + 2):
                step(ROUNDS - 1, o, none if from_sums or o + 3 >= TB + 2 else hots(ROUNDS - 1, o + 3))


def norm_steps(nc, dve, stats, mv, std, rstd, shift, stats_ok, mv_ready, std_ready, rstd_ok, shift_ready):
    def moments(i, o, tile, other):
        b, u = i * TB + o, o % 2
        for n in range(BT):
            last = nc.vector.bn_stats(stats[:, u, n, :], tile(n))
        last.then_inc(stats_ok, 1)
        next(other, None)
        dve.wait_ge(stats_ok, done(b))
        dve.nop(nofuse=True)
        for n in range(BT):
            last = nc.vector.bn_aggr(mv[:, u, n, :], stats[:, u, n, :])
        last.then_inc(mv_ready, 1)

    def inverting(i, o):
        b, u = i * TB + o, o % 2
        dve.wait_ge(std_ready, done(b))
        nc.vector.reciprocal(rstd[:, u, :], std[:, u, :]).then_inc(rstd_ok, 1)
        yield
        dve.wait_ge(rstd_ok, done(b))
        nc.vector.scalar_tensor_tensor(shift[:, u, :], mv[:, u, :, 0], -1.0, rstd[:, u, :],
                                       ALU.mult, ALU.mult).then_inc(shift_ready, 1)
    return moments, inverting


def project_edges(nc, m):
    with ExitStack() as ctx:
        sb, pb, sem = scoped(nc, ctx)
        rows = sb("pe_rows", [P, SLOTS, 2, F])
        idx = sb("pe_idx", [P, SLOTS, 2], I32)
        typ_b = sb("pe_typ_b", [P, TURN, P])
        xt = sb("pe_xt", [P, 2, R, 2, P])
        q = sb("pe_q", [P, 2, F])
        qk = sb("pe_qk", [P, 2, H, HD + R])
        dot = sb("pe_dot", [P, 2, H])
        ps_t = [pb(f"pe_ps_t{i}", [P, 2, P]) for i in range(2)]
        ps_qkv = [pb(f"pe_ps_qkv{i}", [P, 3, F]) for i in range(2)]
        src_in = [sem(f"pe_src_in{i}") for i in range(SLOTS)]
        dst_in = [sem(f"pe_dst_in{i}") for i in range(SLOTS)]
        typ_in = [sem(f"pe_typ_in{i}") for i in range(2)]
        idx_ok, xt_ready, masked = sem("pe_idx_ok"), sem("pe_xt_ready"), sem("pe_masked")
        projected, v_out = sem("pe_projected"), sem("pe_v_out")
        qk_ok, dot_ok, logit_ok = sem("pe_qk_ok"), sem("pe_dot_ok"), sem("pe_logit_ok")
        turns = NT // TURN
        half = TURN // 2
        block = ctx.enter_context(nc.Block())

        @block.sync
        def _(sp):
            with sp.Fori(0, turns) as i:
                for h in range(2):
                    sp.wait_ge(masked, done(i * TURN + (h + 1) * half - 1 - TURN))
                    sp.dma_start(typ_b[:, h * half:(h + 1) * half, :].rearrange("p t e -> p (t e)"),
                                 m.typ_d[bass.ds((i * TURN + h * half) * P, half * P)].partition_broadcast(P)
                                 ).then_inc(typ_in[h], 16)

        @block.gpsimd
        def _(pool):
            with pool.Fori(0, turns) as i:
                for j in range(TURN):
                    t, s = i * TURN + j, j % SLOTS
                    pool.wait_ge(idx_ok, t + 1)
                    pool.nop(nofuse=True)
                    nc.gpsimd.indirect_dma_start(
                        rows[:, s, 0, :], None, m.x1_d,
                        bass.IndirectOffsetOnAxis(idx[:, s, 0:1], axis=0)).then_inc(src_in[s], 16)
                    nc.gpsimd.indirect_dma_start(
                        rows[:, s, 1, :], None, m.x1_d,
                        bass.IndirectOffsetOnAxis(idx[:, s, 1:2], axis=0)).then_inc(dst_in[s], 16)

        @block.tensor
        def _(pe):
            lead(pe, xt_ready, projected)

            def turn_rows(i, j):
                t, s = i * TURN + j, j % SLOTS
                landed = (i * (TURN // SLOTS) + j // SLOTS) * 16 + 16
                pe.wait_ge(src_in[s], landed)
                pe.wait_ge(dst_in[s], landed)
                pe.wait_ge(masked, done(t - 2))
                nc.tensor.transpose(ps_t[j % 2][:, 0, :], rows[:, s, 0, :], m.ident[:])
                nc.tensor.transpose(ps_t[j % 2][:, 1, :], rows[:, s, 1, :], m.ident[:]).then_inc(xt_ready, 1)

            def project(i, j):
                t, u = i * TURN + j, j % 2
                pe.wait_ge(masked, done(t))
                pe.wait_ge(qk_ok, done(t - 2))
                for r in range(R):
                    nc.tensor.matmul(ps_qkv[u][:, 0, :], xt[:, u, r, 1, :], m.w_qkv[:, r, 0, :],
                                     start=(r == 0), stop=(r == R - 1))
                for r in range(R):
                    last = nc.tensor.matmul(ps_qkv[u][:, 1:3, :], xt[:, u, r, 0, :], m.w_qkv[:, r, 1:3, :],
                                            start=(r == 0), stop=(r == R - 1))
                last.then_inc(projected, 1)

            turn_rows(0, 0)
            turn_rows(0, 1)
            with pe.Fori(0, turns - 1) as i:
                for j in range(TURN):
                    turn_rows(i, j + 2)
                    project(i, j)
            for j in range(TURN):
                if j + 2 < TURN:
                    turn_rows(turns - 1, j + 2)
                project(turns - 1, j)

        @block.scalar
        def _(act):
            lead(act, v_out)
            with act.Fori(0, turns) as i:
                for j in range(TURN):
                    t = i * TURN + j
                    act.wait_ge(projected, done(t))
                    act.wait_ge(qk_ok, done(t - 2))
                    nc.scalar.copy(q[:, j % 2, :], ps_qkv[j % 2][:, 0, :])
                    nc.scalar.copy(m.msg[:, bass.ds(t, 1), 0:F], ps_qkv[j % 2][:, 2:3, :]).then_inc(v_out, 1)

        @block.vector
        def _(dve):
            lead(dve, masked, qk_ok, dot_ok, logit_ok)
            for j in range(SLOTS):
                nc.vector.tensor_copy(idx[:, j, :], m.edge_i[:, j, :]).then_inc(idx_ok, 1)

            def mask(i, j, r):
                t, s, u = i * TURN + j, j % SLOTS, j % 2
                if r == 0:
                    dve.wait_ge(xt_ready, done(t))
                    nc.vector.tensor_copy(idx[:, s, :].rearrange("p (o e) -> p o e", o=1),
                                          m.edge_i[:, bass.ds(t + SLOTS, 1), :]).then_inc(idx_ok, 1)
                    if j % half == 0:
                        dve.wait_ge(typ_in[(j // half) % 2], (i + j // TURN) * 16 + 16)
                    dve.wait_ge(projected, done(t - 2))
                last = nc.vector.scalar_tensor_tensor(
                    xt[:, u, r, :, :], typ_b[:, j % TURN, None, :].broadcast_to([P, 2, P]), float(r), ps_t[u][:],
                    ALU.is_equal, ALU.mult)
                if r == R - 1:
                    last.then_inc(masked, 1)

            def dots(i, j):
                t, u = i * TURN + j, j % 2
                nc.vector.tensor_tensor(qk[:, u, :, HD:HD + R],
                                        m.of_type[:, bass.ds(t, 1), :].broadcast_to([P, H, R]),
                                        m.bias_r[:].rearrange("p r h -> p h r"), ALU.mult)
                yield
                dve.wait_ge(v_out, done(t))
                nc.vector.tensor_tensor(qk[:, u, :, 0:HD], q[:, u, :].rearrange("p (h d) -> p h d", h=H),
                                        ps_qkv[u][:, 1, :].rearrange("p (h d) -> p h d", h=H),
                                        ALU.mult).then_inc(qk_ok, 1)
                yield
                dve.wait_ge(qk_ok, done(t))
                nc.vector.tensor_reduce(dot[:, u, :], qk[:, u, :, :], AX.X, ALU.add).then_inc(dot_ok, 1)
                yield
                dve.wait_ge(dot_ok, done(t))
                nc.vector.tensor_scalar(m.logit[:, bass.ds(t, 1), :], dot[:, u:u + 1, :], 1.0 / SCALE, None,
                                        ALU.mult).then_inc(logit_ok, 1)
                yield

            def step(i, j):
                of_t = dots(i, j)
                for r in range(R):
                    mask(i, j + 2, r)
                    if r >= 1:
                        next(of_t)

            for j in range(2):
                for r in range(R):
                    mask(0, j, r)
            with dve.Fori(0, turns - 1) as i:
                for j in range(TURN):
                    step(i, j)
            for j in range(TURN):
                if j + 2 < TURN:
                    step(turns - 1, j)
                else:
                    list(dots(turns - 1, j))


def segment_softmax(nc, m):
    with ExitStack() as ctx:
        sb, pb, sem = scoped(nc, ctx)
        by_row = sb("ss_by_row", [HALF, 2, H, P])
        own = sb("ss_own", [P, H, NT])
        other = sb("ss_other", [P, 2, H, NT + SHIFTS - 1])
        other_key = sb("ss_other_key", [P, 2, NT + SHIFTS - 1])
        same = sb("ss_same", [P, 2, SHIFTS, NT])
        part = sb("ss_part", [P, 2, H, NT])
        top = sb("ss_top", [P, H, NT])
        total = sb("ss_total", [P, H, NT])
        ps = [pb(f"ss_ps{i}", [HALF, 4, P]) for i in range(4)]
        ps_b = [pb(f"ss_ps_b{i}", [P, 4, HALF]) for i in range(4)]
        band = [nc.values_load(m.band_i[0:1, j:j + 1], engines=engines, min_val=1, max_val=most,
                               skip_runtime_bounds_check_because="the setup holds it to the circle")
                for j, engines, most in ((0, [ENG.Activation], EC - SHIFTS),
                                         (1, [ENG.Activation, ENG.DVE, ENG.Pool], EP // (2 * SHIFTS)))]

        def shifted_pass(name, a, vh, pool_folds, begin, masks, bring, fold):
            with ExitStack() as inner:
                _, _, sem2 = scoped(nc, inner)
                landed = [sem2(f"{name}_landed{u}") for u in range(2)]
                mask_ok, masks_ok = sem2(name + "_mask_ok"), sem2(name + "_masks_ok")
                folded = [sem2(f"{name}_folded{e}") for e in range(2)]
                per_block = [2 * SHIFTS, 2 * SHIFTS if pool_folds else SHIFTS]
                inner_block = inner.enter_context(nc.Block())

                @inner_block.scalar
                def _(act):
                    for f in folded:
                        act.nop().then_inc(f, LEAD - 2 * SHIFTS)
                    with act.Fori(0, band[1]) as n:
                        for u, start in enumerate((band[0], EC + 1)):
                            for e in range(2):
                                act.wait_ge(folded[e], LEAD + (n * 2 + u) * per_block[e] - per_block[e])
                            act.nop(nofuse=True)
                            v = a[:, bass.ds(n * SHIFTS + start, EP)]
                            act.dma_start(other[:, u, :, :], bass.AP(
                                tensor=v.tensor, offset=v.offset,
                                ap=[[NT, P], [3 * EC, H], [1, NT + SHIFTS - 1]])).then_inc(landed[u], 16)
                            v = m.key_d[bass.ds(n * SHIFTS + start, EP)]
                            act.dma_start(other_key[:, u, :], bass.AP(
                                tensor=v.tensor, offset=v.offset,
                                ap=[[NT, P], [1, NT + SHIFTS - 1]])).then_inc(landed[u], 16)

                def fold_block(engine, ops, e, u, step, heads):
                    order = [("bring", 0), ("bring", 1)]
                    for k in range(SHIFTS):
                        order.append(("fold", k))
                        if k + 2 < SHIFTS:
                            order.append(("bring", k + 2))
                    at = {what: j + 1 for j, what in enumerate(order)}
                    folder = e if pool_folds else 0
                    mine, folders = (LEAD + step * per_block[x] for x in (e, folder))
                    for what, k in order:
                        if what == "bring":
                            engine.wait_ge(folded[folder], folders + (at["fold", k - 2] if k >= 2 else 0))
                            bring(ops, part[:, k % 2, heads, :], other[:, u, heads, k:k + NT],
                                  same[:, u, None, k, :].broadcast_to([P, heads.stop - heads.start, NT])
                                  ).then_inc(folded[e], 1)
                        elif folder == e:
                            engine.wait_ge(folded[e], mine + max(at["bring", k], at["fold", k - 1] if k else 0))
                            to = heads if pool_folds else slice(0, H)
                            if not pool_folds:
                                engine.wait_ge(folded[1], LEAD + step * per_block[1] + k + 1)
                            fold(ops, to, part[:, k % 2, to, :]).then_inc(folded[e], 1)

                @inner_block.vector
                def _(dve):
                    heads = slice(0, vh)
                    begin().then_inc(folded[0], 2 * SHIFTS)
                    with dve.Fori(0, band[1]) as n:
                        for u in range(2):
                            dve.wait_ge(landed[u], n * 32 + 32)
                            for k in range(SHIFTS):
                                last = nc.vector.tensor_tensor(same[:, u, k, :], other_key[:, u, k:k + NT],
                                                               m.key_b[:], ALU.is_equal)
                            masks(dve, last, same[:, u, :, :], n * 2 + u, mask_ok, masks_ok)
                            dve.wait_ge(masks_ok, n * 2 + u + 1)
                            fold_block(dve, nc.vector, 0, u, n * 2 + u, heads)

                @inner_block.gpsimd
                def _(pool):
                    heads = slice(vh, H)
                    pool.nop().then_inc(folded[1], 2 * SHIFTS)
                    with pool.Fori(0, band[1]) as n:
                        for u in range(2):
                            pool.wait_ge(masks_ok, n * 2 + u + 1)
                            fold_block(pool, nc.gpsimd, 1, u, n * 2 + u, heads)

        with ExitStack() as inner:
            _, _, sem1 = scoped(nc, inner)
            turned, copied, stored, loaded = (sem1("ss_" + n) for n in ("turned", "copied", "stored", "loaded"))
            block = inner.enter_context(nc.Block())

            @block.tensor
            def _(pe):
                for a in range(2):
                    for h in range(H):
                        last = nc.tensor.transpose(ps[a * 2 + h // 4][:, h % 4, :],
                                                   m.logit[:, a * HALF:(a + 1) * HALF, h], m.ident[:])
                        if h % 4 == 3:
                            last.then_inc(turned, 1)

            @block.vector
            def _(dve):
                for i in range(4):
                    dve.wait_ge(turned, i + 1)
                    nc.vector.tensor_copy(by_row[:, i // 2, (i % 2) * 4:(i % 2) * 4 + 4, :], ps[i][:]).then_inc(copied, 1)

            @block.sync
            def _(sp):
                for a in range(2):
                    sp.wait_ge(copied, 2 * a + 2)
                    for c in range(3):
                        at = c * EC + a * HALF * P
                        sp.dma_start(m.logit_d[:, at:at + HALF * P].rearrange("h (t e) -> t h e", e=P),
                                     by_row[:, a, :, :]).then_inc(stored, 16)
                sp.wait_ge(stored, 6 * 16)
                sp.dma_start(own[:], m.logit_d[:, 0:EP].rearrange("h (p t) -> p h t", t=NT)).then_inc(loaded, 16)
                sp.wait_ge(loaded, 16)

        def max_masks(dve, last, to, step, mask_ok, masks_ok):
            last.then_inc(mask_ok, 1)
            dve.wait_ge(mask_ok, step + 1)
            nc.vector.tensor_scalar(to, to, 1.0, MASK, ALU.subtract, ALU.mult).then_inc(masks_ok, 1)

        shifted_pass(
            "ss_max", m.logit_d, 3, False,
            begin=lambda: nc.vector.tensor_scalar(top[:], own[:], NEG, None, ALU.max),
            masks=max_masks,
            bring=lambda ops, to, others, mask: ops.tensor_tensor(to, others, mask, ALU.add),
            fold=lambda ops, heads, of: ops.tensor_tensor(top[:, heads, :], top[:, heads, :], of, ALU.max))

        with ExitStack() as inner:
            _, _, sem1 = scoped(nc, inner)
            less, raised, stored = (sem1("ss_" + n) for n in ("less", "raised", "stored2"))
            block = inner.enter_context(nc.Block())

            @block.vector
            def _(dve):
                nc.vector.tensor_tensor(part[:, 0, :, :], own[:], top[:], ALU.subtract).then_inc(less, 1)

            @block.scalar
            def _(act):
                act.wait_ge(less, 1)
                nc.scalar.activation(own[:], part[:, 0, :, :], ACT.Exp).then_inc(raised, 1)

            @block.sync
            def _(sp):
                sp.wait_ge(raised, 1)
                for c in range(3):
                    sp.dma_start(m.prob_d[:, c * EC:c * EC + EP].rearrange("h (p t) -> p h t", t=NT),
                                 own[:]).then_inc(stored, 16)
                sp.wait_ge(stored, 3 * 16)

        def sum_masks(dve, last, to, step, mask_ok, masks_ok):
            last.then_inc(masks_ok, 1)

        shifted_pass(
            "ss_sum", m.prob_d, 5, True,
            begin=lambda: nc.vector.tensor_copy(total[:], own[:]),
            masks=sum_masks,
            bring=lambda ops, to, others, mask: ops.tensor_tensor(to, others, mask, ALU.mult),
            fold=lambda ops, heads, of: ops.tensor_tensor(total[:, heads, :], total[:, heads, :], of, ALU.add))

        with ExitStack() as inner:
            _, _, sem1 = scoped(nc, inner)
            chain, stored, turned = (sem1("ss_" + n) for n in ("chain3", "stored3", "turned3"))
            loaded = [sem1(f"ss_loaded3{k}") for k in range(2)]
            block = inner.enter_context(nc.Block())

            @block.vector
            def _(dve):
                def step(ins):
                    steps[0] += 1
                    ins.then_inc(chain, 1)
                    dve.wait_ge(chain, steps[0])

                steps = [0]
                for k in range(2):
                    heads = slice(4 * k, 4 * k + 4)
                    step(nc.vector.tensor_scalar(total[:, heads, :], total[:, heads, :], 1e-12, None, ALU.add))
                    step(nc.vector.reciprocal(part[:, 0, heads, :], total[:, heads, :]))
                    step(nc.vector.tensor_tensor(own[:, heads, :], own[:, heads, :], part[:, 0, heads, :], ALU.mult))
                for j, i in enumerate((0, 2, 1, 3)):
                    dve.wait_ge(turned, j + 1)
                    a, h = i // 2, (i % 2) * 4
                    nc.vector.tensor_copy(m.logit[:, a * HALF:(a + 1) * HALF, h:h + 4].rearrange("p t h -> p h t"),
                                          ps_b[i][:])

            @block.sync
            def _(sp):
                for k in range(2):
                    heads = slice(4 * k, 4 * k + 4)
                    sp.wait_ge(chain, 3 * k + 3)
                    sp.dma_start(m.attn_d[heads, :].rearrange("h (p t) -> p h t", t=NT), own[:, heads, :]).then_inc(stored, 16)
                    sp.wait_ge(stored, 16 * k + 16)
                    for a in range(2):
                        sp.dma_start(by_row[:, a, heads, :], m.attn_d[heads, a * HALF * P:(a + 1) * HALF * P].rearrange(
                            "h (t e) -> t h e", e=P)).then_inc(loaded[k], 16)

            @block.tensor
            def _(pe):
                for i in (0, 2, 1, 3):
                    pe.wait_ge(loaded[i % 2], 32)
                    for h in range(4):
                        last = nc.tensor.transpose(ps_b[i][:, h, :], by_row[:, i // 2, (i % 2) * 4 + h, :],
                                                   m.ident[0:HALF, 0:HALF])
                    last.then_inc(turned, 1)


def store_chunk(sp, m, c, landed):
    first = c * (2 * TB)
    tiles = NT + 1 - first if isinstance(c, int) and c == ROUNDS else 2 * TB
    sp.dma_start(m.att_d[bass.ds(first * P, tiles * P), :].rearrange("(t p) f -> p t f", p=P),
                 m.msg[:, bass.ds(first, tiles), :]).then_inc(landed, 16)


def attended_messages(nc, m):
    with ExitStack() as ctx:
        _, _, sem = scoped(nc, ctx)
        av_ready, av_pool, att_out = (sem("am_" + n) for n in ("av_ready", "av_pool", "att_out"))
        share = 0.62
        first = 2 * TB
        middle = (first + NT) // 2
        pieces = [(0, first), (first, middle), (middle, NT)]
        block = ctx.enter_context(nc.Block())

        def multiply(ops, lo, hi):
            av = m.msg[:, lo:hi, 0:F].rearrange("p t (h d) -> p t h d", h=H)
            return ops.tensor_tensor(av, av, m.logit[:, lo:hi, :, None].broadcast_to([P, hi - lo, H, HD]), ALU.mult)

        def shared(lo, hi):
            return lo + int((hi - lo) * share)

        @block.vector
        def _(dve):
            nc.vector.tensor_copy(m.msg[:, :, F:W], m.edge_f[:, 0:NT + 1, :])
            for lo, hi in pieces:
                multiply(nc.vector, lo, shared(lo, hi)).then_inc(av_ready, 1)

        @block.gpsimd
        def _(pool):
            for lo, hi in pieces:
                multiply(nc.gpsimd, shared(lo, hi), hi).then_inc(av_pool, 1)

        @block.sync
        def _(sp):
            sp.wait_ge(av_ready, 1)
            sp.wait_ge(av_pool, 1)
            store_chunk(sp, m, 0, att_out)
            sp.wait_ge(att_out, 16)


def layer1_nodes(nc, m, from_sums):
    name = "n1s_" if from_sums else "n1_"
    with ExitStack() as ctx:
        sb, pb, sem = scoped(nc, ctx)
        xg = sb(name + "xg", [P, XSLOTS, GT, F])
        if from_sums:
            sg = sb(name + "sg", [P, 2, GT, F])
        else:
            win = sb(name + "win", [P, WSLOTS, BT, W])
            rel = sb(name + "rel", [P, 2, BT])
            onehot = sb(name + "onehot", [P, 2, BT, P])
        st = sb(name + "st", [P, 4, BT, P])
        yg = sb(name + "yg", [P, 2, GT, F])
        xbeta = sb(name + "xbeta", [P, 2, BT, F])
        norm = sb(name + "norm", [P, 2, BT, F])
        scaled = sb(name + "scaled", [P, 2, BT, F])
        z = sb(name + "z", [P, 2, BT, F])
        ps_t = [pb(f"{name}ps_t{i}", [P, BT, P]) for i in range(4)]
        ps_h = [pb(f"{name}ps_h{i}", [P, BT, F]) for i in range(4)]
        x_in = [sem(f"{name}x_in{i}") for i in range(XSLOTS)]
        s_in = [sem(f"{name}s_in{i}") for i in range(2)]
        win_in = [sem(f"{name}win_in{i}") for i in range(WSLOTS)]
        stored = [sem(f"{name}stored{i}") for i in range(2)]
        x_tail, s_tail, y_tail = (sem(name + n) for n in ("x_tail", "s_tail", "y_tail"))
        att_out = sem(name + "att_out")
        st_ready, st_copied, h_ready = (sem(name + n) for n in ("st_ready", "st_copied", "h_ready"))
        rel_ok, hot_ready = sem(name + "rel_ok"), sem(name + "hot_ready")
        norm_ready, y_ready = sem(name + "norm_ready"), sem(name + "y_ready")
        xbeta_ready, scaled_ready, z_ready = (sem(name + n) for n in ("xbeta_ready", "scaled_ready", "z_ready"))
        buf, ev = [], []
        for k in range(2):
            buf.append([sb(f"{name}{n}{k}", [P, 2, BT, *w]) for n, w in (
                ("stats", [6]), ("mv", [2]), ("std", []), ("rstd", []), ("shift", []))])
            ev.append([sem(f"{name}{n}{k}") for n in ("stats_ok", "mv_ready", "std_ready", "rstd_ok", "shift_ready")])
        block = ctx.enter_context(nc.Block())

        @block.sync
        def _(sp):
            def store(i, o):
                g = (i - 1) * XSLOTS + o // GB
                sp.wait_ge(y_ready, done((i - 1) * TB + o // GB * GB + 1))
                sp.nop(nofuse=True)
                store_group(sp, m.out, yg[:, y_slot(o), :, :], g, stored[y_slot(o)], y_tail)

            starts = []

            def step(i, o):
                b, g = i * TB + o, i * XSLOTS + o // GB
                if o % GB == 0:
                    sp.wait_ge(h_ready, done(b + 1 - TB))
                    sp.wait_ge(xbeta_ready, done(b + 1 - TB))
                    load_group(sp, xg[:, x_slot(o), :, :], m.x1_d, g, x_in[x_slot(o)], x_tail)
                    if from_sums:
                        sp.wait_ge(st_ready, done(b + 1 - 2 * GB))
                        load_group(sp, sg[:, y_slot(o), :, :], m.sums_d, g, s_in[y_slot(o)], s_tail)
                if not from_sums:
                    if o % GB == 0:
                        starts[:] = window_starts(nc, m, i, o)
                    if o == GB:
                        store_chunk(sp, m, i + 1, att_out)
                    if o == TB // 2:
                        sp.wait_ge(att_out, i * 16 + 16)
                        sp.nop(nofuse=True)
                    load_windows(sp, m.att_d, win, win_in, st_ready, starts, i, o)
                if o % GB == GB - 1 and not (isinstance(i, int) and i == 0):
                    store(i, o)

            for o in range(TB):
                step(0, o)
            with sp.Fori(1, ROUNDS - 1) as i:
                for o in range(TB):
                    step(i, o)
            for o in range(TB + 2):
                step(ROUNDS - 1, o)
            for o in range(TB + 2, 2 * TB + 2, GB):
                store(ROUNDS - 1, o + GB - 1)
            sp.wait_ge(stored[0], LEAD + GROUPS // 2 * 16 + 16)
            sp.wait_ge(stored[1], LEAD + GROUPS // 2 * 16)
            sp.wait_ge(y_tail, 16)

        def x_landed(engine, i, o):
            engine.wait_ge(x_in[x_slot(o)], (i + o // TB) * 16 + 16)

        @block.tensor
        def _(pe):
            lead(pe, st_ready, h_ready)

            def sum_up(i, o):
                b, u = i * TB + o, o % 2
                pe.wait_ge(st_copied, done(b - 4))
                if from_sums:
                    pe.wait_ge(s_in[y_slot(o)], (i * (XSLOTS // 2) + o // GB // 2) * 16 + 16)
                else:
                    pe.wait_ge(hot_ready, done(b))
                for n in range(BT):
                    if from_sums:
                        last = nc.tensor.matmul(ps_t[o % 4][:, n, :], sg[:, y_slot(o), (o % 2) * BT + n, :], m.ident[:],
                                                start=True, stop=True)
                    else:
                        last = nc.tensor.matmul(ps_t[o % 4][:, n, :], win[:, o % WSLOTS, n, 0:F], onehot[:, u, n, :],
                                                start=True, stop=True)
                last.then_inc(st_ready, 1)

            def multiply(i, o):
                b, half = i * TB + o, (o % 2) * BT
                x_landed(pe, i, o)
                pe.wait_ge(st_copied, done(b))
                pe.wait_ge(norm_ready, done(b - 4))
                nc.tensor.matmul(ps_h[o % 4][:].rearrange("p b f -> p (b f)"), m.ones_3[:], m.bo_parts[:],
                                 start=True, stop=False)
                for n in range(BT):
                    nc.tensor.matmul(ps_h[o % 4][:, n, :], m.ident[:], xg[:, x_slot(o), half + n, :],
                                     start=False, stop=False)
                    last = nc.tensor.matmul(ps_h[o % 4][:, n, :], st[:, o % 4, n, :], m.w_out[:],
                                            start=False, stop=(n == BT - 1))
                last.then_inc(h_ready, 1)

            sum_up(0, 0)
            sum_up(0, 1)
            with pe.Fori(0, ROUNDS) as i:
                for o in range(TB):
                    multiply(i, o)
                    sum_up(i, o + 2)
            multiply(ROUNDS, 0)
            multiply(ROUNDS, 1)

        @block.scalar
        def _(act):
            lead(act, st_copied, norm_ready, y_ready, ev[0][2], ev[1][2], *stored)
            nc.scalar.preload_act_table(ACT.Sqrt)

            def copy_st(i, o):
                b, u = i * TB + o, o % 4
                act.wait_ge(st_ready, done(b))
                act.wait_ge(h_ready, done(b - 4))
                nc.scalar.copy(st[:, u, :, :], ps_t[o % 4][:]).then_inc(st_copied, 1)

            def root(k, i, o):
                b, u = i * TB + o, o % 2
                _, mv, std, _, _ = buf[k]
                act.wait_ge(ev[k][1], done(b))
                nc.scalar.activation(std[:, u, :], mv[:, u, :, 1], ACT.Sqrt, bias=m.eps_c[:]).then_inc(ev[k][2], 1)

            def normalise(k, to, of, i, o, ready):
                u = o % 2
                _, _, _, rstd, shift = buf[k]
                act.wait_ge(ev[k][4], done(i * TB + o))
                for n in range(BT):
                    last = nc.scalar.activation(to(n), of(n), ACT.Identity, bias=shift[:, u, n:n + 1],
                                                scale=rstd[:, u, n:n + 1])
                last.then_inc(ready, 1)

            def first_norm(i, o):
                act.wait_ge(scaled_ready, done(i * TB + o - 2))
                normalise(0, lambda n: norm[:, o % 2, n, :], lambda n: ps_h[o % 4][:, n, :], i, o, norm_ready)

            def second_norm(i, o):
                s = y_slot(o)
                if o % GB == 0:
                    act.wait_ge(stored[s], LEAD + (i * (XSLOTS // 2) + o // GB // 2) * 16)
                normalise(1, lambda n: yg[:, s, (o % 2) * BT + n, :], lambda n: z[:, o % 2, n, :], i, o, y_ready)

            copy_st(0, 0)
            copy_st(0, 1)
            for o in range(2):
                copy_st(0, o + 2)
                root(0, 0, o)
                first_norm(0, o)
            with act.Fori(0, ROUNDS - 1) as i:
                for o in range(TB):
                    root(0, i, o + 2)
                    copy_st(i, o + 4)
                    root(1, i, o)
                    first_norm(i, o + 2)
                    second_norm(i, o)
            i = ROUNDS - 1
            for o in range(TB + 2):
                if o + 2 < TB + 2:
                    root(0, i, o + 2)
                if o + 4 < TB + 2:
                    copy_st(i, o + 4)
                root(1, i, o)
                if o + 2 < TB + 2:
                    first_norm(i, o + 2)
                second_norm(i, o)

        @block.gpsimd
        def _(pool):
            lead(pool, xbeta_ready, scaled_ready, z_ready)
            beta4 = m.bet_b[:, None, :].broadcast_to([P, BT, F])
            gamma4 = m.gam_b[:, None, :].broadcast_to([P, BT, F])

            def add_beta(i, o):
                b, u, s, half = i * TB + o, o % 2, x_slot(o), (o % 2) * BT
                x_landed(pool, i, o)
                pool.wait_ge(z_ready, done(b - 2))
                nc.gpsimd.tensor_tensor(xbeta[:, u, :, :], xg[:, s, half:half + BT, :], beta4, ALU.add).then_inc(xbeta_ready, 1)

            def scale(i, o):
                b, u = i * TB + o, o % 2
                pool.wait_ge(norm_ready, done(b))
                pool.wait_ge(z_ready, done(b - 2))
                nc.gpsimd.tensor_tensor(scaled[:, u, :, :], norm[:, u, :, :], gamma4, ALU.mult).then_inc(scaled_ready, 1)

            def add(i, o):
                b, u = i * TB + o, o % 2
                pool.wait_ge(scaled_ready, done(b))
                pool.wait_ge(xbeta_ready, done(b))
                pool.wait_ge(y_ready, done(b - 2))
                nc.gpsimd.tensor_tensor(z[:, u, :, :], scaled[:, u, :, :], xbeta[:, u, :, :], ALU.add).then_inc(z_ready, 1)

            add_beta(0, 0)
            with pool.Fori(0, ROUNDS) as i:
                for o in range(TB):
                    scale(i, o)
                    add_beta(i, o + 1)
                    add(i, o)
            scale(ROUNDS, 0)
            add_beta(ROUNDS, 1)
            add(ROUNDS, 0)
            scale(ROUNDS, 1)
            add(ROUNDS, 1)

        @block.vector
        def _(dve):
            lead(dve, rel_ok, hot_ready, *(e for k in range(2) for e in (ev[k][0], ev[k][1], ev[k][3], ev[k][4])))
            moments, inverting = zip(*(norm_steps(nc, dve, *buf[k], *ev[k]) for k in range(2)))
            if not from_sums:
                hots = one_hots(nc, dve, m, win, win_in, rel, rel_ok, onehot, hot_ready, st_ready, False)

            def first_moments(i, o, other):
                dve.wait_ge(h_ready, done(i * TB + o))
                moments[0](i, o, lambda n: ps_h[o % 4][:, n, :], other)

            def second_moments(i, o, other):
                dve.wait_ge(z_ready, done(i * TB + o))
                moments[1](i, o, lambda n: z[:, o % 2, n, :], other)

            none = iter(())

            def step(i, o, first, other):
                invert_0, invert_1 = inverting[0](i, o + 2) if first else none, inverting[1](i, o)
                if first:
                    first_moments(i, o + 2, other)
                second_moments(i, o, invert_0)
                next(invert_0, None)
                next(other, None)
                next(other, None)
                next(invert_1)
                for _ in other:
                    pass
                next(invert_1, None)

            for o in range(5):
                if not from_sums:
                    list(hots(0, o))
                if o >= 3:
                    first_moments(0, o - 3, none)
                    list(inverting[0](0, o - 3))
            with dve.Fori(0, ROUNDS - 1) as i:
                for o in range(TB):
                    step(i, o, True, none if from_sums else hots(i, o + 5))
            for o in range(TB + 2):
                step(ROUNDS - 1, o, o + 2 < TB + 2,
                     none if from_sums or o + 5 >= TB + 2 else hots(ROUNDS - 1, o + 5))


_INS = ["x", "src", "dst", "edge_type_5", "edge_weight", "L0_gnn_W", "L1_gnn_W_Q", "L1_gnn_W_K", "L1_gnn_W_V",
        "L1_gnn_attn_bias", "L1_gnn_out_proj_w", "L1_gnn_out_proj_b", "L1_gnn_ln_gamma", "L1_gnn_ln_beta"]


def kernel(**inputs):
    import numpy as _np
    import concourse.bacc as _bacc
    from concourse.bass_utils import run_bass_kernel_spmd as _run

    nc = _bacc.Bacc("TRN2", target_bir_lowering=False, num_devices=1)
    arrays, args = {}, []
    for name in _INS:
        a = _np.ascontiguousarray(inputs[name])
        arrays[f"in_{name}"] = a
        args.append(nc.dram_tensor(f"in_{name}", a.shape, mybir.dt.from_np(a.dtype), kind="ExternalInput").ap())
    args.append(nc.dram_tensor("out_x", (N, F), F32, kind="ExternalOutput").ap())
    gnn(nc, *args)
    r = _run(nc, [arrays], core_ids=[0])
    return r.results[0]["out_x"]
```
